# Optimizing a Trainium2 kernel written in Bass

```python
import numpy as np
import jax
import jax.numpy as jnp

def _softmax(x, axis=-1):
    return jax.nn.softmax(x, axis=axis)

def _gelu(x):
    return jax.nn.gelu(x, approximate=True)

def _silu(x):
    return jax.nn.silu(x)

def _sigmoid(x):
    return jax.nn.sigmoid(x)

def _layernorm(x, axis=-1, eps=1e-05):
    m = jnp.mean(x, axis=axis, keepdims=True)
    v = jnp.var(x, axis=axis, keepdims=True)
    return (x - m) / jnp.sqrt(v + eps)

def _scatter_add(tgt, idx, src, axis=0):
    return tgt.at[idx].add(src)

def _segment_sum(src, seg, n):
    return jax.ops.segment_sum(src, seg, n)
kernel_name = 'mk_xattn_ffn_d4_seqx_r4_0c9775'

def setup_inputs(seed: int=0):
    np.random.seed(seed)
    _w = jnp.asarray

    def _rec_inputs():
        import jax
        import jax.numpy as jnp
        _rk = jax.random.key(seed)
        x = -0.0002928 + 1 * jax.random.normal(jax.random.fold_in(_rk, 1), (8, 256, 256), jnp.float32)
        _lenS = 256 - jax.random.randint(jax.random.fold_in(_rk, 7), (8,), 0, max(1, 256 // 4) + 1, jnp.int32)
        _lenS2 = 256 - jax.random.randint(jax.random.fold_in(_rk, 8), (8,), 0, max(1, 256 // 4) + 1, jnp.int32)
        _ctx_1024P = jax.random.normal(jax.random.fold_in(_rk, 11), (8, 16, 256), jnp.float32)
        _ctx_1024c = jax.random.dirichlet(jax.random.fold_in(_rk, 511), 0.3 * jnp.ones((16,), jnp.float32), (8, 256))
        _ctx_1024t = jnp.einsum('bsk,bkd->bsd', _ctx_1024c, _ctx_1024P)
        _ctx_1024t = _ctx_1024t * jax.lax.rsqrt(jnp.mean(jnp.square(_ctx_1024t)) + 1e-12) * 0.953939
        ctx_1024 = -1.39393e-06 + 0.999914 * (_ctx_1024t + 0.3 * jax.random.normal(jax.random.fold_in(_rk, 611), (8, 256, 256), jnp.float32))
        return (x, ctx_1024)
    x, ctx_1024 = _rec_inputs()

    def _L0_xattn_setup():
        import jax, jax.numpy as jnp
        import numpy as np
        D_MODEL = 256
        N_HEAD = 16
        D_HEAD = D_MODEL // N_HEAD
        key = jax.random.key(seed)
        ks = jax.random.split(key, 6)
        B, L, M = (2, 512, 512)
        q = jax.random.normal(ks[0], (B, L, D_MODEL), dtype=jnp.float32)
        kv = jax.random.normal(ks[1], (B, L, D_MODEL), dtype=jnp.float32)
        mem = jax.random.normal(ks[2], (B, M, D_MODEL), dtype=jnp.float32)
        s = 1.0 / np.sqrt(D_MODEL)
        w_q = jax.random.normal(ks[3], (D_MODEL, D_MODEL), dtype=jnp.float32) * s
        w_kv = jax.random.normal(ks[4], (D_MODEL, 2 * D_HEAD), dtype=jnp.float32) * s
        w_concat = jax.random.normal(ks[5], (D_MODEL, D_MODEL), dtype=jnp.float32) * s
        return {'q': q, 'kv': kv, 'mem': mem, 'w_q': w_q, 'w_kv': w_kv, 'w_concat': w_concat}
    _L0_xattn_all = _L0_xattn_setup()
    _L0_xattn_in = {k: v for k, v in _L0_xattn_all.items() if k in ('w_q', 'w_kv', 'w_concat')}
    del _L0_xattn_all

    def _L0_ffn_setup():
        import jax, jax.numpy as jnp
        import numpy as np
        DIM = 256
        E = 16
        TOPK = 2
        G = 4
        TOPK_G = 2
        INTER = 128
        N_SHARED = 2
        ROUTE_SCALE = 1.0

        def _gate(xf, gate_w, gate_b):
            scores = xf @ gate_w.T
            scores = jax.nn.softmax(scores.astype(jnp.float32), axis=-1)
            orig = scores
            scores = scores + gate_b
            T = xf.shape[0]
            sg = scores.reshape(T, G, E // G)
            group_scores = jax.lax.top_k(sg, 2)[0].sum(-1)
            _, gidx = jax.lax.top_k(group_scores, TOPK_G)
            keep = jax.nn.one_hot(gidx, G).sum(axis=1) > 0
            sg = jnp.where(keep[:, :, None], sg, -jnp.inf)
            scores = sg.reshape(T, E)
            _, idx = jax.lax.top_k(scores, TOPK)
            weights = jnp.take_along_axis(orig, idx, axis=1)
            weights = (weights * ROUTE_SCALE).astype(xf.dtype)
            return (weights, idx)
        key = jax.random.key(seed)
        ks = jax.random.split(key, 16)
        s = lambda fan_in: 1.0 / np.sqrt(fan_in)
        inp = {'x': jax.random.normal(ks[0], (4, 256, DIM), dtype=jnp.float32), 'gate_w': jax.random.normal(ks[1], (E, DIM), dtype=jnp.float32) * s(DIM), 'gate_b': jnp.zeros((E,), dtype=jnp.float32), 'We1': jax.random.normal(ks[2], (E, DIM, INTER), dtype=jnp.float32) * s(DIM), 'be1': jnp.zeros((E, INTER), dtype=jnp.float32), 'We2': jax.random.normal(ks[3], (E, INTER, DIM), dtype=jnp.float32) * s(INTER), 'be2': jnp.zeros((E, DIM), dtype=jnp.float32), 'We3': jax.random.normal(ks[4], (E, DIM, INTER), dtype=jnp.float32) * s(DIM), 'be3': jnp.zeros((E, INTER), dtype=jnp.float32), 'ws1': jax.random.normal(ks[5], (DIM, N_SHARED * INTER), dtype=jnp.float32) * s(DIM), 'bs1': jnp.zeros((N_SHARED * INTER,), dtype=jnp.float32), 'ws2': jax.random.normal(ks[6], (N_SHARED * INTER, DIM), dtype=jnp.float32) * s(N_SHARED * INTER), 'bs2': jnp.zeros((DIM,), dtype=jnp.float32), 'ws3': jax.random.normal(ks[7], (DIM, N_SHARED * INTER), dtype=jnp.float32) * s(DIM), 'bs3': jnp.zeros((N_SHARED * INTER,), dtype=jnp.float32)}
        return inp
    _L0_ffn_all = _L0_ffn_setup()
    _L0_ffn_in = {k: v for k, v in _L0_ffn_all.items() if k in ('gate_w', 'gate_b', 'We1', 'be1', 'We2', 'be2', 'We3', 'be3', 'ws1', 'bs1', 'ws2', 'bs2', 'ws3', 'bs3')}
    del _L0_ffn_all

    def _L1_xattn_setup():
        import jax, jax.numpy as jnp
        import numpy as np
        SCALE_BASE = 512.0
        GN_EPS = 1e-05

        def _xpos(x, downscale):
            L, D = (x.shape[-2], x.shape[-1])
            half = D // 2
            base = (jnp.arange(0, D, 2, dtype=jnp.float32) + 0.4 * D) / (1.4 * D)
            min_pos = -(L // 2)
            power = (jnp.arange(min_pos, min_pos + L, dtype=jnp.float32) / SCALE_BASE)[:, None]
            scale = base[None, :] ** power
            inv_freq = 1.0 / 10000.0 ** (jnp.arange(half, dtype=jnp.float32) / half)
            ang = jnp.arange(L, dtype=jnp.float32)[:, None] * inv_freq[None, :]
            sin, cos = (jnp.sin(ang), jnp.cos(ang))
            if downscale:
                scale = 1.0 / scale
            sin_s = jnp.repeat(sin * scale, 2, axis=-1)
            cos_s = jnp.repeat(cos * scale, 2, axis=-1)
            x1, x2 = (x[..., ::2], x[..., 1::2])
            rot = jnp.stack((-x2, x1), axis=-1).reshape(x.shape)
            return x * cos_s + rot * sin_s

        def _decay_mask(L, H):
            gammas = 1.0 - jnp.exp(jnp.linspace(np.log(1.0 / 32.0), np.log(1.0 / 512.0), H)).astype(jnp.float32)
            idx = jnp.arange(L)
            dist = idx[:, None] - idx[None, :]
            causal = dist >= 0
            d = jnp.maximum(dist, 0).astype(jnp.float32)
            return jnp.where(causal[None], gammas[:, None, None] ** d[None], 0.0)
        key = jax.random.key(seed)
        ks = jax.random.split(key, 9)
        B, L, D, H = (2, 512, 256, 16)
        hd = D // H
        return {'query': jax.random.normal(ks[0], (B, L, D), jnp.float32), 'key': jax.random.normal(ks[1], (B, L, D), jnp.float32), 'value': jax.random.normal(ks[2], (B, L, D), jnp.float32), 'W_Q': jax.random.normal(ks[3], (H, D, hd), jnp.float32) / D, 'W_K': jax.random.normal(ks[4], (H, D, hd), jnp.float32) / D, 'W_V': jax.random.normal(ks[5], (H, D, hd), jnp.float32) / D, 'g_w': jax.random.normal(ks[6], (D, D), jnp.float32) * (2.0 / (D + D)) ** 0.5, 'g_b': jnp.zeros((D,), jnp.float32), 'out_w': jax.random.normal(ks[7], (D, D), jnp.float32) * (2.0 / (D + D)) ** 0.5, 'out_b': jnp.zeros((D,), jnp.float32)}
    _L1_xattn_all = _L1_xattn_setup()
    _L1_xattn_in = {k: v for k, v in _L1_xattn_all.items() if k in ('W_Q', 'W_K', 'W_V', 'g_w', 'g_b', 'out_w', 'out_b')}
    del _L1_xattn_all

    def _L1_ffn_setup():
        import jax, jax.numpy as jnp
        import numpy as np
        B, S, D, E, K = (4, 512, 256, 8, 2)
        H = 4 * D
        key = jax.random.key(seed)
        ks = jax.random.split(key, 4)
        sc = lambda n: 1.0 / np.sqrt(n)
        return {'x': jax.random.normal(ks[0], (B, S, D), jnp.float32), 'gate_w': jax.random.normal(ks[1], (D, E), jnp.float32) * sc(D), 'gate_b': jnp.zeros((E,), jnp.float32), 'w1': jax.random.normal(ks[2], (E, D, H), jnp.float32) * sc(D), 'b1': jnp.zeros((E, H), jnp.float32), 'w2': jax.random.normal(ks[3], (E, H, D), jnp.float32) * sc(H), 'b2': jnp.zeros((E, D), jnp.float32)}
    _L1_ffn_all = _L1_ffn_setup()
    _L1_ffn_in = {k: v for k, v in _L1_ffn_all.items() if k in ('gate_w', 'gate_b', 'w1', 'b1', 'w2', 'b2')}
    del _L1_ffn_all

    def _L2_xattn_setup():
        import jax, jax.numpy as jnp
        import numpy as np
        D_MODEL = 256
        N_HEADS = 16
        HEAD_DIM = D_MODEL // N_HEADS
        key = jax.random.key(seed)
        ks = jax.random.split(key, 10)
        B, NQ, S = (8, 64, 1024)
        inv = 1.0 / np.sqrt(D_MODEL)
        inp = {'queries': jax.random.normal(ks[0], (B, NQ, D_MODEL), dtype=jnp.float32), 'context': jax.random.normal(ks[1], (B, S, D_MODEL), dtype=jnp.float32), 'wq': jax.random.normal(ks[2], (D_MODEL, D_MODEL), dtype=jnp.float32) * inv, 'bq': jnp.zeros((D_MODEL,), dtype=jnp.float32), 'wk': jax.random.normal(ks[3], (D_MODEL, D_MODEL), dtype=jnp.float32) * inv, 'bk': jnp.zeros((D_MODEL,), dtype=jnp.float32), 'wv': jax.random.normal(ks[4], (D_MODEL, D_MODEL), dtype=jnp.float32) * inv, 'bv': jnp.zeros((D_MODEL,), dtype=jnp.float32), 'wo': jax.random.normal(ks[5], (D_MODEL, D_MODEL), dtype=jnp.float32) * inv, 'bo': jnp.zeros((D_MODEL,), dtype=jnp.float32)}
        return inp
    _L2_xattn_all = _L2_xattn_setup()
    _L2_xattn_in = {k: v for k, v in _L2_xattn_all.items() if k in ('wq', 'bq', 'wk', 'bk', 'wv', 'bv', 'wo', 'bo')}
    del _L2_xattn_all

    def _L2_ffn_setup():
        import jax, jax.numpy as jnp
        import numpy as np
        import math
        DIM = 256
        NUM_HEADS = 16
        SHARED_HEADS = 1
        ROUTED_HEADS = 3
        HEAD_DIM = DIM // NUM_HEADS
        B, N = (2, 512)
        key = jax.random.key(seed)
        ks = jax.random.split(key, 16)
        s = 1.0 / math.sqrt(DIM)
        inp = {'x': jax.random.normal(ks[0], (B, N, DIM), dtype=jnp.float32), 'Wq': jax.random.uniform(ks[1], (DIM, DIM), minval=-s, maxval=s), 'bq': jax.random.uniform(ks[2], (DIM,), minval=-s, maxval=s), 'Wk': jax.random.uniform(ks[3], (DIM, DIM), minval=-s, maxval=s), 'bk': jax.random.uniform(ks[4], (DIM,), minval=-s, maxval=s), 'Wv': jax.random.uniform(ks[5], (DIM, DIM), minval=-s, maxval=s), 'bv': jax.random.uniform(ks[6], (DIM,), minval=-s, maxval=s), 'Wp': jax.random.uniform(ks[7], (DIM, DIM), minval=-s, maxval=s), 'bp': jax.random.uniform(ks[8], (DIM,), minval=-s, maxval=s), 'Wr': jax.random.uniform(ks[9], (NUM_HEADS - SHARED_HEADS, DIM), minval=-s, maxval=s), 'br': jax.random.uniform(ks[10], (NUM_HEADS - SHARED_HEADS,), minval=-s, maxval=s), 'Ws': jax.random.uniform(ks[11], (2, DIM), minval=-s, maxval=s), 'bs': jax.random.uniform(ks[12], (2,), minval=-s, maxval=s), 'temperature': jnp.full((NUM_HEADS, 1, 1), float(np.log(np.expm1(1.0 / 0.24))), dtype=jnp.float32), 'query_embedding': 0.02 * jax.random.normal(ks[13], (NUM_HEADS, 1, HEAD_DIM), dtype=jnp.float32)}
        return inp
    _L2_ffn_all = _L2_ffn_setup()
    _L2_ffn_in = {k: v for k, v in _L2_ffn_all.items() if k in ('Wq', 'bq', 'Wk', 'bk', 'Wv', 'bv', 'Wp', 'bp', 'Wr', 'br', 'Ws', 'bs', 'temperature', 'query_embedding')}
    del _L2_ffn_all

    def _L3_xattn_setup():
        import jax, jax.numpy as jnp
        import numpy as np
        NUM_HEADS = 16
        EMBED_DIM = 256
        KEY_DIM = 64
        VALUE_DIM = 64
        NEG = -1000000000.0
        key = jax.random.key(seed)
        ks = jax.random.split(key, 7)
        B, S, E = (2, 512, EMBED_DIM)
        scale = 0.02
        return {'q': jax.random.normal(ks[0], (B, S, E), dtype=jnp.float32), 'k': jax.random.normal(ks[1], (B, S, E), dtype=jnp.float32), 'v': jax.random.normal(ks[2], (B, S, E), dtype=jnp.float32), 'Wq': jax.random.normal(ks[3], (NUM_HEADS, E, KEY_DIM), dtype=jnp.float32) * scale, 'Wk': jax.random.normal(ks[4], (NUM_HEADS, E, KEY_DIM), dtype=jnp.float32) * scale, 'Wv': jax.random.normal(ks[5], (NUM_HEADS, E, VALUE_DIM), dtype=jnp.float32) * scale, 'Wo': jax.random.normal(ks[6], (NUM_HEADS * VALUE_DIM, E), dtype=jnp.float32) * scale}
    _L3_xattn_all = _L3_xattn_setup()
    _L3_xattn_in = {k: v for k, v in _L3_xattn_all.items() if k in ('Wq', 'Wk', 'Wv', 'Wo')}
    del _L3_xattn_all

    def _L3_ffn_setup():
        import jax, jax.numpy as jnp
        import numpy as np
        D_MODEL = 256
        EXPERT_DIM = 128
        N_EXPERTS = 8
        TOP_K = 2

        def _sq_relu(h):
            return jnp.square(jax.nn.relu(h))
        key = jax.random.key(seed)
        ks = jax.random.split(key, 6)
        s = 0.02
        x = jax.random.normal(ks[0], (2, 512, D_MODEL), dtype=jnp.float32)
        Ws1 = jax.random.normal(ks[1], (D_MODEL, EXPERT_DIM), dtype=jnp.float32) * s
        Ws2 = jax.random.normal(ks[2], (EXPERT_DIM, D_MODEL), dtype=jnp.float32) * s
        W1 = jax.random.normal(ks[3], (N_EXPERTS, D_MODEL, EXPERT_DIM), dtype=jnp.float32) * s
        W2 = jax.random.normal(ks[4], (N_EXPERTS, EXPERT_DIM, D_MODEL), dtype=jnp.float32) * s
        Wr = jax.random.normal(ks[5], (D_MODEL, N_EXPERTS), dtype=jnp.float32) * s
        return {'x': x, 'Ws1': Ws1, 'Ws2': Ws2, 'W1': W1, 'W2': W2, 'Wr': Wr}
    _L3_ffn_all = _L3_ffn_setup()
    _L3_ffn_in = {k: v for k, v in _L3_ffn_all.items() if k in ('Ws1', 'Ws2', 'W1', 'W2', 'Wr')}
    del _L3_ffn_all
    return {'x': x, 'ctx_1024': ctx_1024, 'L0_xattn_w_q': _L0_xattn_in['w_q'], 'L0_xattn_w_kv': _L0_xattn_in['w_kv'], 'L0_xattn_w_concat': _L0_xattn_in['w_concat'], 'L0_ffn_gate_w': _L0_ffn_in['gate_w'], 'L0_ffn_gate_b': _L0_ffn_in['gate_b'], 'L0_ffn_We1': _L0_ffn_in['We1'], 'L0_ffn_be1': _L0_ffn_in['be1'], 'L0_ffn_We2': _L0_ffn_in['We2'], 'L0_ffn_be2': _L0_ffn_in['be2'], 'L0_ffn_We3': _L0_ffn_in['We3'], 'L0_ffn_be3': _L0_ffn_in['be3'], 'L0_ffn_ws1': _L0_ffn_in['ws1'], 'L0_ffn_bs1': _L0_ffn_in['bs1'], 'L0_ffn_ws2': _L0_ffn_in['ws2'], 'L0_ffn_bs2': _L0_ffn_in['bs2'], 'L0_ffn_ws3': _L0_ffn_in['ws3'], 'L0_ffn_bs3': _L0_ffn_in['bs3'], 'L1_xattn_W_Q': _L1_xattn_in['W_Q'], 'L1_xattn_W_K': _L1_xattn_in['W_K'], 'L1_xattn_W_V': _L1_xattn_in['W_V'], 'L1_xattn_g_w': _L1_xattn_in['g_w'], 'L1_xattn_g_b': _L1_xattn_in['g_b'], 'L1_xattn_out_w': _L1_xattn_in['out_w'], 'L1_xattn_out_b': _L1_xattn_in['out_b'], 'L1_ffn_gate_w': _L1_ffn_in['gate_w'], 'L1_ffn_gate_b': _L1_ffn_in['gate_b'], 'L1_ffn_w1': _L1_ffn_in['w1'], 'L1_ffn_b1': _L1_ffn_in['b1'], 'L1_ffn_w2': _L1_ffn_in['w2'], 'L1_ffn_b2': _L1_ffn_in['b2'], 'L2_xattn_wq': _L2_xattn_in['wq'], 'L2_xattn_bq': _L2_xattn_in['bq'], 'L2_xattn_wk': _L2_xattn_in['wk'], 'L2_xattn_bk': _L2_xattn_in['bk'], 'L2_xattn_wv': _L2_xattn_in['wv'], 'L2_xattn_bv': _L2_xattn_in['bv'], 'L2_xattn_wo': _L2_xattn_in['wo'], 'L2_xattn_bo': _L2_xattn_in['bo'], 'L2_ffn_Wq': _L2_ffn_in['Wq'], 'L2_ffn_bq': _L2_ffn_in['bq'], 'L2_ffn_Wk': _L2_ffn_in['Wk'], 'L2_ffn_bk': _L2_ffn_in['bk'], 'L2_ffn_Wv': _L2_ffn_in['Wv'], 'L2_ffn_bv': _L2_ffn_in['bv'], 'L2_ffn_Wp': _L2_ffn_in['Wp'], 'L2_ffn_bp': _L2_ffn_in['bp'], 'L2_ffn_Wr': _L2_ffn_in['Wr'], 'L2_ffn_br': _L2_ffn_in['br'], 'L2_ffn_Ws': _L2_ffn_in['Ws'], 'L2_ffn_bs': _L2_ffn_in['bs'], 'L2_ffn_temperature': _L2_ffn_in['temperature'], 'L2_ffn_query_embedding': _L2_ffn_in['query_embedding'], 'L3_xattn_Wq': _L3_xattn_in['Wq'], 'L3_xattn_Wk': _L3_xattn_in['Wk'], 'L3_xattn_Wv': _L3_xattn_in['Wv'], 'L3_xattn_Wo': _L3_xattn_in['Wo'], 'L3_ffn_Ws1': _L3_ffn_in['Ws1'], 'L3_ffn_Ws2': _L3_ffn_in['Ws2'], 'L3_ffn_W1': _L3_ffn_in['W1'], 'L3_ffn_W2': _L3_ffn_in['W2'], 'L3_ffn_Wr': _L3_ffn_in['Wr']}

def reference(x, ctx_1024, L0_xattn_w_q, L0_xattn_w_kv, L0_xattn_w_concat, L0_ffn_gate_w, L0_ffn_gate_b, L0_ffn_We1, L0_ffn_be1, L0_ffn_We2, L0_ffn_be2, L0_ffn_We3, L0_ffn_be3, L0_ffn_ws1, L0_ffn_bs1, L0_ffn_ws2, L0_ffn_bs2, L0_ffn_ws3, L0_ffn_bs3, L1_xattn_W_Q, L1_xattn_W_K, L1_xattn_W_V, L1_xattn_g_w, L1_xattn_g_b, L1_xattn_out_w, L1_xattn_out_b, L1_ffn_gate_w, L1_ffn_gate_b, L1_ffn_w1, L1_ffn_b1, L1_ffn_w2, L1_ffn_b2, L2_xattn_wq, L2_xattn_bq, L2_xattn_wk, L2_xattn_bk, L2_xattn_wv, L2_xattn_bv, L2_xattn_wo, L2_xattn_bo, L2_ffn_Wq, L2_ffn_bq, L2_ffn_Wk, L2_ffn_bk, L2_ffn_Wv, L2_ffn_bv, L2_ffn_Wp, L2_ffn_bp, L2_ffn_Wr, L2_ffn_br, L2_ffn_Ws, L2_ffn_bs, L2_ffn_temperature, L2_ffn_query_embedding, L3_xattn_Wq, L3_xattn_Wk, L3_xattn_Wv, L3_xattn_Wo, L3_ffn_Ws1, L3_ffn_Ws2, L3_ffn_W1, L3_ffn_W2, L3_ffn_Wr):
    import jax
    import jax.numpy as jnp

    def _L0_xattn_ref(q, kv, mem, w_q, w_kv, w_concat):
        import jax, jax.numpy as jnp
        import numpy as np
        D_MODEL = 256
        N_HEAD = 16
        D_HEAD = D_MODEL // N_HEAD
        B, L, D = q.shape
        c = jnp.concatenate([mem, kv], axis=1)
        qh = (q @ w_q).reshape(B, L, N_HEAD, D_HEAD).transpose(0, 2, 1, 3)
        kvp = c @ w_kv
        k, v = (kvp[..., :D_HEAD], kvp[..., D_HEAD:])
        attn_score = jnp.einsum('bhid,bjd->bhij', qh, k) / np.sqrt(D_HEAD)
        attn_prob = jax.nn.softmax(attn_score, axis=-1)
        out = jnp.einsum('bhij,bjd->bhid', attn_prob, v)
        out = out.transpose(0, 2, 1, 3).reshape(B, L, D)
        return out @ w_concat

    def _L0_ffn_ref(x, gate_w, gate_b, We1, be1, We2, be2, We3, be3, ws1, bs1, ws2, bs2, ws3, bs3):
        import jax, jax.numpy as jnp
        import numpy as np
        DIM = 256
        E = 16
        TOPK = 2
        G = 4
        TOPK_G = 2
        INTER = 128
        N_SHARED = 2
        ROUTE_SCALE = 1.0

        def _gate(xf, gate_w, gate_b):
            scores = xf @ gate_w.T
            scores = jax.nn.softmax(scores.astype(jnp.float32), axis=-1)
            orig = scores
            scores = scores + gate_b
            T = xf.shape[0]
            sg = scores.reshape(T, G, E // G)
            group_scores = jax.lax.top_k(sg, 2)[0].sum(-1)
            _, gidx = jax.lax.top_k(group_scores, TOPK_G)
            keep = jax.nn.one_hot(gidx, G).sum(axis=1) > 0
            sg = jnp.where(keep[:, :, None], sg, -jnp.inf)
            scores = sg.reshape(T, E)
            _, idx = jax.lax.top_k(scores, TOPK)
            weights = jnp.take_along_axis(orig, idx, axis=1)
            weights = (weights * ROUTE_SCALE).astype(xf.dtype)
            return (weights, idx)
        shape = x.shape
        xf = x.reshape(-1, DIM)
        weights, idx = _gate(xf, gate_w, gate_b)
        combine = (jax.nn.one_hot(idx, E, dtype=xf.dtype) * weights[..., None]).sum(1)
        h1 = jnp.einsum('td,edi->tei', xf, We1) + be1
        h3 = jnp.einsum('td,edi->tei', xf, We3) + be3
        h = jax.nn.silu(h1) * h3
        yo = jnp.einsum('tei,eid->ted', h, We2) + be2
        y = jnp.einsum('te,ted->td', combine, yo)
        z = jax.nn.silu(xf @ ws1 + bs1) * (xf @ ws3 + bs3) @ ws2 + bs2
        return (y + z).reshape(shape)

    def _L1_xattn_ref(query, key, value, W_Q, W_K, W_V, g_w, g_b, out_w, out_b):
        import jax, jax.numpy as jnp
        import numpy as np
        SCALE_BASE = 512.0
        GN_EPS = 1e-05

        def _xpos(x, downscale):
            L, D = (x.shape[-2], x.shape[-1])
            half = D // 2
            base = (jnp.arange(0, D, 2, dtype=jnp.float32) + 0.4 * D) / (1.4 * D)
            min_pos = -(L // 2)
            power = (jnp.arange(min_pos, min_pos + L, dtype=jnp.float32) / SCALE_BASE)[:, None]
            scale = base[None, :] ** power
            inv_freq = 1.0 / 10000.0 ** (jnp.arange(half, dtype=jnp.float32) / half)
            ang = jnp.arange(L, dtype=jnp.float32)[:, None] * inv_freq[None, :]
            sin, cos = (jnp.sin(ang), jnp.cos(ang))
            if downscale:
                scale = 1.0 / scale
            sin_s = jnp.repeat(sin * scale, 2, axis=-1)
            cos_s = jnp.repeat(cos * scale, 2, axis=-1)
            x1, x2 = (x[..., ::2], x[..., 1::2])
            rot = jnp.stack((-x2, x1), axis=-1).reshape(x.shape)
            return x * cos_s + rot * sin_s

        def _decay_mask(L, H):
            gammas = 1.0 - jnp.exp(jnp.linspace(np.log(1.0 / 32.0), np.log(1.0 / 512.0), H)).astype(jnp.float32)
            idx = jnp.arange(L)
            dist = idx[:, None] - idx[None, :]
            causal = dist >= 0
            d = jnp.maximum(dist, 0).astype(jnp.float32)
            return jnp.where(causal[None], gammas[:, None, None] ** d[None], 0.0)
        B, L, D = query.shape
        H = W_Q.shape[0]
        q = jnp.einsum('bld,hde->bhle', query, W_Q)
        k = jnp.einsum('bld,hde->bhle', key, W_K)
        v = jnp.einsum('bld,hde->bhle', value, W_V)
        q = _xpos(q, downscale=False)
        k = _xpos(k, downscale=True)
        sim = jnp.einsum('bhnd,bhsd->bhns', q, k) * _decay_mask(L, H)[None]
        ret = jnp.einsum('bhns,bhsd->bhnd', sim, v)
        mu = ret.mean(axis=-1, keepdims=True)
        var = ret.var(axis=-1, keepdims=True)
        ret = (ret - mu) / jnp.sqrt(var + GN_EPS)
        ret = ret.transpose(0, 2, 1, 3).reshape(B, L, D)
        gate = jax.nn.silu(query @ g_w.T + g_b)
        return ret * gate @ out_w.T + out_b

    def _L1_ffn_ref(x, gate_w, gate_b, w1, b1, w2, b2):
        import jax, jax.numpy as jnp
        import numpy as np
        B, S, D, E, K = (4, 512, 256, 8, 2)
        H = 4 * D
        Bx, Sx, Dx = x.shape
        n_exp = w1.shape[0]
        logits = jnp.einsum('bsd,de->bse', x, gate_w) + gate_b
        scores = jax.nn.softmax(logits, axis=-1)
        topk_s, topk_i = jax.lax.top_k(scores, K)
        onehot = jax.nn.one_hot(topk_i, n_exp, dtype=scores.dtype)
        dispatch = jnp.einsum('bske,bsk->bse', onehot, topk_s)
        xf = x.reshape(-1, Dx)
        wf = dispatch.reshape(-1, n_exp)
        out = jnp.zeros_like(xf)
        for i in range(n_exp):
            wi = wf[:, i:i + 1]
            h = jax.nn.relu(xf * wi @ w1[i] + b1[i])
            y = h @ w2[i] + b2[i]
            out = jnp.where(wi > 0, y, out)
        return out.reshape(Bx, Sx, Dx)

    def _L2_xattn_ref(queries, context, wq, bq, wk, bk, wv, bv, wo, bo):
        import jax, jax.numpy as jnp
        import numpy as np
        D_MODEL = 256
        N_HEADS = 16
        HEAD_DIM = D_MODEL // N_HEADS
        B, NQ, D = queries.shape
        S = context.shape[1]
        H, HD = (N_HEADS, HEAD_DIM)
        scale = HD ** (-0.5)
        q = queries @ wq.T + bq
        k = context @ wk.T + bk
        v = context @ wv.T + bv
        q = q.reshape(B, NQ, H, HD).transpose(0, 2, 1, 3)
        k = k.reshape(B, S, H, HD).transpose(0, 2, 1, 3)
        v = v.reshape(B, S, H, HD).transpose(0, 2, 1, 3)
        attn = jnp.einsum('bhnd,bhsd->bhns', q, k) * scale
        attn = jax.nn.softmax(attn, axis=-1)
        out = jnp.einsum('bhns,bhsd->bhnd', attn, v)
        out = out.transpose(0, 2, 1, 3).reshape(B, NQ, D)
        return out @ wo.T + bo

    def _L2_ffn_ref(x, Wq, bq, Wk, bk, Wv, bv, Wp, bp, Wr, br, Ws, bs, temperature, query_embedding):
        import jax, jax.numpy as jnp
        import numpy as np
        import math
        DIM = 256
        NUM_HEADS = 16
        SHARED_HEADS = 1
        ROUTED_HEADS = 3
        HEAD_DIM = DIM // NUM_HEADS
        B, N = (2, 512)
        Bsz, Nn, C = x.shape
        H, hd = (NUM_HEADS, HEAD_DIM)

        def heads(W, b):
            y = x @ W.T + b
            return y.reshape(Bsz, Nn, H, hd).transpose(0, 2, 1, 3)
        q = heads(Wq, bq)
        k = heads(Wk, bk)
        v = heads(Wv, bv)
        q_norm = q / jnp.linalg.norm(q, axis=-1, keepdims=True)
        q_scaled = (q_norm + query_embedding[None]) * jax.nn.softplus(temperature)[None]
        attn = jnp.einsum('bhqd,bhkd->bhqk', q_scaled, k) / math.sqrt(hd)
        attn = jax.nn.softmax(attn, axis=-1)
        h = jnp.einsum('bhqk,bhkd->bhqd', attn, v)
        h = h.transpose(0, 2, 1, 3).reshape(Bsz, Nn, C)
        gates = jax.nn.softmax(h @ Wr.T + br, axis=-1)
        _, idx = jax.lax.top_k(gates, ROUTED_HEADS)
        mask = jax.nn.one_hot(idx, H - SHARED_HEADS, dtype=gates.dtype).sum(axis=-2)
        routed_gates = gates * mask * ROUTED_HEADS
        sw = jax.nn.softmax(h @ Ws.T + bs, axis=-1)
        shared_gates = sw * SHARED_HEADS
        weight_0 = sw * 2.0
        shared_gates = weight_0[..., 0:1] * shared_gates
        routed_gates = weight_0[..., 1:2] * routed_gates
        masked_gates = jnp.concatenate([shared_gates, routed_gates], axis=-1)
        out = h * masked_gates.sum(axis=-1, keepdims=True)
        return out @ Wp.T + bp

    def _L3_xattn_ref(q, k, v, Wq, Wk, Wv, Wo):
        import jax, jax.numpy as jnp
        import numpy as np
        NUM_HEADS = 16
        EMBED_DIM = 256
        KEY_DIM = 64
        VALUE_DIM = 64
        NEG = -1000000000.0
        B, S, _ = q.shape
        query = jnp.einsum('bse,hed->bhsd', q, Wq)
        key_p = jnp.einsum('bse,hed->bhsd', k, Wk)
        value = jnp.einsum('bse,hed->bhsd', v, Wv)
        scores = jnp.einsum('bhqd,bhkd->bhqk', query, key_p) / jnp.sqrt(jnp.asarray(KEY_DIM, jnp.float32))
        causal = jnp.tril(jnp.ones((S, S), dtype=scores.dtype))
        scores = scores + (1.0 - causal) * NEG
        alphas = jax.nn.softmax(scores, axis=-1)
        attention = jnp.einsum('bhqk,bhkd->bhqd', alphas, value)
        attention = attention.reshape(B, S, NUM_HEADS * VALUE_DIM)
        out = jnp.einsum('bsf,fe->bse', attention, Wo)
        return out

    def _L3_ffn_ref(x, Ws1, Ws2, W1, W2, Wr):
        import jax, jax.numpy as jnp
        import numpy as np
        D_MODEL = 256
        EXPERT_DIM = 128
        N_EXPERTS = 8
        TOP_K = 2

        def _sq_relu(h):
            return jnp.square(jax.nn.relu(h))
        shape = x.shape
        xf = x.reshape(-1, D_MODEL)
        out_shared = _sq_relu(xf @ Ws1) @ Ws2
        logits = xf @ Wr
        top_vals, top_idx = jax.lax.top_k(logits, TOP_K)
        rw = jax.nn.softmax(top_vals.astype(jnp.float32), axis=-1).astype(x.dtype)
        onehot = jax.nn.one_hot(top_idx, N_EXPERTS, dtype=x.dtype)
        prob = jnp.einsum('tk,tke->te', rw, onehot)
        prob = jnp.trunc(prob)
        h = _sq_relu(jnp.einsum('td,edf->tef', xf, W1))
        y = jnp.einsum('tef,efd->ted', h, W2)
        out_routed = jnp.einsum('ted,te->td', y, prob)
        return (out_shared + out_routed).reshape(shape)
    x = x + _L0_xattn_ref(_layernorm(x, axis=-1), ctx_1024, ctx_1024, L0_xattn_w_q, L0_xattn_w_kv, L0_xattn_w_concat)
    x = x + _L0_ffn_ref(_layernorm(x, axis=-1), L0_ffn_gate_w, L0_ffn_gate_b, L0_ffn_We1, L0_ffn_be1, L0_ffn_We2, L0_ffn_be2, L0_ffn_We3, L0_ffn_be3, L0_ffn_ws1, L0_ffn_bs1, L0_ffn_ws2, L0_ffn_bs2, L0_ffn_ws3, L0_ffn_bs3)
    x = x + _L1_xattn_ref(_layernorm(x, axis=-1), ctx_1024, ctx_1024, L1_xattn_W_Q, L1_xattn_W_K, L1_xattn_W_V, L1_xattn_g_w, L1_xattn_g_b, L1_xattn_out_w, L1_xattn_out_b)
    x = x + _L1_ffn_ref(_layernorm(x, axis=-1), L1_ffn_gate_w, L1_ffn_gate_b, L1_ffn_w1, L1_ffn_b1, L1_ffn_w2, L1_ffn_b2)
    x = x + _L2_xattn_ref(_layernorm(x, axis=-1), ctx_1024, L2_xattn_wq, L2_xattn_bq, L2_xattn_wk, L2_xattn_bk, L2_xattn_wv, L2_xattn_bv, L2_xattn_wo, L2_xattn_bo)
    x = x + _L2_ffn_ref(_layernorm(x, axis=-1), L2_ffn_Wq, L2_ffn_bq, L2_ffn_Wk, L2_ffn_bk, L2_ffn_Wv, L2_ffn_bv, L2_ffn_Wp, L2_ffn_bp, L2_ffn_Wr, L2_ffn_br, L2_ffn_Ws, L2_ffn_bs, L2_ffn_temperature, L2_ffn_query_embedding)
    x = x + _L3_xattn_ref(_layernorm(x, axis=-1), ctx_1024, ctx_1024, L3_xattn_Wq, L3_xattn_Wk, L3_xattn_Wv, L3_xattn_Wo)
    x = x + _L3_ffn_ref(_layernorm(x, axis=-1), L3_ffn_Ws1, L3_ffn_Ws2, L3_ffn_W1, L3_ffn_W2, L3_ffn_Wr)
    return x

_drawn_inputs = setup_inputs


def setup_inputs(seed=0):
    import zlib

    import numpy as np

    out = dict(_drawn_inputs(seed))
    spreads = {'L0_ffn_gate_b': (0.0, 0.1),
     'L0_ffn_be1': (0.0, 0.274),
     'L0_ffn_be2': (0.0, 0.1),
     'L0_ffn_be3': (0.0, 0.333),
     'L0_ffn_bs1': (0.0, 0.1),
     'L0_ffn_bs2': (0.0, 0.1),
     'L0_ffn_bs3': (0.0, 0.1),
     'L1_xattn_g_b': (0.0, 0.1),
     'L1_xattn_out_b': (0.0, 0.1),
     'L1_ffn_gate_b': (0.0, 0.1),
     'L1_ffn_b1': (0.0, 0.1),
     'L1_ffn_b2': (0.0, 0.1),
     'L2_xattn_bq': (0.0, 0.544),
     'L2_xattn_bk': (0.0, 2.0),
     'L2_xattn_bv': (0.0, 0.1),
     'L2_xattn_bo': (0.0, 0.1),
     'L2_ffn_temperature': (4.151041507720947, 0.6)}
    factors = {'L2_ffn_Wq': 3.673,
     'L2_ffn_bq': 8.0,
     'L2_ffn_Wk': 3.681,
     'L2_ffn_bk': 64.0,
     'L2_ffn_Wr': 8.0,
     'L2_ffn_br': 8.0,
     'L2_ffn_Ws': 8.0,
     'L2_ffn_bs': 46.523,
     'L2_ffn_query_embedding': 8.0,
     'L3_xattn_Wq': 8.0,
     'L3_xattn_Wk': 8.0,
     'L3_ffn_Ws1': 3.505,
     'L3_ffn_Ws2': 3.117,
     'L2_ffn_bp': 2.743}
    for name, (base, spread) in spreads.items():
        noise = np.random.default_rng([zlib.crc32(name.encode()), seed]).standard_normal(out[name].shape)
        drawn = base * np.exp(spread * noise) if base else spread * noise
        out[name] = jnp.asarray(drawn.astype(out[name].dtype))
    for name, factor in factors.items():
        out[name] = (out[name] * factor).astype(out[name].dtype)
    return out
```

```python
from contextlib import ExitStack

import numpy as np
import concourse.bass as bass
from concourse import mybir

F32 = mybir.dt.float32
BF16 = mybir.dt.bfloat16
ALU = mybir.AluOpType
ACT = mybir.ActivationFunctionType
AX = mybir.AxisListType

P = 128
B, S, D = 8, 256, 256
TT = S // P
KD = D // P
NT = B * TT
H = 16
EPS = 1e-5


class Banks:

    def __init__(self, uses, n=2):
        self.bank = {u: i % n for i, u in enumerate(uses)}
        self.nth = {u: i // n for i, u in enumerate(uses)}
        self.per = [sum(1 for u in uses if self.bank[u] == k) for k in range(n)]

    def before(self, b, u):
        return b * self.per[self.bank[u]] + self.nth[u] + 1

    def after(self, b, u):
        return self.before(b, u) + 1


class Common:

    def __init__(self, nc, ctx, io):
        self.nc, self.io = nc, io
        sb = lambda n, s, t=F32: ctx.enter_context(nc.sbuf_tensor(f"g_{n}", s, t))
        self.x = sb("x_all", [P, NT, D])
        self.stats = sb("ln_stats", [P, NT, 6])
        self.mean = sb("ln_mean", [P, NT])
        self.rstd = sb("ln_rstd", [P, NT])
        self.tmp = sb("ln_tmp", [P, 4, NT])
        self.ident = sb("ident", [P, P])


def start_semaphores(nc, sems, from_one):
    numbers = sorted(x.num for x in sems + from_one)
    with nc.Block() as block:
        @block.sync
        def _(sp):
            start = numbers[0]
            for n, after in zip(numbers, numbers[1:] + [None]):
                if after != n + 1:
                    sp.sem_clear(range(start, n + 1))
                    start = after
            for x in from_one:
                sp.sem_inc(x, 1)


def load_x(nc, g):
    with ExitStack() as ctx:
        loaded = ctx.enter_context(nc.semaphore("x_loaded"))
        block = ctx.enter_context(nc.Block())

        @block.sync
        def _(sp):
            sp.dma_start(g.ident[:], g.io["c_ident"]).then_inc(loaded, 16)
            sp.dma_start(g.x[:], g.io["x"].rearrange("b (t p) d -> p (b t) d", p=P)).then_inc(loaded, 16)

        @block.vector
        def _(dve):
            dve.wait_ge(loaded, 32)
            for t in range(NT):
                dve.bn_stats(g.stats[:, t, :], g.x[:, t, :])


def norm_factors(dve, g, sqrt_in, sqrt_out):
    st, tmp = g.stats, g.tmp
    dve.tensor_tensor(g.mean[:], st[:, :, 1], st[:, :, 4], ALU.add)
    dve.tensor_tensor(tmp[:, 0, :], st[:, :, 1], st[:, :, 4], ALU.subtract)
    dve.tensor_tensor(tmp[:, 1, :], st[:, :, 2], st[:, :, 5], ALU.add)
    dve.drain()
    dve.tensor_scalar(g.mean[:], g.mean[:], 0.5, None, ALU.mult)
    dve.tensor_tensor(tmp[:, 0, :], tmp[:, 0, :], tmp[:, 0, :], ALU.mult)
    dve.tensor_scalar(tmp[:, 1, :], tmp[:, 1, :], 1.0 / D, EPS, ALU.mult, ALU.add)
    dve.drain()
    dve.scalar_tensor_tensor(out=tmp[:, 1, :], in0=tmp[:, 0, :], scalar=0.25, in1=tmp[:, 1, :],
                             op0=ALU.mult, op1=ALU.add).then_inc(sqrt_in, 1)
    dve.wait_ge(sqrt_out, 1)
    dve.reciprocal(g.rstd[:], tmp[:, 2, :])
    dve.drain()
    dve.tensor_tensor(tmp[:, 0, :], g.rstd[:], g.rstd[:], ALU.mult)
    dve.drain()
    dve.tensor_tensor(tmp[:, 0, :], tmp[:, 0, :], tmp[:, 1, :], ALU.mult)
    dve.drain()
    dve.tensor_scalar(tmp[:, 0, :], tmp[:, 0, :], -0.5, 1.5, ALU.mult, ALU.add)
    dve.drain()
    dve.tensor_tensor(g.rstd[:], g.rstd[:], tmp[:, 0, :], ALU.mult)
    dve.drain()


def norm_sqrt(act, g, sqrt_in, sqrt_out):
    act.wait_ge(sqrt_in, 1)
    act.activation(g.tmp[:, 2, :], g.tmp[:, 1, :], ACT.Sqrt).then_inc(sqrt_out, 1)


def normalise(dve, g, b, xn, ready):
    for t in range(TT):
        i = b * TT + t
        op = dve.tensor_scalar(xn[:, t, :], g.x[:, bass.ds(i, 1), :].rearrange("p a d -> p (a d)"),
                               g.mean[:, bass.ds(i, 1)], g.rstd[:, bass.ds(i, 1)], ALU.subtract, ALU.mult)
    if ready is not None:
        op.then_inc(ready, 1)


def add_to_x(dve, g, b, y):
    xb = g.x[:, bass.ds(b * TT, TT), :]
    op = dve.tensor_tensor(xb, xb, y, ALU.add)
    return op


def next_stats(dve, g, b):
    for t in range(TT):
        i = b * TT + t
        dve.bn_stats(g.stats[:, bass.ds(i, 1), :].rearrange("p a d -> p (a d)"),
                     g.x[:, bass.ds(i, 1), :].rearrange("p a d -> p (a d)"))


def transpose_xn(pe, g, xn, out):
    for k in range(KD):
        for t in range(TT):
            op = pe.transpose(out[:, k, t * P:(t + 1) * P], xn[:, t, k * P:(k + 1) * P], g.ident[:])
    return op


def attention(nc, g, name, hd, w, kv_from_x=False, shared_kv=False, causal=False, bias=False, router=False,
              interleave=False):
    io = g.io
    CQ = H * hd // P
    CK = 1 if shared_kv else CQ
    HC = P // hd
    HP = 32 if hd == 16 else 64
    HO = P // HP
    CO = H // HO
    KH = HC if shared_kv else H
    VH = 1 if shared_kv else H
    scale = float(hd) ** -0.5
    NQ = max(1, CQ // 2)
    NKB = max(1, CK // 2)
    NV = 1 if shared_kv else max(1, H * hd // D)
    gp_uses = (["xT"] + [f"q{i}" for i in range(NQ)] + [f"k{i}" for i in range(NKB)]
               + [f"v{i}" for i in range(NV)] + (["qT"] if router else []) + ["neg"]
               + (["gate"] if router else []) + ["y"])
    gp = Banks(gp_uses)
    SU = H // 2
    sc = Banks([("max", u) for u in range(SU)] + [("exp", u) for u in range(SU)])
    ot = Banks(list(range(CO)))

    with ExitStack() as ctx:
        sb = lambda n, s, t=F32: ctx.enter_context(nc.sbuf_tensor(f"{name}_sb_{n}", s, t))
        sems, from_one = [], []

        def sem(n, one=False):
            s = ctx.enter_context(nc.semaphore(f"{name}_{n}"))
            (from_one if one else sems).append(s)
            return s
        wq = sb("wq", [P, KD, H * hd])
        wk = sb("wk", [P, KD, CK * P])
        wv = sb("wv", [P, KD, VH * hd])
        wo = sb("wo", [P, CO, D])
        mask = sb("mask", [P, HC])
        sel = sb("sel", [P, H, P], BF16)
        xn = sb("xn", [P, TT, D])
        xnT = sb("xnT", [P, KD, S])
        kvT = xnT if kv_from_x else sb("kvT", [P, KD, S])
        qT = sb("qT", [P, CQ, S])
        kT = sb("kT", [P, CK, S])
        kM = sb("kM", [P, KH, S])
        v = sb("v", [P, TT, VH, HP])
        ones = sb("ones", [P, HP])
        mx = sb("mx", [P, TT, H])
        negT = sb("negT", [P, S], BF16)
        rest = sb("rest", [H, S])
        probs = sb("probs", [P, 2, HO, TT, S])
        rden = sb("rden", [P, 2, S])
        oT = sb("oT", [P, CO, S])
        if causal:
            eye = sb("eye", [P, P], BF16)
            neg_qk = sb("neg_qk", [P, P], BF16)
            neg_kq = sb("neg_kq", [P, P], BF16)
        if bias:
            bq = sb("bq", [P, CQ])
            bk = sb("bk", [P, CK])
            bv = sb("bv", [P, D])
            bo = sb("bo", [P, D])
        if router:
            bqt = sb("bqt", [P, D])
            qe = sb("qe", [P, D])
            sp_t = sb("sp_t", [P, 4, H])
            spq = sb("spq", [P, H])
            qtm = sb("qtm", [P, TT, D])
            qsq = sb("qsq", [P, TT, D])
            qn = sb("qn", [P, 3, TT, H])
            wr = sb("wr", [P, CO, H + 1])
            br = sb("br", [P, H + 1])
            lg = sb("lg", [P, TT, 24])
            le = sb("le", [P, TT, 24])
            top = sb("top", [P, TT, 8])
            sm = sb("sm", [P, TT, 8])
            yt = sb("yt", [P, TT, D])
        GP = [ctx.enter_context(nc.psum_tensor(f"{name}_gp{i}", [P, 2, S], F32)) for i in range(2)]
        SC = [ctx.enter_context(nc.psum_tensor(f"{name}_sc{i}", [P, 2, 2, S], F32)) for i in range(2)]
        OT = [ctx.enter_context(nc.psum_tensor(f"{name}_ot{i}", [P, 2, S], F32)) for i in range(2)]

        weights_in = sem("weights_in")
        kv_in = sem("kv_in")
        sqrt_in, sqrt_out = sem("sqrt_in"), sem("sqrt_out")
        fixed = sem("fixed")
        xn_ready = sem("xn_ready")
        q_sums = sem("q_sums")
        q_roots = sem("q_roots")
        q_scaled = sem("q_scaled")
        softplus = sem("softplus")
        gate_in, gate_exp = sem("gate_in"), sem("gate_exp")
        km_ready = sem("km_ready")
        act_step = sem("act_step")
        gp_full = [sem(f"gp_full{i}", one=True) for i in range(2)]
        gp_read = [sem(f"gp_read{i}", one=True) for i in range(2)]
        sc_full = [sem(f"sc_full{i}", one=True) for i in range(2)]
        sc_read = [sem(f"sc_read{i}", one=True) for i in range(2)]
        ot_full = [sem(f"ot_full{i}", one=True) for i in range(2)]
        ot_read = [sem(f"ot_read{i}", one=True) for i in range(2)]

        def gp_wait(eng, sems, b, u, after):
            eng.wait_ge(sems[gp.bank[u]], gp.after(b, u) if after else gp.before(b, u))

        loads = [(wq, w["wq"].rearrange("(k p) n -> p k n", p=P)),
                 (wk, w["wk"].rearrange("(k p) n -> p k n", p=P)),
                 (wv, w["wv"].rearrange("(k p) n -> p k n", p=P)),
                 (wo, w["wo"].rearrange("(c p) n -> p c n", p=P)),
                 (mask, io[f"c_mask{hd}"]), (sel, io["c_sel"])]
        if causal:
            loads += [(eye, io["c_eye"]), (neg_qk, io["c_neg_qk"]), (neg_kq, io["c_neg_kq"])]
        if bias:
            loads += [(bk, w["bk"]),
                      (bv, w["bv"].rearrange("(a n) -> a n", a=1).broadcast_to([P, D])),
                      (bo, w["bo"].rearrange("(a n) -> a n", a=1).broadcast_to([P, D]))]
            if not router:
                loads += [(bq, w["bq"])]
        if router:
            loads += [(bqt, w["bq"].rearrange("(a n) -> a n", a=1).broadcast_to([P, D])),
                      (qe, w["qe"].rearrange("(a n) -> a n", a=1).broadcast_to([P, D])),
                      (sp_t[:, 0, :], w["temp"].rearrange("(a n) -> a n", a=1).broadcast_to([P, H])),
                      (wr, w["wr"].rearrange("(c p) n -> p c n", p=P)),
                      (br, w["br"].rearrange("(a n) -> a n", a=1).broadcast_to([P, H + 1]))]
        all_in = 16 * len(loads)

        start_semaphores(nc, sems, from_one)
        block = ctx.enter_context(nc.Block())

        @block.sync
        def _(sp):
            for dst, src in loads:
                sp.dma_start(dst if isinstance(dst, bass.AP) else dst[:], src).then_inc(weights_in, 16)
            if not kv_from_x:
                with sp.Fori(0, B) as b:
                    u = f"v{NV - 1}"
                    sp.wait_ge(gp_full[gp.bank[u]], b * gp.per[gp.bank[u]] + 1)
                    sp.dma_start(kvT[:], io["ctxT"][b].rearrange("(k p) s -> p k s", p=P)).then_inc(kv_in, 16)

        @block.gpsimd
        def _(pool):
            pool.memset(v[:], 0.0).then_inc(fixed, 1)
            pool.memset(ones[:], 1.0).then_inc(fixed, 1)
            pool.memset(negT[:], 0.0).then_inc(fixed, 1)
            pool.wait_ge(weights_in, all_in)
            with pool.Fori(0, B) as b:
                for i in range(NKB):
                    gp_wait(pool, gp_read, b, f"k{i}", True)
                    for c in range(2 * i, min(2 * i + 2, CK)):
                        out = kM[:, c * HC:(c + 1) * HC, :]
                        op = pool.tensor_tensor(out, kT[:, c:c + 1, :].broadcast_to([P, HC, S]),
                                                mask[:].rearrange("p (h a) -> p h a", a=1).broadcast_to([P, HC, S]),
                                                ALU.mult)
                op.then_inc(km_ready, 1)

        @block.scalar
        def _(act):
            norm_sqrt(act, g, sqrt_in, sqrt_out)
            act.wait_ge(weights_in, all_in)
            if router:
                act.activation(sp_t[:, 1, :], sp_t[:, 0, :], ACT.Abs).then_inc(act_step, 1)
                act.wait_ge(act_step, 1)
                act.activation(sp_t[:, 1, :], sp_t[:, 1, :], ACT.Exp, scale=-1.0).then_inc(act_step, 1)
                act.wait_ge(act_step, 2)
                act.activation(sp_t[:, 2, :], sp_t[:, 1, :], ACT.Ln, bias=1.0).then_inc(softplus, 1)
            with act.Fori(0, B) as b:
                gp_wait(act, gp_full, b, "xT", True)
                act.activation(xnT[:], GP[gp.bank["xT"]][:], ACT.Copy).then_inc(gp_read[gp.bank["xT"]], 1)
                for i in range(NQ) if not router else []:
                    u = f"q{i}"
                    gp_wait(act, gp_full, b, u, True)
                    n = min(2, CQ - 2 * i)
                    if bias:
                        for c in range(n):
                            op = act.activation(qT[:, 2 * i + c, :], GP[gp.bank[u]][:, c, :], ACT.Identity,
                                                bias=bq[:, 2 * i + c:2 * i + c + 1])
                    else:
                        op = act.activation(qT[:, 2 * i:2 * i + n, :], GP[gp.bank[u]][:, 0:n, :], ACT.Copy)
                    op.then_inc(gp_read[gp.bank[u]], 1)
                for i in range(NKB):
                    u = f"k{i}"
                    gp_wait(act, gp_full, b, u, True)
                    n = min(2, CK - 2 * i)
                    if bias:
                        for c in range(n):
                            op = act.activation(kT[:, 2 * i + c, :], GP[gp.bank[u]][:, c, :], ACT.Identity,
                                                bias=bk[:, 2 * i + c:2 * i + c + 1])
                    else:
                        op = act.activation(kT[:, 2 * i:2 * i + n, :], GP[gp.bank[u]][:, 0:n, :], ACT.Copy)
                    op.then_inc(gp_read[gp.bank[u]], 1)
                if router:
                    act.wait_ge(q_sums, b + 1)
                    act.activation(qn[:, 1], qn[:, 0], ACT.Sqrt).then_inc(q_roots, 1)
                    gp_wait(act, gp_full, b, "qT", True)
                    act.activation(qT[:], GP[gp.bank["qT"]][:], ACT.Copy).then_inc(gp_read[gp.bank["qT"]], 1)
                for u in range(SU):
                    use = ("exp", u)
                    pair = sc.bank[use]
                    c = 2 * u // HO
                    if 2 * u % HO == 0:
                        if c >= 2:
                            act.wait_ge(ot_full[c % 2], ot.before(b, c))
                        else:
                            act.wait_ge(ot_full[c % 2], b * ot.per[c % 2] + 1)
                    act.wait_ge(sc_full[pair], sc.after(b, use))
                    h0 = 2 * u % HO
                    pr = probs[:, c % 2, h0:h0 + 2]
                    if causal:
                        act.activation(pr[:, :, 0, :], SC[pair][:, :, 0, :], ACT.Exp, scale=scale)
                        act.activation(pr[:, :, 1, P:S], SC[pair][:, :, 1, P:S], ACT.Exp, scale=scale)\
                           .then_inc(sc_read[pair], 1)
                    else:
                        act.activation(pr, SC[pair][:], ACT.Exp, scale=scale).then_inc(sc_read[pair], 1)
                if router:
                    act.wait_ge(gate_in, b + 1)
                    act.activation(le[:, :, 0:H + 1], lg[:, :, 0:H + 1], ACT.Exp).then_inc(gate_exp, 1)

        @block.tensor
        def _(pe):
            pe.wait_ge(weights_in, all_in)
            pe.wait_ge(fixed, 3)
            def proj(b, u, wgt, cols, rhs, n0):
                gp_wait(pe, gp_read, b, u, False)
                for c in range(cols):
                    for k in range(KD):
                        op = pe.matmul(GP[gp.bank[u]][:, c, :], wgt[:, k, (n0 + c) * P:(n0 + c + 1) * P],
                                       rhs[:, k, :], start=(k == 0), stop=(k == KD - 1))
                op.then_inc(gp_full[gp.bank[u]], 1)

            with pe.Fori(0, B) as b:
                pe.wait_ge(xn_ready, b + 1)
                gp_wait(pe, gp_read, b, "xT", False)
                transpose_xn(pe, g, xn, GP[gp.bank["xT"]]).then_inc(gp_full[gp.bank["xT"]], 1)
                gp_wait(pe, gp_read, b, "xT", True)
                if router:
                    u = "q0"
                    gp_wait(pe, gp_read, b, u, False)
                    for t in range(TT):
                        for k in range(KD):
                            op = pe.matmul(GP[gp.bank[u]][:, t, :], xnT[:, k, t * P:(t + 1) * P], wq[:, k, :],
                                           start=(k == 0), stop=(k == KD - 1))
                    op.then_inc(gp_full[gp.bank[u]], 1)
                else:
                    for i in range(NQ):
                        proj(b, f"q{i}", wq, 2, xnT, 2 * i)
                if not kv_from_x:
                    pe.wait_ge(kv_in, 16 * b + 16)
                for i in range(NKB):
                    proj(b, f"k{i}", wk, min(2, CK), kvT, 2 * i)
                VW = min(VH * hd, D)
                for i in range(NV):
                    u = f"v{i}"
                    gp_wait(pe, gp_read, b, u, False)
                    for t in range(TT):
                        for k in range(KD):
                            op = pe.matmul(GP[gp.bank[u]][:, t, 0:VW], kvT[:, k, t * P:(t + 1) * P],
                                           wv[:, k, i * VW:(i + 1) * VW], start=(k == 0), stop=(k == KD - 1))
                    op.then_inc(gp_full[gp.bank[u]], 1)

                if router:
                    pe.wait_ge(q_scaled, b + 1)
                    gp_wait(pe, gp_read, b, "qT", False)
                    transpose_xn(pe, g, qtm, GP[gp.bank["qT"]]).then_inc(gp_full[gp.bank["qT"]], 1)
                gp_wait(pe, gp_read, b, "qT" if router else f"q{NQ - 1}", True)
                gp_wait(pe, gp_read, b, f"k{NKB - 1}", True)
                pe.wait_ge(km_ready, b + 1)
                for u in range(SU):
                    use = ("max", u)
                    pair = sc.bank[use]
                    pe.wait_ge(sc_read[pair], sc.before(b, use))
                    for j in range(2):
                        h = 2 * u + j
                        for t in range(TT):
                            keys = (t + 1) * P if causal else S
                            out = SC[pair][:, j, t, 0:keys]
                            op = pe.matmul(out, qT[:, h // HC, t * P:(t + 1) * P], kM[:, h % KH, 0:keys],
                                           start=True, stop=True)
                            if causal:
                                op = pe.matmul(SC[pair][:, j, t, t * P:keys], eye[:], neg_qk[:],
                                               start=False, stop=True, skip_group_check=True)
                    op.then_inc(sc_full[pair], 1)

                gp_wait(pe, gp_read, b, "neg", False)
                for pair in range(2):
                    u = SU - 2 + pair
                    pe.wait_ge(sc_read[pair], sc.after(b, ("max", u)))
                for t in range(TT):
                    op = pe.transpose(GP[gp.bank["neg"]][0:H, 0, t * P:(t + 1) * P], mx[:, t, :], g.ident[:])
                op.then_inc(gp_full[gp.bank["neg"]], 1)

                def scores(u):
                    use = ("exp", u)
                    pair = sc.bank[use]
                    pe.wait_ge(sc_read[pair], sc.before(b, use))
                    for j in range(2):
                        h = 2 * u + j
                        for t in range(TT):
                            q0 = t * P if causal else 0
                            out = SC[pair][:, j, t, q0:S]
                            pe.matmul(out, kM[:, h % KH, t * P:(t + 1) * P], qT[:, h // HC, q0:S],
                                      start=True, stop=False)
                            op = pe.matmul(out, sel[:, h, :], negT[:, q0:S], start=False, stop=True)
                            if causal:
                                op = pe.matmul(SC[pair][:, j, t, t * P:(t + 1) * P], eye[:], neg_kq[:],
                                               start=False, stop=True, skip_group_check=True)
                    op.then_inc(sc_full[pair], 1)

                def weigh(c):
                    for u in range(c * HO // 2, (c + 1) * HO // 2):
                        use = ("exp", u)
                        pe.wait_ge(sc_read[sc.bank[use]], sc.after(b, use))
                    pe.wait_ge(ot_read[c % 2], ot.before(b, c))
                    if interleave:
                        for what in range(2):
                            for j in range(HO):
                                h = c * HO + j
                                for t in range(TT):
                                    q0 = t * P if causal else 0
                                    for par in range(2):
                                        lhs = v[:, t, h, :] if what == 0 else ones[:]
                                        op = pe.matmul(OT[c % 2][par * HP:(par + 1) * HP, what,
                                                                 j * P + q0 // 2:(j + 1) * P], lhs,
                                                       probs[:, c % 2, j, t, q0 + par:S:2],
                                                       start=(t == 0), stop=(t == TT - 1))
                        op.then_inc(ot_full[c % 2], 1)
                        return
                    for what in range(2):
                        for t in range(TT):
                            q0 = t * P if causal else 0
                            for j in range(HO):
                                h = c * HO + j
                                lhs = v[:, t, h % VH, :] if what == 0 else ones[:]
                                op = pe.matmul(OT[c % 2][j * HP:(j + 1) * HP, what, q0:S], lhs,
                                               probs[:, c % 2, j, t, q0:S], start=(t == 0), stop=(t == TT - 1))
                    op.then_inc(ot_full[c % 2], 1)

                gp_wait(pe, gp_read, b, "neg", True)
                gp_wait(pe, gp_read, b, f"v{NV - 1}", True)
                done = 0
                for u in range(SU):
                    scores(u)
                    ready = 2 * u // HO
                    while done < ready:
                        weigh(done)
                        done += 1
                while done < CO:
                    weigh(done)
                    done += 1

                for i in range(2):
                    pe.wait_ge(ot_read[i], ot.after(b, CO - 2 + i))
                for u, wgt, n in ([("gate", wr, H + 1)] if router else []) + [("y", wo, D)]:
                    gp_wait(pe, gp_read, b, u, False)
                    for t in range(TT):
                        for c in range(CO):
                            if interleave:
                                lhs = oT[:].rearrange("p c (j i r) -> p r (c j) i", j=HO, r=CO)[:, c, 8 * t:8 * t + 8, :]
                            else:
                                lhs = oT[:, c, t * P:(t + 1) * P]
                            op = pe.matmul(GP[gp.bank[u]][:, t, 0:n], lhs, wgt[:, c, :],
                                           start=(c == 0), stop=(c == CO - 1))
                    op.then_inc(gp_full[gp.bank[u]], 1)

        @block.vector
        def _(dve):
            over_tokens = lambda row: row[:].rearrange("p (a n) -> p a n", a=1).broadcast_to([P, TT, D])

            def gate_logits(b):
                gp_wait(dve, gp_full, b, "gate", True)
                dve.tensor_tensor(lg[:, :, 0:H + 1], GP[gp.bank["gate"]][:, :, 0:H + 1],
                                  br[:].rearrange("p (a n) -> p a n", a=1).broadcast_to([P, TT, H + 1]), ALU.add)\
                   .then_inc(gp_read[gp.bank["gate"]], 1)
                dve.drain()
                for i, (lo, hi) in enumerate(((0, H - 1), (H - 1, H + 1))):
                    dve.tensor_reduce(sm[:, :, i], lg[:, :, lo:hi], AX.X, ALU.max)
                dve.drain()
                for i, (lo, hi) in enumerate(((0, H - 1), (H - 1, H + 1))):
                    op = dve.tensor_tensor(lg[:, :, lo:hi], lg[:, :, lo:hi],
                                           sm[:, :, i:i + 1].broadcast_to([P, TT, hi - lo]), ALU.subtract)
                op.then_inc(gate_in, 1)

            def gate_factor(b):
                dve.wait_ge(gate_exp, b + 1)
                for i, (lo, hi) in enumerate(((0, H - 1), (H - 1, H + 1))):
                    dve.tensor_reduce(sm[:, :, i], le[:, :, lo:hi], AX.X, ALU.add)
                for t in range(TT):
                    dve.max(top[:, t, :], le[:, t, 0:H - 1])
                dve.drain()
                dve.tensor_reduce(sm[:, :, 2], top[:, :, 0:3], AX.X, ALU.add)
                dve.reciprocal(sm[:, :, 3:5], sm[:, :, 0:2])
                dve.drain()
                dve.tensor_tensor(sm[:, :, 2], sm[:, :, 2], sm[:, :, 3], ALU.mult)
                dve.tensor_tensor(sm[:, :, 5:7], le[:, :, H - 1:H + 1], sm[:, :, 4:5].broadcast_to([P, TT, 2]), ALU.mult)
                dve.drain()
                dve.tensor_tensor(sm[:, :, 0], sm[:, :, 5], sm[:, :, 6], ALU.add)
                dve.tensor_tensor(sm[:, :, 1], sm[:, :, 6], sm[:, :, 2], ALU.mult)
                dve.drain()
                dve.tensor_tensor(sm[:, :, 0], sm[:, :, 0], sm[:, :, 5], ALU.mult)
                dve.tensor_scalar(sm[:, :, 1], sm[:, :, 1], 3.0, None, ALU.mult)
                dve.drain()
                dve.tensor_tensor(sm[:, :, 0], sm[:, :, 0], sm[:, :, 1], ALU.add)
                dve.drain()
                dve.tensor_scalar(sm[:, :, 7], sm[:, :, 0], 2.0, None, ALU.mult)
                dve.drain()

            norm_factors(dve, g, sqrt_in, sqrt_out)
            dve.wait_ge(weights_in, all_in)
            dve.wait_ge(fixed, 3)
            if router:
                dve.wait_ge(softplus, 1)
                dve.tensor_scalar(sp_t[:, 3, :], sp_t[:, 0, :], 0.0, None, ALU.max)
                dve.drain()
                dve.tensor_tensor(spq[:], sp_t[:, 3, :], sp_t[:, 2, :], ALU.add)
                dve.drain()
                qeh = qe[:].rearrange("p (h d) -> p h d", d=hd)
                dve.tensor_tensor(qeh, qeh, spq[:].rearrange("p (h a) -> p h a", a=1).broadcast_to([P, H, hd]), ALU.mult)
                dve.drain()
            with dve.Fori(0, B) as b:
                normalise(dve, g, b, xn, xn_ready)
                if router:
                    gp_wait(dve, gp_full, b, "q0", True)
                    dve.tensor_tensor(qtm[:], GP[gp.bank["q0"]][:], over_tokens(bqt), ALU.add)\
                       .then_inc(gp_read[gp.bank["q0"]], 1)
                    dve.drain()
                    dve.tensor_tensor(qsq[:], qtm[:], qtm[:], ALU.mult)
                    dve.drain()
                    dve.tensor_reduce(qn[:, 0], qsq[:].rearrange("p t (h d) -> p t h d", d=hd), AX.X, ALU.add)\
                       .then_inc(q_sums, 1)
                for i in range(NV):
                    u = f"v{i}"
                    gp_wait(dve, gp_full, b, u, True)
                    if shared_kv:
                        op = dve.tensor_copy(v[:, :, 0, 0:hd], GP[gp.bank[u]][:, :, 0:hd])
                    else:
                        hv = D // hd
                        src = GP[gp.bank[u]][:].rearrange("p t (h d) -> p t h d", d=hd)
                        for t in range(TT):
                            dst = v[:, t, i * hv:(i + 1) * hv, 0:hd]
                            if bias:
                                op = dve.tensor_tensor(dst, src[:, t], bv[:].rearrange("p (h d) -> p h d", d=hd), ALU.add)
                            else:
                                op = dve.tensor_copy(dst, src[:, t])
                    op.then_inc(gp_read[gp.bank[u]], 1)
                if router:
                    dve.wait_ge(q_roots, b + 1)
                    dve.reciprocal(qn[:, 2], qn[:, 1])
                    dve.drain()
                    dve.tensor_tensor(qn[:, 1], qn[:, 2], qn[:, 2], ALU.mult)
                    dve.drain()
                    dve.tensor_tensor(qn[:, 1], qn[:, 1], qn[:, 0], ALU.mult)
                    dve.drain()
                    dve.tensor_scalar(qn[:, 1], qn[:, 1], -0.5, 1.5, ALU.mult, ALU.add)
                    dve.drain()
                    dve.tensor_tensor(qn[:, 2], qn[:, 2], qn[:, 1], ALU.mult)
                    dve.drain()
                    dve.tensor_tensor(qn[:, 2], qn[:, 2],
                                      spq[:].rearrange("p (a h) -> p a h", a=1).broadcast_to([P, TT, H]), ALU.mult)
                    dve.drain()
                    qh = qtm[:].rearrange("p t (h d) -> p t h d", d=hd)
                    dve.tensor_tensor(qh, qh, qn[:, 2].rearrange("p t (h a) -> p t h a", a=1)
                                      .broadcast_to([P, TT, H, hd]), ALU.mult)
                    dve.drain()
                    dve.tensor_tensor(qtm[:], qtm[:], over_tokens(qe), ALU.add).then_inc(q_scaled, 1)
                for u in range(SU):
                    use = ("max", u)
                    pair = sc.bank[use]
                    dve.wait_ge(sc_full[pair], sc.after(b, use))
                    for t in range(TT):
                        keys = (t + 1) * P if causal else S
                        op = dve.tensor_reduce(mx[:, t, 2 * u:2 * u + 2], SC[pair][:, :, t, 0:keys], AX.X, ALU.max,
                                               negate=True)
                    op.then_inc(sc_read[pair], 1)
                u = "neg"
                gp_wait(dve, gp_full, b, u, True)
                src = GP[gp.bank[u]][0:H, 0, :]
                dve.tensor_copy(negT[0:H, :], src)
                dve.drain()
                dve.tensor_tensor(rest[:], src, negT[0:H, :], ALU.subtract)
                dve.drain()
                dve.tensor_copy(negT[32:32 + H, :], rest[:])
                dve.drain()
                dve.tensor_tensor(negT[64:64 + H, :], rest[:], negT[32:32 + H, :], ALU.subtract)\
                   .then_inc(gp_read[gp.bank[u]], 1)
                for c in range(CO):
                    dve.wait_ge(ot_full[c % 2], ot.after(b, c))
                    dve.reciprocal(rden[:, c % 2], OT[c % 2][:, 1, :])
                    dve.drain()
                    dve.tensor_tensor(oT[:, c, :], OT[c % 2][:, 0, :], rden[:, c % 2], ALU.mult).then_inc(ot_read[c % 2], 1)
                if router:
                    gate_logits(b)
                    gate_factor(b)
                    gp_wait(dve, gp_full, b, "y", True)
                    for t in range(TT):
                        op = dve.scalar_tensor_tensor(out=yt[:, t], in0=GP[gp.bank["y"]][:, t], scalar=sm[:, t, 7:8],
                                                      in1=bo[:], op0=ALU.mult, op1=ALU.add)
                    op.then_inc(gp_read[gp.bank["y"]], 1)
                    dve.drain()
                    add_to_x(dve, g, b, yt[:])
                else:
                    gp_wait(dve, gp_full, b, "y", True)
                    add_to_x(dve, g, b, GP[gp.bank["y"]][:]).then_inc(gp_read[gp.bank["y"]], 1)
                    if bias:
                        dve.drain()
                        add_to_x(dve, g, b, over_tokens(bo))
                dve.drain()
                next_stats(dve, g, b)
                dve.drain()


def root(dve, out, square, inverse, half):
    dve.tensor_tensor(half, inverse, inverse, ALU.mult)
    dve.drain()
    dve.tensor_tensor(half, half, square, ALU.mult)
    dve.drain()
    dve.tensor_scalar(half, half, -0.5, 1.5, ALU.mult, ALU.add)
    dve.drain()
    dve.tensor_tensor(out, inverse, half, ALU.mult)
    dve.drain()


def retention(nc, g, name, w):
    io = g.io
    hd = 16
    CQ, HC, HP, HO, CO = 2, 8, 32, 4, 4
    SU = H // 2
    gp = Banks(["xT", "q0", "k0", "qr", "kr", "v0", "g0", "T0", "T1", "aT", "y"])
    sc = Banks(list(range(SU)))
    ot = Banks(list(range(CO)))
    with ExitStack() as ctx:
        sb = lambda n, s, t=F32: ctx.enter_context(nc.sbuf_tensor(f"{name}_sb_{n}", s, t))
        sems, from_one = [], []

        def sem(n, one=False):
            s = ctx.enter_context(nc.semaphore(f"{name}_{n}"))
            (from_one if one else sems).append(s)
            return s
        wq, wk, wv, wg, wo = (sb(n, [P, KD, D]) for n in ("wq", "wk", "wv", "wg", "wo"))
        turn = sb("turn", [P, P])
        mask = sb("mask", [P, HC])
        tri = sb("tri", [P, P])
        tables = sb("tables", [P, 4, CQ, S])
        gb, bo = sb("gb", [P, D]), sb("bo", [P, D])
        xn = sb("xn", [P, TT, D])
        xnT = sb("xnT", [P, KD, S])
        kvT = sb("kvT", [P, KD, S])
        raw = sb("raw", [P, 2, CQ, S])
        qk = sb("qk", [P, 2, CQ, S])
        part = sb("part", [P, 2, CQ, S])
        kM = sb("kM", [P, H, S])
        v = sb("v", [P, TT, H, HP])
        sim = sb("sim", [P, 2, HO, TT, S])
        oraw = sb("oraw", [P, CO, S])
        ret = sb("ret", [P, TT, D])
        sq = sb("sq", [P, TT, D])
        gn = sb("gn", [P, 4, TT, H])
        gz = sb("gz", [P, TT, D])
        gate = sb("gate", [P, TT, D])
        aT = sb("aT", [P, KD, S])
        GP = [ctx.enter_context(nc.psum_tensor(f"{name}_gp{i}", [P, 2, S], F32)) for i in range(2)]
        SC = [ctx.enter_context(nc.psum_tensor(f"{name}_sc{i}", [P, 2, 2, S], F32)) for i in range(2)]
        OT = [ctx.enter_context(nc.psum_tensor(f"{name}_ot{i}", [P, 2, S], F32)) for i in range(2)]

        weights_in, kv_in = sem("weights_in"), sem("kv_in")
        sqrt_in, sqrt_out, fixed = sem("sqrt_in"), sem("sqrt_out"), sem("fixed")
        xn_ready, turned, km_ready = sem("xn_ready"), sem("turned"), sem("km_ready")
        gate_z, gate_ready = sem("gate_z"), sem("gate_ready")
        variance, deviation, ret_ready = sem("variance"), sem("deviation"), sem("ret_ready")
        gp_full = [sem(f"gp_full{i}", one=True) for i in range(2)]
        gp_read = [sem(f"gp_read{i}", one=True) for i in range(2)]
        sc_full = [sem(f"sc_full{i}", one=True) for i in range(2)]
        sc_read = [sem(f"sc_read{i}", one=True) for i in range(2)]
        ot_full = [sem(f"ot_full{i}", one=True) for i in range(2)]
        ot_read = [sem(f"ot_read{i}", one=True) for i in range(2)]

        def full(eng, b, u):
            eng.wait_ge(gp_full[gp.bank[u]], gp.after(b, u))

        def free(eng, b, u):
            eng.wait_ge(gp_read[gp.bank[u]], gp.before(b, u))

        def read(eng, b, u):
            eng.wait_ge(gp_read[gp.bank[u]], gp.after(b, u))

        row = lambda a: a.rearrange("(a n) -> a n", a=1).broadcast_to([P, D])
        loads = [(t[:], w[n].rearrange("(k p) n -> p k n", p=P))
                 for t, n in ((wq, "wq"), (wk, "wk"), (wv, "wv"), (wg, "wg"), (wo, "wo"))]
        loads += [(turn[:], io["c_turn"]), (mask[:], io["c_mask16"]), (tri[:], io["c_tri"]),
                  (tables[:], io["c_tables"]), (gb[:], row(w["gb"])), (bo[:], row(w["bo"]))]
        all_in = 16 * len(loads)
        start_semaphores(nc, sems, from_one)
        block = ctx.enter_context(nc.Block())

        @block.sync
        def _(sp):
            for dst, src in loads:
                sp.dma_start(dst, src).then_inc(weights_in, 16)
            with sp.Fori(0, B) as b:
                sp.wait_ge(gp_full[gp.bank["v0"]], b * gp.per[gp.bank["v0"]] + 1)
                sp.dma_start(kvT[:], io["ctxT"][b].rearrange("(k p) s -> p k s", p=P)).then_inc(kv_in, 16)

        @block.gpsimd
        def _(pool):
            pool.memset(v[:], 0.0).then_inc(fixed, 1)
            pool.wait_ge(weights_in, all_in)
            with pool.Fori(0, B) as b:
                pool.wait_ge(turned, 2 * b + 2)
                for c in range(CQ):
                    op = pool.tensor_tensor(kM[:, c * HC:(c + 1) * HC, :],
                                            qk[:, 1, c:c + 1, :].broadcast_to([P, HC, S]),
                                            mask[:].rearrange("p (h a) -> p h a", a=1).broadcast_to([P, HC, S]),
                                            ALU.mult)
                op.then_inc(km_ready, 1)

        @block.scalar
        def _(act):
            norm_sqrt(act, g, sqrt_in, sqrt_out)
            with act.Fori(0, B) as b:
                def evac(dst, u):
                    full(act, b, u)
                    act.activation(dst, GP[gp.bank[u]][:], ACT.Copy).then_inc(gp_read[gp.bank[u]], 1)
                evac(xnT[:], "xT")
                evac(raw[:, 0], "q0")
                evac(raw[:, 1], "k0")
                act.wait_ge(gate_z, b + 1)
                act.activation(gate[:], gz[:], ACT.Silu).then_inc(gate_ready, 1)
                for c in range(CO):
                    act.wait_ge(ot_full[c % 2], ot.after(b, c))
                    act.activation(oraw[:, c, :], OT[c % 2][:, 0, :], ACT.Copy).then_inc(ot_read[c % 2], 1)
                act.wait_ge(variance, b + 1)
                act.activation(gn[:, 1], gn[:, 0], ACT.Sqrt).then_inc(deviation, 1)
                evac(aT[:], "aT")

        @block.tensor
        def _(pe):
            pe.wait_ge(weights_in, all_in)
            pe.wait_ge(fixed, 1)
            with pe.Fori(0, B) as b:
                def feature_major(u, wgt, rhs):
                    free(pe, b, u)
                    for c in range(CQ):
                        for k in range(KD):
                            op = pe.matmul(GP[gp.bank[u]][:, c, :], wgt[:, k, c * P:(c + 1) * P], rhs[:, k, :],
                                           start=(k == 0), stop=(k == KD - 1))
                    op.then_inc(gp_full[gp.bank[u]], 1)

                def token_major(u, act_T, wgt):
                    free(pe, b, u)
                    for t in range(TT):
                        for k in range(KD):
                            op = pe.matmul(GP[gp.bank[u]][:, t, :], act_T[:, k, t * P:(t + 1) * P], wgt[:, k, :],
                                           start=(k == 0), stop=(k == KD - 1))
                    op.then_inc(gp_full[gp.bank[u]], 1)

                def turn_pairs(u, i):
                    free(pe, b, u)
                    for c in range(CQ):
                        op = pe.matmul(GP[gp.bank[u]][:, c, :], turn[:], raw[:, i, c, :], start=True, stop=True)
                    op.then_inc(gp_full[gp.bank[u]], 1)

                pe.wait_ge(xn_ready, b + 1)
                free(pe, b, "xT")
                transpose_xn(pe, g, xn, GP[gp.bank["xT"]]).then_inc(gp_full[gp.bank["xT"]], 1)
                read(pe, b, "xT")
                feature_major("q0", wq, xnT)
                pe.wait_ge(kv_in, 16 * b + 16)
                feature_major("k0", wk, kvT)
                read(pe, b, "q0")
                turn_pairs("qr", 0)
                read(pe, b, "k0")
                turn_pairs("kr", 1)
                token_major("v0", kvT, wv)
                token_major("g0", xnT, wg)
                read(pe, b, "v0")
                pe.wait_ge(km_ready, b + 1)
                pe.wait_ge(turned, 2 * b + 2)

                def scores(u):
                    pe.wait_ge(sc_read[sc.bank[u]], sc.before(b, u))
                    for j in range(2):
                        h = 2 * u + j
                        for t in range(TT):
                            op = pe.matmul(SC[sc.bank[u]][:, j, t, t * P:S], kM[:, h, t * P:(t + 1) * P],
                                           qk[:, 0, h // HC, t * P:S], start=True, stop=True)
                    op.then_inc(sc_full[sc.bank[u]], 1)

                def weigh(c):
                    for u in (2 * c, 2 * c + 1):
                        pe.wait_ge(sc_read[sc.bank[u]], sc.after(b, u))
                    pe.wait_ge(ot_read[c % 2], ot.before(b, c))
                    for t in range(TT):
                        for j in range(HO):
                            op = pe.matmul(OT[c % 2][j * HP:(j + 1) * HP, 0, t * P:S], v[:, t, c * HO + j, :],
                                           sim[:, c % 2, j, t, t * P:S], start=(t == 0), stop=(t == TT - 1))
                    op.then_inc(ot_full[c % 2], 1)

                for u in range(SU):
                    scores(u)
                    if u % 2 == 0 and u:
                        weigh(u // 2 - 1)
                weigh(CO - 1)
                for i in range(2):
                    pe.wait_ge(ot_read[i], ot.after(b, CO - 2 + i))
                for t in range(TT):
                    u = f"T{t}"
                    free(pe, b, u)
                    flat = GP[gp.bank[u]][:].rearrange("p a n -> p (a n)")
                    for c in range(CO):
                        op = pe.transpose(flat[:, c * P:(c + 1) * P], oraw[:, c, t * P:(t + 1) * P], g.ident[:])
                    op.then_inc(gp_full[gp.bank[u]], 1)
                pe.wait_ge(ret_ready, b + 1)
                free(pe, b, "aT")
                transpose_xn(pe, g, ret, GP[gp.bank["aT"]]).then_inc(gp_full[gp.bank["aT"]], 1)
                read(pe, b, "aT")
                token_major("y", aT, wo)

        @block.vector
        def _(dve):
            rows = lambda a: a[:].rearrange("p (a n) -> p a n", a=1).broadcast_to([P, TT, D])
            heads = lambda a: a[:].rearrange("p t (h d) -> p (t h) d", d=hd)
            per_head = lambda a: a.rearrange("p t (h a) -> p (t h) a", a=1).broadcast_to([P, TT * H, hd])
            norm_factors(dve, g, sqrt_in, sqrt_out)
            dve.wait_ge(weights_in, all_in)
            dve.wait_ge(fixed, 1)
            with dve.Fori(0, B) as b:
                normalise(dve, g, b, xn, xn_ready)
                for i, u, src in ((0, "qr", "q0"), (1, "kr", "k0")):
                    read(dve, b, src)
                    dve.tensor_tensor(part[:, 0], raw[:, i], tables[:, 2 * i], ALU.mult)
                    full(dve, b, u)
                    dve.tensor_tensor(part[:, 1], GP[gp.bank[u]][:], tables[:, 2 * i + 1], ALU.mult)\
                       .then_inc(gp_read[gp.bank[u]], 1)
                    dve.drain()
                    dve.tensor_tensor(qk[:, i], part[:, 0], part[:, 1], ALU.add).then_inc(turned, 1)
                    dve.drain()
                full(dve, b, "v0")
                for t in range(TT):
                    op = dve.tensor_copy(v[:, t, :, 0:hd],
                                         GP[gp.bank["v0"]][:, t, :].rearrange("p (h d) -> p h d", d=hd))
                op.then_inc(gp_read[gp.bank["v0"]], 1)
                full(dve, b, "g0")
                dve.tensor_tensor(gz[:], GP[gp.bank["g0"]][:], rows(gb), ALU.add).then_inc(gp_read[gp.bank["g0"]], 1)
                dve.drain()
                dve.sem_inc(gate_z, 1)
                for u in range(SU):
                    c = u // 2
                    if u % 2 == 0:
                        dve.wait_ge(ot_full[c % 2], ot.before(b, c))
                    dve.wait_ge(sc_full[sc.bank[u]], sc.after(b, u))
                    dst = sim[:, c % 2, 2 * (u % 2):2 * (u % 2) + 2]
                    src = SC[sc.bank[u]]
                    for t in range(TT):
                        dve.tensor_tensor(dst[:, :, t, t * P:(t + 1) * P], src[:, :, t, t * P:(t + 1) * P],
                                          tri[:].rearrange("p (a n) -> p a n", a=1).broadcast_to([P, 2, P]), ALU.mult)
                    dve.tensor_copy(dst[:, :, 0, P:S], src[:, :, 0, P:S]).then_inc(sc_read[sc.bank[u]], 1)
                    dve.drain()
                for t in range(TT):
                    u = f"T{t}"
                    full(dve, b, u)
                    src = GP[gp.bank[u]][:].rearrange("p a n -> p (a n)").rearrange("p (h e) -> p h e", e=HP)[:, :, 0:hd]
                    dve.tensor_copy(ret[:, t, :].rearrange("p (h d) -> p h d", d=hd), src)\
                       .then_inc(gp_read[gp.bank[u]], 1)
                dve.drain()
                dve.tensor_reduce(gn[:, 0].rearrange("p t h -> p (t h)"), heads(ret), AX.X, ALU.add)
                dve.drain()
                dve.tensor_scalar(gn[:, 0], gn[:, 0], 1.0 / hd, None, ALU.mult)
                dve.drain()
                dve.tensor_tensor(heads(ret), heads(ret), per_head(gn[:, 0]), ALU.subtract)
                dve.drain()
                dve.tensor_tensor(sq[:], ret[:], ret[:], ALU.mult)
                dve.drain()
                dve.tensor_reduce(gn[:, 0].rearrange("p t h -> p (t h)"), heads(sq), AX.X, ALU.add)
                dve.drain()
                dve.tensor_scalar(gn[:, 0], gn[:, 0], 1.0 / hd, EPS, ALU.mult, ALU.add).then_inc(variance, 1)
                dve.wait_ge(deviation, b + 1)
                dve.reciprocal(gn[:, 2], gn[:, 1])
                dve.drain()
                root(dve, gn[:, 2], gn[:, 0], gn[:, 2], gn[:, 3])
                dve.tensor_tensor(heads(ret), heads(ret), per_head(gn[:, 2]), ALU.mult)
                dve.drain()
                dve.wait_ge(gate_ready, b + 1)
                dve.tensor_tensor(ret[:], ret[:], gate[:], ALU.mult).then_inc(ret_ready, 1)
                full(dve, b, "y")
                add_to_x(dve, g, b, GP[gp.bank["y"]][:]).then_inc(gp_read[gp.bank["y"]], 1)
                dve.drain()
                add_to_x(dve, g, b, rows(bo))
                dve.drain()
                next_stats(dve, g, b)
                dve.drain()


def top_rank(dve, rank, cmp, eq, s, earlier, t, n):
    other = s[:, t, 0:n].rearrange("p (a n) -> p a n", a=1).broadcast_to([P, n, n])
    own = s[:, t, 0:n].rearrange("p (n a) -> p n a", a=1).broadcast_to([P, n, n])
    dve.tensor_tensor(cmp, other, own, ALU.is_gt)
    dve.tensor_tensor(eq, other, own, ALU.is_equal)
    dve.drain()
    dve.tensor_tensor(eq, eq, earlier, ALU.mult)
    dve.drain()
    dve.tensor_tensor(cmp, cmp, eq, ALU.add)
    dve.drain()
    dve.tensor_reduce(rank[:, t, 0:n], cmp, AX.X, ALU.add)
    dve.drain()


def experts(nc, g, name, w, gated):
    io = g.io
    E = 16 if gated else 8
    SH = 2 if gated else 1
    HX = 2 if gated else 1
    gp = Banks(["xT", "logits", "cT"])
    n_h = E + SH
    hb = Banks(list(range(n_h)))
    cb = Banks(list(range(SH, n_h)))
    with ExitStack() as ctx:
        sb = lambda n, s, t=F32: ctx.enter_context(nc.sbuf_tensor(f"{name}_sb_{n}", s, t))
        sems, from_one = [], []

        def sem(n, one=False):
            s = ctx.enter_context(nc.semaphore(f"{name}_{n}"))
            (from_one if one else sems).append(s)
            return s
        w1 = sb("w1", [P, n_h, KD, P])
        w2 = sb("w2", [P, n_h, D])
        wr = sb("wr", [P, KD, E])
        sel = sb("sel", [P, H, P], BF16)
        earlier = sb("earlier", [P, H, H])
        if gated:
            w3 = sb("w3", [P, n_h, KD, P])
            b1, b3 = sb("b1", [P, n_h]), sb("b3", [P, n_h])
            br = sb("br", [P, E])
            b2 = sb("b2", [P, D])
            bs = sb("bs", [P, D])
            pairs = sb("pairs", [P, TT, 4, 6])
            gs = sb("gs", [P, TT, 4])
            grank = sb("grank", [P, TT, 4])
        xn = sb("xn", [P, TT, D])
        xnT = sb("xnT", [P, KD, S])
        lg = sb("lg", [P, TT, E])
        ex = sb("ex", [P, TT, E])
        red = sb("red", [P, 2, TT])
        score = sb("score", [P, TT, E])
        cmp, eq = sb("cmp", [P, E, E]), sb("eq", [P, E, E])
        rank = sb("rank", [P, TT, E])
        top = sb("top", [P, TT, 8])
        c = sb("c", [P, TT, E])
        cT = sb("cT", [P, S])
        cTb = sb("cTb", [P, S], BF16)
        rest = sb("rest", [E, S])
        act_out = sb("act_out", [P, 2, S])
        hT = sb("hT", [P, 2, S])
        hc = sb("hc", [P, 2, S])
        yt = sb("yt", [P, TT, D])
        GP = [ctx.enter_context(nc.psum_tensor(f"{name}_gp{i}", [P, 2, S], F32)) for i in range(2)]
        HB = [ctx.enter_context(nc.psum_tensor(f"{name}_hb{i}", [P, 2, S], F32)) for i in range(2)]
        CB = [ctx.enter_context(nc.psum_tensor(f"{name}_cb{i}", [P, 2, S], F32)) for i in range(2)]
        YB = [ctx.enter_context(nc.psum_tensor(f"{name}_yb{i}", [P, 2, S], F32)) for i in range(TT)]

        weights_in, sqrt_in, sqrt_out, fixed = sem("weights_in"), sem("sqrt_in"), sem("sqrt_out"), sem("fixed")
        xn_ready, logits_ready, exp_ready, c_ready = (sem("xn_ready"), sem("logits_ready"), sem("exp_ready"),
                                                      sem("c_ready"))
        gp_full = [sem(f"gp_full{i}", one=True) for i in range(2)]
        gp_read = [sem(f"gp_read{i}", one=True) for i in range(2)]
        hb_full = [sem(f"hb_full{i}", one=True) for i in range(2)]
        act_ready = [sem(f"act_ready{i}", one=True) for i in range(2)]
        hb_read = [sem(f"hb_read{i}", one=True) for i in range(2)]
        cb_full = [sem(f"cb_full{i}", one=True) for i in range(2)]
        h_ready = [sem(f"h_ready{i}", one=True) for i in range(2)]
        h_used = [sem(f"h_used{i}", one=True) for i in range(2)]
        y_full, y_read = sem("y_full"), sem("y_read", one=True)

        def full(eng, b, u):
            eng.wait_ge(gp_full[gp.bank[u]], gp.after(b, u))

        def free(eng, b, u):
            eng.wait_ge(gp_read[gp.bank[u]], gp.before(b, u))

        def read(eng, b, u):
            eng.wait_ge(gp_read[gp.bank[u]], gp.after(b, u))

        row = lambda a, n: a.rearrange("(a n) -> a n", a=1).broadcast_to([P, n])
        loads = [(w1[:], w["w1"]), (w2[:], w["w2"]), (wr[:], w["wr"].rearrange("(k p) n -> p k n", p=P)),
                 (sel[:], io["c_sel"]), (earlier[:], io["c_earlier"])]
        if gated:
            loads += [(w3[:], w["w3"]), (b1[:], w["b1"]), (b3[:], w["b3"]), (br[:], row(w["br"], E)),
                      (b2[:], w["b2"]), (bs[:], row(w["bs"], D))]
        all_in = 16 * len(loads)
        start_semaphores(nc, sems, from_one)
        block = ctx.enter_context(nc.Block())

        @block.sync
        def _(sp):
            for dst, src in loads:
                sp.dma_start(dst, src).then_inc(weights_in, 16)

        @block.gpsimd
        def _(pool):
            pool.memset(cT[:], 0.0).then_inc(fixed, 1)
            pool.memset(cTb[:], 0.0).then_inc(fixed, 1)

        @block.scalar
        def _(act):
            norm_sqrt(act, g, sqrt_in, sqrt_out)
            act.wait_ge(weights_in, all_in)
            with act.Fori(0, B) as b:
                full(act, b, "xT")
                act.activation(xnT[:], GP[gp.bank["xT"]][:], ACT.Copy).then_inc(gp_read[gp.bank["xT"]], 1)
                act.wait_ge(logits_ready, b + 1)
                act.activation(ex[:], lg[:], ACT.Exp).then_inc(exp_ready, 1)
                for e in range(n_h):
                    i = e % 2
                    act.wait_ge(hb_full[i], hb.after(b, e))
                    act.wait_ge(hb_read[i], hb.before(b, e))
                    if gated:
                        act.activation(act_out[:, i], HB[i][:, 0], ACT.Silu, bias=b1[:, e:e + 1]).then_inc(act_ready[i], 1)
                    else:
                        act.activation(act_out[:, i], HB[i][:, 0], ACT.Relu).then_inc(act_ready[i], 1)

        @block.tensor
        def _(pe):
            pe.wait_ge(weights_in, all_in)
            pe.wait_ge(fixed, 2)
            with pe.Fori(0, B) as b:
                pe.wait_ge(xn_ready, b + 1)
                free(pe, b, "xT")
                transpose_xn(pe, g, xn, GP[gp.bank["xT"]]).then_inc(gp_full[gp.bank["xT"]], 1)
                read(pe, b, "xT")
                free(pe, b, "logits")
                for t in range(TT):
                    for k in range(KD):
                        op = pe.matmul(GP[gp.bank["logits"]][:, t, 0:E], xnT[:, k, t * P:(t + 1) * P], wr[:, k, :],
                                       start=(k == 0), stop=(k == KD - 1))
                op.then_inc(gp_full[gp.bank["logits"]], 1)

                def hidden(e):
                    i = e % 2
                    pe.wait_ge(hb_read[i], hb.before(b, e))
                    for x, wgt in enumerate((w1, w3) if gated else (w1,)):
                        for k in range(KD):
                            op = pe.matmul(HB[i][:, x], wgt[:, e, k, :], xnT[:, k, :], start=(k == 0), stop=(k == KD - 1))
                    op.then_inc(hb_full[i], 1)

                def spread(e):
                    i = cb.bank[e]
                    if e - 2 >= SH:
                        pe.wait_ge(h_ready[e % 2], hb.after(b, e - 2))
                    pe.matmul(CB[i][:, 0], sel[:, e - SH, :], cTb[:], start=True, stop=True).then_inc(cb_full[i], 1)

                def out(e):
                    i = e % 2
                    pe.wait_ge(h_ready[i], hb.after(b, e))
                    for t in range(TT):
                        op = pe.matmul(YB[t][:, 0], hT[:, i, t * P:(t + 1) * P], w2[:, e, :], start=(e == 0),
                                       stop=(e == n_h - 1))
                    op.then_inc(h_used[i], 1)

                hidden(0)
                hidden(1)
                pe.wait_ge(c_ready, b + 1)
                free(pe, b, "cT")
                for t in range(TT):
                    op = pe.transpose(GP[gp.bank["cT"]][0:E, 0, t * P:(t + 1) * P], c[:, t, :], g.ident[:])
                op.then_inc(gp_full[gp.bank["cT"]], 1)
                read(pe, b, "cT")
                for e in range(SH, 2):
                    spread(e)
                pe.wait_ge(y_read, b + 1)
                for e in range(2, n_h):
                    spread(e)
                    hidden(e)
                    out(e - 2)
                out(n_h - 2)
                out(n_h - 1)
                if gated:
                    for t in range(TT):
                        op = pe.matmul(YB[t][:, 0], cT[:, t * P:(t + 1) * P], b2[:], start=False, stop=True,
                                       skip_group_check=True)
                    op.then_inc(y_full, 1)

        @block.vector
        def _(dve):
            norm_factors(dve, g, sqrt_in, sqrt_out)
            dve.wait_ge(weights_in, all_in)
            dve.wait_ge(fixed, 2)
            wide = lambda a, n: a.rearrange("p (t a) -> p t a", a=1).broadcast_to([P, TT, n])
            with dve.Fori(0, B) as b:
                normalise(dve, g, b, xn, xn_ready)
                full(dve, b, "logits")
                src = GP[gp.bank["logits"]][:, :, 0:E]
                if gated:
                    dve.tensor_reduce(red[:, 0], src, AX.X, ALU.max)
                    dve.drain()
                    dve.tensor_tensor(lg[:], src, wide(red[:, 0], E), ALU.subtract).then_inc(gp_read[gp.bank["logits"]], 1)
                    dve.drain()
                    dve.sem_inc(logits_ready, 1)
                    dve.wait_ge(exp_ready, b + 1)
                    dve.tensor_reduce(red[:, 0], ex[:], AX.X, ALU.add)
                    dve.drain()
                    dve.reciprocal(red[:, 1], red[:, 0])
                    dve.drain()
                    dve.tensor_tensor(ex[:], ex[:], wide(red[:, 1], E), ALU.mult)
                    dve.drain()
                    dve.tensor_tensor(score[:], ex[:], br[:].rearrange("p (a n) -> p a n", a=1)
                                      .broadcast_to([P, TT, E]), ALU.add)
                    dve.drain()
                    sg = score[:].rearrange("p t (g e) -> p t g e", e=4)
                    dve.tensor_tensor(pairs[:, :, :, 0:3], sg[:, :, :, 0:3], sg[:, :, :, 1:4], ALU.add)
                    dve.tensor_tensor(pairs[:, :, :, 3:5], sg[:, :, :, 0:2], sg[:, :, :, 2:4], ALU.add)
                    dve.tensor_tensor(pairs[:, :, :, 5:6], sg[:, :, :, 0:1], sg[:, :, :, 3:4], ALU.add)
                    dve.drain()
                    dve.tensor_reduce(gs[:], pairs[:], AX.X, ALU.max)
                    dve.drain()
                    for t in range(TT):
                        top_rank(dve, grank, cmp[:, 0:4, 0:4], eq[:, 0:4, 0:4], gs, earlier[:, 0:4, 0:4], t, 4)
                    dve.tensor_scalar(grank[:], grank[:], 1.5, None, ALU.is_lt)
                    dve.drain()
                    dve.tensor_scalar(gs[:], grank[:], 1e30, -1e30, ALU.mult, ALU.add)
                    for t in range(TT):
                        dve.tensor_tensor(score[:, t].rearrange("p (g e) -> p g e", e=4),
                                          score[:, t].rearrange("p (g e) -> p g e", e=4),
                                          grank[:, t].rearrange("p (g a) -> p g a", a=1).broadcast_to([P, 4, 4]), ALU.mult)
                    dve.drain()
                    for t in range(TT):
                        dve.tensor_tensor(score[:, t].rearrange("p (g e) -> p g e", e=4),
                                          score[:, t].rearrange("p (g e) -> p g e", e=4),
                                          gs[:, t].rearrange("p (g a) -> p g a", a=1).broadcast_to([P, 4, 4]), ALU.add)
                    dve.drain()
                    for t in range(TT):
                        top_rank(dve, rank, cmp[:], eq[:], score, earlier[:], t, E)
                    dve.tensor_scalar(rank[:], rank[:], 1.5, None, ALU.is_lt)
                    dve.drain()
                    dve.tensor_tensor(c[:], rank[:], ex[:], ALU.mult).then_inc(c_ready, 1)
                else:
                    dve.tensor_copy(score[:], src).then_inc(gp_read[gp.bank["logits"]], 1)
                    dve.drain()
                    for t in range(TT):
                        dve.max(top[:, t, :], score[:, t, :])
                    dve.drain()
                    dve.tensor_tensor(lg[:], top[:], top[:, :, 0:1].broadcast_to([P, TT, 8]), ALU.subtract)
                    dve.drain()
                    dve.sem_inc(logits_ready, 1)
                    dve.wait_ge(exp_ready, b + 1)
                    dve.tensor_scalar(red[:, 0], ex[:, :, 1], 1.0, None, ALU.add)
                    dve.drain()
                    dve.reciprocal(red[:, 1], red[:, 0])
                    dve.drain()
                    dve.tensor_scalar(red[:, 1], red[:, 1], 1.0, None, ALU.is_ge)
                    dve.tensor_tensor(c[:], score[:], top[:, :, 0:1].broadcast_to([P, TT, 8]), ALU.is_ge)
                    dve.drain()
                    dve.tensor_tensor(c[:], c[:], wide(red[:, 1], E), ALU.mult).then_inc(c_ready, 1)

                def hidden(e, routed):
                    i = e % 2
                    dve.wait_ge(act_ready[i], hb.after(b, e))
                    dve.wait_ge(h_used[i], hb.before(b, e))
                    dst = hc[:, i] if routed else hT[:, i]
                    if gated:
                        op = dve.scalar_tensor_tensor(out=dst, in0=HB[i][:, 1], scalar=b3[:, e:e + 1],
                                                      in1=act_out[:, i], op0=ALU.add, op1=ALU.mult)
                    else:
                        op = dve.scalar_tensor_tensor(out=dst, in0=HB[i][:, 0], scalar=0.0,
                                                      in1=act_out[:, i], op0=ALU.max, op1=ALU.mult)
                    op.then_inc(hb_read[i], 1)
                    if not routed:
                        dve.drain()
                        dve.sem_inc(h_ready[i], 1)
                        return
                    dve.drain()
                    dve.wait_ge(cb_full[cb.bank[e]], cb.after(b, e))
                    dve.tensor_tensor(hT[:, i], hc[:, i], CB[cb.bank[e]][:, 0], ALU.mult).then_inc(h_ready[i], 1)

                full(dve, b, "cT")
                src = GP[gp.bank["cT"]][0:E, 0, :]
                dve.tensor_copy(cT[0:E, :], src)
                dve.tensor_copy(cTb[0:E, :], src)
                dve.drain()
                dve.tensor_tensor(rest[:], src, cTb[0:E, :], ALU.subtract)
                dve.drain()
                dve.tensor_copy(cTb[32:32 + E, :], rest[:])
                dve.drain()
                dve.tensor_tensor(cTb[64:64 + E, :], rest[:], cTb[32:32 + E, :], ALU.subtract)\
                   .then_inc(gp_read[gp.bank["cT"]], 1)
                for e in range(n_h):
                    hidden(e, e >= SH)
                if gated:
                    dve.wait_ge(y_full, b + 1)
                else:
                    dve.wait_ge(h_used[(n_h - 1) % 2], hb.after(b, n_h - 1))
                for t in range(TT):
                    if gated:
                        op = dve.tensor_tensor(yt[:, t], YB[t][:, 0], bs[:], ALU.add)
                    else:
                        op = dve.tensor_copy(yt[:, t], YB[t][:, 0])
                op.then_inc(y_read, 1)
                dve.drain()
                add_to_x(dve, g, b, yt[:])
                dve.drain()
                next_stats(dve, g, b)
                dve.drain()


def sorted_experts(nc, g, name, w):
    io = g.io
    E, F = 8, 1024
    FC = F // P
    NS = 24
    U = 4
    WROW = KD * F + FC * D + FC
    with ExitStack() as ctx:
        sb = lambda n, s, t=F32: ctx.enter_context(nc.sbuf_tensor(f"{name}_sb_{n}", s, t))
        sems, from_one = [], []

        def sem(n, one=False):
            s = ctx.enter_context(nc.semaphore(f"{name}_{n}"))
            (from_one if one else sems).append(s)
            return s
        x_slots = nc.dram_tensor(f"{name}_x_slots", (NS * P, D), F32).ap()
        y_slots = nc.dram_tensor(f"{name}_y_slots", (NS * P, D), F32).ap()
        wr = sb("wr", [P, KD, E])
        br = sb("br", [P, E])
        before_p = sb("before_p", [P, P])
        ones = sb("ones", [P, P])
        earlier = sb("earlier", [P, H, H])
        steps = sb("steps", [P, NS])
        xn = sb("xn", [P, TT, D])
        xnT = sb("xnT", [P, KD, S])
        lg = sb("lg", [P, NT, E])
        sc = sb("sc", [P, NT, E])
        red = sb("red", [P, NT])
        cmp, eq = sb("cmp", [P, NT, E, E]), sb("eq", [P, NT, E, E])
        rank = sb("rank", [P, NT, E])
        win = sb("win", [P, NT, E])
        pre = sb("pre", [P, NT, E])
        tot = sb("tot", [P, NT, E])
        run = sb("run", [P, 2, NT, E])
        tiles = sb("tiles", [P, 3, E])
        cmp2 = sb("cmp2", [P, E, NT])
        cmp3 = sb("cmp3", [P, NS, E])
        cmp4 = sb("cmp4", [P, E, E])
        posf = sb("posf", [P, NT])
        pos = sb("pos", [P, NT], mybir.dt.int32)
        slotf = sb("slotf", [P, NS])
        slot = sb("slot", [P, NS], mybir.dt.int32)
        rw = sb("rw", [P, NT])
        rows = sb("rows", [P, NT, D])
        zero = sb("zero", [P, D])
        wb = sb("wb", [P, U, WROW])
        b2 = sb("b2", [P, U, D])
        xs = sb("xs", [P, U, D])
        xsT = sb("xsT", [P, U, KD, P])
        hT = sb("hT", [P, U, FC, P])
        ys = sb("ys", [P, U, D])
        GP = [ctx.enter_context(nc.psum_tensor(f"{name}_gp{i}", [P, 2, S], F32)) for i in range(2)]
        HB = [[ctx.enter_context(nc.psum_tensor(f"{name}_hb{j}{i}", [P, FC // 2, P], F32)) for i in range(2)]
              for j in range(2)]
        YB = [ctx.enter_context(nc.psum_tensor(f"{name}_yb{j}", [P, 2, S], F32)) for j in range(2)]

        weights_in, sqrt_in, sqrt_out = sem("weights_in"), sem("sqrt_in"), sem("sqrt_out")
        fixed, cleared = sem("fixed"), sem("cleared")
        xn_ready, xn_turned, xnT_ready = sem("xn_ready"), sem("xn_turned", one=True), sem("xnT_ready")
        logits_full, logits_read = sem("logits_full"), sem("logits_read", one=True)
        shifted, exp_ready = sem("shifted"), sem("exp_ready")
        win_ready, counted = sem("win_ready"), sem("counted")
        slots_known, rows_ready, scattered, gathered = (sem("slots_known"), sem("rows_ready"), sem("scattered"),
                                                        sem("gathered"))
        each = lambda n, one=False: [sem(f"{n}{j}", one) for j in range(U)]
        w_in, x_in, xT_ready, h_full, h_act, h_dve, y_full = (
            each(n) for n in ("w_in", "x_in", "xT_ready", "h_full", "h_act", "h_dve", "y_full"))
        turned, y_ready, y_stored = (each(n, one=True) for n in ("turned", "y_ready", "y_stored"))
        start_semaphores(nc, sems, from_one)
        block = ctx.enter_context(nc.Block())
        w1 = lambda j, k, c: wb[:, j, k * F + c * P:k * F + (c + 1) * P]
        w2 = lambda j, c: wb[:, j, KD * F + c * D:KD * F + (c + 1) * D]
        b1 = lambda j, c: wb[:, j, KD * F + FC * D + c:KD * F + FC * D + c + 1]

        @block.sync
        def _(sp):
            for dst, src in ((wr, w["wr"].rearrange("(k p) n -> p k n", p=P)),
                             (br, w["br"].rearrange("(a n) -> a n", a=1).broadcast_to([P, E])),
                             (before_p, io["c_before"]), (earlier, io["c_earlier"]), (steps, io["c_steps"])):
                sp.dma_start(dst[:], src).then_inc(weights_in, 16)
            sp.wait_ge(fixed, 2)
            for i in range(NS):
                sp.dma_start(x_slots[i * P:(i + 1) * P, :], zero[:]).then_inc(cleared, 16)
            sp.wait_ge(slots_known, 1)
            with sp.Fori(0, NS // U) as i:
                for j in range(U):
                    e = sp.value_load(slot[0:1, bass.ds(U * i + j, 1)], min_val=0, max_val=E - 1)
                    sp.wait_ge(y_ready[j], i + 1)
                    sp.dma_start(wb[:, j, :], w["w"][bass.ds(e, 1), :, :].rearrange("a p n -> p (a n)"))\
                      .then_inc(w_in[j], 16)
                    sp.dma_start(b2[:, j, :], w["b2"][bass.ds(e, 1), :].broadcast_to([P, D])).then_inc(w_in[j], 16)
                    sp.wait_ge(scattered, 16 * NT)
                    sp.wait_ge(turned[j], i + 1)
                    sp.dma_start(xs[:, j, :], x_slots[bass.ds((U * i + j) * P, P), :]).then_inc(x_in[j], 16)

        @block.gpsimd
        def _(pool):
            pool.memset(ones[:], 1.0).then_inc(fixed, 1)
            pool.memset(zero[:], 0.0).then_inc(fixed, 1)
            pool.wait_ge(cleared, 16 * NS)
            for t in range(NT):
                pool.wait_ge(rows_ready, t + 1)
                pool.indirect_dma_start(x_slots, bass.IndirectOffsetOnAxis(pos[:, t:t + 1], 0), rows[:, t, :], None)\
                    .then_inc(scattered, 16)
            for j in range(U):
                pool.wait_ge(y_stored[j], 16 * (NS // U) + 1)
            pool.wait_ge(scattered, 16 * NT)
            for t in range(NT):
                pool.indirect_dma_start(rows[:, t, :], None, y_slots, bass.IndirectOffsetOnAxis(pos[:, t:t + 1], 0))\
                    .then_inc(gathered, 16)

        @block.scalar
        def _(act):
            norm_sqrt(act, g, sqrt_in, sqrt_out)
            with act.Fori(0, B) as b:
                act.wait_ge(xn_turned, b + 2)
                act.activation(xnT[:], GP[0][:], ACT.Copy).then_inc(xnT_ready, 1)
            act.wait_ge(shifted, 1)
            act.activation(sc[:], lg[:], ACT.Exp).then_inc(exp_ready, 1)
            with act.Fori(0, NS // U) as i:
                for pair in ((0, 1), (2, 3)):
                    for j in pair:
                        act.wait_ge(turned[j], i + 2)
                        act.activation(xsT[:, j], GP[j % 2][:, :, 0:P], ACT.Copy).then_inc(xT_ready[j], 1)
                    for j in pair:
                        act.wait_ge(h_full[j], i + 1)
                        for c in range(FC // 2):
                            op = act.activation(hT[:, j, c, :], HB[j % 2][0][:, c, :], ACT.Relu, bias=b1(j, c))
                        op.then_inc(h_act[j], 1)
                    for j in pair:
                        act.wait_ge(y_ready[j], i + 2)
                        act.dma_start(y_slots[bass.ds((U * i + j) * P, P), :], ys[:, j, :]).then_inc(y_stored[j], 16)

        @block.tensor
        def _(pe):
            pe.wait_ge(weights_in, 16 * 5)
            with pe.Fori(0, B) as b:
                pe.wait_ge(xn_ready, b + 1)
                transpose_xn(pe, g, xn, GP[0]).then_inc(xn_turned, 1)
                pe.wait_ge(xnT_ready, b + 1)
                pe.wait_ge(logits_read, b + 1)
                for t in range(TT):
                    for k in range(KD):
                        op = pe.matmul(GP[1][:, t, 0:E], xnT[:, k, t * P:(t + 1) * P], wr[:, k, :],
                                       start=(k == 0), stop=(k == KD - 1))
                op.then_inc(logits_full, 1)
            pe.wait_ge(win_ready, 1)
            pe.wait_ge(fixed, 2)
            flat = win[:].rearrange("p t e -> p (t e)")
            pe.matmul(HB[0][0][:, 0, :], before_p[:], flat, start=True, stop=True)
            pe.matmul(HB[0][1][:, 0, :], ones[:], flat, start=True, stop=True).then_inc(counted, 1)
            with pe.Fori(0, NS // U) as i:
                for pair in ((0, 1), (2, 3)):
                    for j in pair:
                        pe.wait_ge(x_in[j], 16 * i + 16)
                        for k in range(KD):
                            op = pe.transpose(GP[j % 2][:, k, 0:P], xs[:, j, k * P:(k + 1) * P], g.ident[:])
                        op.then_inc(turned[j], 1)
                    for j in pair:
                        pe.wait_ge(xT_ready[j], i + 1)
                        pe.wait_ge(w_in[j], 32 * i + 32)
                        for c in range(FC):
                            for k in range(KD):
                                op = pe.matmul(HB[j % 2][c // (FC // 2)][:, c % (FC // 2), :], w1(j, k, c), xsT[:, j, k, :],
                                               start=(k == 0), stop=(k == KD - 1))
                        op.then_inc(h_full[j], 1)
                    for j in pair:
                        pe.wait_ge(h_act[j], i + 1)
                        pe.wait_ge(h_dve[j], i + 1)
                        pe.wait_ge(y_ready[(j + 2) % U], i + 1 + j // 2)
                        for c in range(FC):
                            op = pe.matmul(YB[j % 2][:, 0], hT[:, j, c, :], w2(j, c), start=(c == 0), stop=(c == FC - 1))
                        op.then_inc(y_full[j], 1)

        @block.vector
        def _(dve):
            wide = lambda a: a[:].rearrange("p (t a) -> p t a", a=1).broadcast_to([P, NT, E])
            norm_factors(dve, g, sqrt_in, sqrt_out)
            dve.wait_ge(weights_in, 16 * 5)
            with dve.Fori(0, B) as b:
                dve.wait_ge(xn_turned, b + 1)
                normalise(dve, g, b, xn, xn_ready)
                dve.wait_ge(logits_full, b + 1)
                dve.tensor_tensor(lg[:, bass.ds(b * TT, TT), :], GP[1][:, :, 0:E],
                                  br[:].rearrange("p (a n) -> p a n", a=1).broadcast_to([P, TT, E]), ALU.add)\
                   .then_inc(logits_read, 1)
            dve.drain()
            dve.tensor_reduce(red[:], lg[:], AX.X, ALU.max)
            dve.drain()
            dve.tensor_tensor(lg[:], lg[:], wide(red), ALU.subtract).then_inc(shifted, 1)
            dve.wait_ge(exp_ready, 1)
            dve.tensor_reduce(red[:], sc[:], AX.X, ALU.add)
            dve.drain()
            dve.reciprocal(red[:], red[:])
            dve.drain()
            dve.tensor_tensor(sc[:], sc[:], wide(red), ALU.mult)
            dve.drain()
            for t in range(NT):
                other = sc[:, t, :].rearrange("p (a n) -> p a n", a=1).broadcast_to([P, E, E])
                own = sc[:, t, :].rearrange("p (n a) -> p n a", a=1).broadcast_to([P, E, E])
                dve.tensor_tensor(cmp[:, t], other, own, ALU.is_gt)
                dve.tensor_tensor(eq[:, t], other, own, ALU.is_equal)
            dve.drain()
            early = earlier[:, 0:E, 0:E].rearrange("p (a i) j -> p a i j", a=1).broadcast_to([P, NT, E, E])
            dve.tensor_tensor(eq[:], eq[:], early, ALU.mult)
            dve.drain()
            dve.tensor_tensor(cmp[:], cmp[:], eq[:], ALU.add)
            dve.drain()
            dve.tensor_reduce(rank[:], cmp[:], AX.X, ALU.add)
            dve.drain()
            dve.tensor_scalar(rank[:], rank[:], 1.5, None, ALU.is_lt)
            dve.tensor_scalar(win[:], sc[:], 0.0, None, ALU.is_gt)
            dve.drain()
            dve.tensor_tensor(rank[:], rank[:], win[:], ALU.mult)
            dve.drain()
            for t in range(NT):
                dve.tensor_tensor(cmp[:, t], rank[:, t, :].rearrange("p (n a) -> p n a", a=1).broadcast_to([P, E, E]),
                                  earlier[:, 0:E, 0:E], ALU.mult)
            dve.drain()
            dve.tensor_reduce(win[:], cmp[:].rearrange("p t j i -> p t i j"), AX.X, ALU.add)
            dve.drain()
            dve.tensor_scalar(win[:], win[:], 0.5, None, ALU.is_lt)
            dve.drain()
            dve.tensor_tensor(win[:], win[:], rank[:], ALU.mult).then_inc(win_ready, 1)
            dve.drain()
            dve.tensor_tensor(sc[:], sc[:], win[:], ALU.mult)
            dve.drain()
            dve.tensor_reduce(rw[:], sc[:], AX.X, ALU.add)
            dve.drain()
            dve.tensor_tensor(rw[:], rw[:], g.rstd[:], ALU.mult)
            dve.wait_ge(counted, 1)
            dve.tensor_copy(pre[:], HB[0][0][:, 0, :].rearrange("p (t e) -> p t e", e=E))
            dve.tensor_copy(tot[:], HB[0][1][:, 0, :].rearrange("p (t e) -> p t e", e=E))
            dve.tensor_copy(run[:, 0], HB[0][1][:, 0, :].rearrange("p (t e) -> p t e", e=E))
            dve.drain()
            a, d = 0, 1
            while d < NT:
                dve.tensor_copy(run[:, 1 - a, 0:d], run[:, a, 0:d])
                dve.tensor_tensor(run[:, 1 - a, d:NT], run[:, a, d:NT], run[:, a, 0:NT - d], ALU.add)
                dve.drain()
                a, d = 1 - a, 2 * d
            dve.tensor_tensor(pre[:], pre[:], tot[:], ALU.subtract)
            for e in range(E):
                dve.tensor_scalar(cmp2[:, e, :], steps[:, 0:NT], run[:, a, NT - 1, e:e + 1], None, ALU.is_lt)
            dve.drain()
            dve.tensor_tensor(pre[:], pre[:], run[:, a], ALU.add)
            dve.tensor_reduce(tiles[:, 0], cmp2[:], AX.X, ALU.add)
            dve.drain()
            dve.tensor_tensor(cmp4[:], tiles[:, 0:1, :].broadcast_to([P, E, E]), earlier[:, 0:E, 0:E], ALU.mult)
            dve.drain()
            dve.tensor_reduce(tiles[:, 1], cmp4[:], AX.X, ALU.add)
            dve.drain()
            dve.tensor_tensor(tiles[:, 0], tiles[:, 0], tiles[:, 1], ALU.add)
            dve.tensor_scalar(tiles[:, 2], tiles[:, 1], float(P), None, ALU.mult)
            dve.drain()
            dve.tensor_tensor(pre[:], pre[:], tiles[:, 2:3, :].broadcast_to([P, NT, E]), ALU.add)
            for sl in range(NS):
                dve.tensor_scalar(cmp3[:, sl, :], tiles[:, 0, :], float(sl), None, ALU.is_le)
            dve.drain()
            dve.tensor_tensor(pre[:], pre[:], win[:], ALU.mult)
            dve.tensor_reduce(slotf[:], cmp3[:], AX.X, ALU.add)
            dve.drain()
            dve.tensor_reduce(posf[:], pre[:], AX.X, ALU.add)
            dve.tensor_scalar(slotf[:], slotf[:], float(E - 1), None, ALU.min)
            dve.drain()
            dve.tensor_copy(pos[:], posf[:])
            dve.tensor_copy(slot[:], slotf[:]).then_inc(slots_known, 1)
            dve.drain()
            for t in range(NT):
                dve.tensor_scalar(rows[:, t, :], g.x[:, t, :], g.mean[:, t:t + 1], rw[:, t:t + 1],
                                  ALU.subtract, ALU.mult).then_inc(rows_ready, 1)
            with dve.Fori(0, NS // U) as i:
                for pair in ((0, 1), (2, 3)):
                    for j in pair:
                        dve.wait_ge(h_full[j], i + 1)
                        for c in range(FC // 2):
                            op = dve.tensor_scalar(hT[:, j, FC // 2 + c, :], HB[j % 2][1][:, c, :], b1(j, FC // 2 + c), 0.0,
                                                   ALU.add, ALU.max)
                        op.then_inc(h_dve[j], 1)
                    for j in pair:
                        dve.wait_ge(y_full[j], i + 1)
                        dve.wait_ge(y_stored[j], 16 * i + 1)
                        dve.tensor_tensor(ys[:, j, :], YB[j % 2][:, 0], b2[:, j, :], ALU.add).then_inc(y_ready[j], 1)
            dve.wait_ge(gathered, 16 * NT)
            dve.tensor_tensor(g.x[:], g.x[:], rows[:], ALU.add)
            dve.drain()
            for t in range(NT):
                dve.bn_stats(g.stats[:, t, :], g.x[:, t, :])
            dve.drain()


def store_x(nc, g):
    with ExitStack() as ctx:
        stored = ctx.enter_context(nc.semaphore("x_stored"))
        start_semaphores(nc, [stored], [])
        block = ctx.enter_context(nc.Block())

        @block.sync
        def _(sp):
            sp.dma_start(g.io["out"].rearrange("b (t p) d -> p (b t) d", p=P), g.x[:]).then_inc(stored, 16)
            sp.wait_ge(stored, 16)


def constants():
    bf = lambda a: (np.ascontiguousarray(a, np.float32).view(np.uint32) >> 16).astype(np.uint16)
    c = {"c_ident": np.eye(P, dtype=np.float32), "c_eye": bf(np.eye(P))}
    for hd in (16, 64):
        m = np.zeros((P, P // hd), np.float32)
        for h in range(P // hd):
            m[h * hd:(h + 1) * hd, h] = 1
        c[f"c_mask{hd}"] = m
    sel = np.zeros((P, H, P), np.float32)
    for part in range(3):
        for h in range(H):
            sel[32 * part + h, h, :] = 1
    c["c_sel"] = bf(sel)
    c["c_earlier"] = np.broadcast_to(np.tril(np.ones((H, H), np.float32), -1), (P, H, H)).copy()
    c["c_before"] = np.triu(np.ones((P, P), np.float32), 1)
    c["c_steps"] = np.broadcast_to(np.arange(24, dtype=np.float32) * P, (P, 24)).copy()
    turn = np.zeros((P, P), np.float32)
    for i in range(0, P, 2):
        turn[i + 1, i], turn[i, i + 1] = -1, 1
    c["c_turn"] = turn
    c["c_tri"] = np.triu(np.ones((P, P), np.float32))
    hd = 16
    half = hd // 2
    base = (np.arange(0, hd, 2) + 0.4 * hd) / (1.4 * hd)
    power = (np.arange(-(S // 2), -(S // 2) + S) / 512.0)[:, None]
    length = base[None, :] ** power
    angle = np.arange(S)[:, None] / 10000.0 ** (np.arange(half) / half)[None, :]
    gammas = 1.0 - np.exp(np.linspace(np.log(1 / 32), np.log(1 / 512), H))
    tables = np.zeros((4, H, hd, S))
    for i, (f, sign) in enumerate(((np.cos, 1), (np.sin, 1), (np.cos, -1), (np.sin, -1))):
        t = np.repeat(f(angle) * length ** sign, 2, axis=-1).T
        tables[i] = t[None] * gammas[:, None, None] ** (sign * np.arange(S))[None, None, :]
    c["c_tables"] = tables.reshape(4, 2, P, S).transpose(2, 0, 1, 3).astype(np.float32)
    q, k = np.arange(P)[:, None], np.arange(P)[None, :]
    c["c_neg_qk"] = bf(np.where(k > q, -8e9, 0.0))
    c["c_neg_kq"] = np.ascontiguousarray(c["c_neg_qk"].T)
    return c


def pad_heads(w, hp):
    out = np.zeros((H, hp) + w.shape[1:], w.dtype)
    out[:, :w.shape[0] // H] = w.reshape((H, w.shape[0] // H) + w.shape[1:])
    return out.reshape((H * hp,) + w.shape[1:])


def layouts(i):
    T = lambda a: np.ascontiguousarray(np.asarray(a).T)
    a = {"x": i["x"], "ctxT": np.ascontiguousarray(np.asarray(i["ctx_1024"]).transpose(0, 2, 1))}
    wkv = np.asarray(i["L0_xattn_w_kv"])
    a["a0_wq"] = i["L0_xattn_w_q"]
    a["a0_wk"] = np.tile(wkv[:, :16], (1, 8))
    a["a0_wv"] = wkv[:, 16:]
    a["a0_wo"] = pad_heads(np.asarray(i["L0_xattn_w_concat"]), 32)
    E, I = 16, 128
    first = lambda w, ws: np.concatenate(
        [np.asarray(ws).reshape(KD, P, -1, P).transpose(1, 2, 0, 3),
         np.asarray(w).reshape(-1, KD, P, P).transpose(2, 0, 1, 3)], 1)
    second = lambda w, ws: np.concatenate(
        [np.asarray(ws).reshape(-1, P, D).transpose(1, 0, 2), np.asarray(w).transpose(1, 0, 2)], 1)
    a["f0_w1"] = first(i["L0_ffn_We1"], i["L0_ffn_ws1"])
    a["f0_w3"] = first(i["L0_ffn_We3"], i["L0_ffn_ws3"])
    a["f0_w2"] = second(i["L0_ffn_We2"], i["L0_ffn_ws2"])
    for n in "13":
        a[f"f0_b{n}"] = np.concatenate([T(np.asarray(i[f"L0_ffn_bs{n}"]).reshape(-1, P)), T(i[f"L0_ffn_be{n}"])], 1)
    a["f0_b2"] = np.concatenate([np.asarray(i["L0_ffn_be2"]), np.zeros((P - E, D), np.float32)])
    a["f0_bs"] = i["L0_ffn_bs2"]
    a["f0_wr"], a["f0_br"] = T(i["L0_ffn_gate_w"]), i["L0_ffn_gate_b"]
    per_partition = lambda n: np.asarray(i[f"L1_ffn_{n}"]).reshape(8, -1, P, i[f"L1_ffn_{n}"].shape[-1])\
        .transpose(0, 2, 1, 3).reshape(8, P, -1)
    a["f1_w"] = np.concatenate([per_partition("w1"), per_partition("w2"),
                                np.asarray(i["L1_ffn_b1"]).reshape(8, -1, P).transpose(0, 2, 1)], 2)
    a["f1_b2"], a["f1_wr"], a["f1_br"] = i["L1_ffn_b2"], i["L1_ffn_gate_w"], i["L1_ffn_gate_b"]
    a["f3_w1"] = first(i["L3_ffn_W1"], i["L3_ffn_Ws1"])
    a["f3_w2"] = second(i["L3_ffn_W2"], i["L3_ffn_Ws2"])
    a["f3_wr"] = i["L3_ffn_Wr"]
    for n in "QKV":
        a[f"a1_w{n.lower()}"] = np.asarray(i[f"L1_xattn_W_{n}"]).transpose(1, 0, 2).reshape(D, D)
    a["a1_wg"], a["a1_wo"] = T(i["L1_xattn_g_w"]), T(i["L1_xattn_out_w"])
    a["a1_gb"], a["a1_bo"] = i["L1_xattn_g_b"], i["L1_xattn_out_b"]
    a["a2_wq"], a["a2_wk"], a["a2_wv"] = (T(i[f"L2_xattn_w{n}"]) for n in "qkv")
    a["a2_wo"] = pad_heads(T(i["L2_xattn_wo"]), 32)
    for n in ("bq", "bk"):
        a[f"a2_{n}"] = T(np.asarray(i[f"L2_xattn_{n}"]).reshape(-1, P))
    for n in ("bv", "bo"):
        a[f"a2_{n}"] = i[f"L2_xattn_{n}"]
    for n in "qkv":
        a[f"f2_w{n}"] = T(i[f"L2_ffn_W{n}"])
    a["f2_wo"] = pad_heads(T(i["L2_ffn_Wp"]), 32)
    a["f2_bq"], a["f2_bv"], a["f2_bo"] = (i[f"L2_ffn_b{n}"] for n in "qvp")
    a["f2_bk"] = T(np.asarray(i["L2_ffn_bk"]).reshape(-1, P))
    a["f2_wr"] = pad_heads(np.concatenate([T(i["L2_ffn_Wr"]), T(i["L2_ffn_Ws"])], 1), 32)
    a["f2_br"] = np.concatenate([np.asarray(i["L2_ffn_br"]), np.asarray(i["L2_ffn_bs"])])
    a["f2_qe"] = np.asarray(i["L2_ffn_query_embedding"]).reshape(-1)
    a["f2_temp"] = np.asarray(i["L2_ffn_temperature"]).reshape(-1)
    for n in "qkv":
        w = np.asarray(i[f"L3_xattn_W{n}"])
        a[f"a3_w{n}"] = w.transpose(1, 0, 2).reshape(D, -1)
    a["a3_wo"] = i["L3_xattn_Wo"]
    a.update(constants())
    return {k: np.ascontiguousarray(v) for k, v in a.items()}


def sub(a, pre):
    return {n[len(pre):]: v for n, v in a.items() if n.startswith(pre)}


STAGES = ["a0", "f0", "a1", "f1", "a2", "f2", "a3", "f3"]


def program(nc, io, stages):
    for n in ("c_eye", "c_sel", "c_neg_qk", "c_neg_kq"):
        io[n] = io[n].bitcast(BF16)
    with ExitStack() as ctx:
        g = Common(nc, ctx, io)
        load_x(nc, g)
        for s in stages:
            w = sub(io, s + "_")
            if s == "a0":
                attention(nc, g, s, 16, w, shared_kv=True)
            elif s == "f0":
                experts(nc, g, s, w, True)
            elif s == "f3":
                experts(nc, g, s, w, False)
            elif s == "f1":
                sorted_experts(nc, g, s, w)
            elif s == "a1":
                retention(nc, g, s, w)
            elif s == "a2":
                attention(nc, g, s, 16, w, bias=True)
            elif s == "a3":
                attention(nc, g, s, 64, w, causal=True, interleave=True)
            elif s == "f2":
                attention(nc, g, s, 16, w, bias=True, kv_from_x=True, router=True)
        store_x(nc, g)


def kernel(**inputs):
    import concourse.bacc as bacc
    from concourse.bass_utils import run_bass_kernel_spmd

    nc = bacc.Bacc("TRN2", target_bir_lowering=False, num_devices=1)
    arrays = layouts(inputs)
    io = {n: nc.dram_tensor(n, a.shape, mybir.dt.from_np(a.dtype), kind="ExternalInput").ap()
          for n, a in arrays.items()}
    io["out"] = nc.dram_tensor("out", (B, S, D), F32, kind="ExternalOutput").ap()
    program(nc, io, STAGES)
    result = run_bass_kernel_spmd(nc, [arrays], core_ids=[0])
    return result.results[0]["out"]
```

```python
from contextlib import ExitStack

import numpy as np
import concourse.bass as bass
from concourse import mybir

F32 = mybir.dt.float32
BF16 = mybir.dt.bfloat16
ROUNDED = mybir.dt.float32r
ALU = mybir.AluOpType
ACT = mybir.ActivationFunctionType
AX = mybir.AxisListType

P = 128
B, S, D = 8, 256, 256
TT = S // P
KD = D // P
NT = B * TT
H = 16
EPS = 1e-5


class Banks:

    def __init__(self, uses, n=2):
        self.bank = {u: i % n for i, u in enumerate(uses)}
        self.nth = {u: i // n for i, u in enumerate(uses)}
        self.per = [sum(1 for u in uses if self.bank[u] == k) for k in range(n)]

    def before(self, b, u):
        return b * self.per[self.bank[u]] + self.nth[u] + 1

    def after(self, b, u):
        return self.before(b, u) + 1


DEPTH = 2


class Step:

    def __init__(self, s=None, i=None, j=0):
        self.s, self.i, self.j = s, i, j

    def has(self, part):
        return self.i is not None or 0 <= self.s - part < B

    def seq(self, part):
        return self.s - part if self.i is None else self.i * 2 + (DEPTH + self.j - part)

    def half(self, part):
        return (self.s - part if self.i is None else DEPTH + self.j - part) % 2


def run_steps(eng, body):
    for s in range(DEPTH):
        body(Step(s))
    with eng.Fori(0, (B - DEPTH) // 2) as i:
        for j in range(2):
            body(Step(i=i, j=j))
    for s in range(B, B + DEPTH):
        body(Step(s))


class StepBanks:

    def __init__(self, uses, n=2):
        self.uses = uses
        self.bank = {u: i % n for i, (u, _) in enumerate(uses)}

    def in_step(self, st, k, until=None):
        n = 0
        for u, part in self.uses:
            if u == until:
                break
            n += self.bank[u] == k and st.has(part)
        return n

    def before(self, st, u):
        k = self.bank[u]
        count = self.in_step(st, k, u) + 1
        if st.i is None:
            return count + sum(self.in_step(Step(s), k) for s in range(st.s))
        per = self.in_step(Step(DEPTH), k)
        count += sum(self.in_step(Step(s), k) for s in range(DEPTH)) + st.j * per
        return st.i * (2 * per) + count

    def after(self, st, u):
        return self.before(st, u) + 1

    def at_start(self, st, u):
        return self.before(st, next(v for v, _ in self.uses if self.bank[v] == self.bank[u]))

    def per(self, u):
        return self.in_step(Step(DEPTH), self.bank[u])


class Common:

    def __init__(self, nc, ctx, io):
        self.nc, self.io = nc, io
        sb = lambda n, s, t=F32: ctx.enter_context(nc.sbuf_tensor(f"g_{n}", s, t))
        self.x = sb("x_all", [P, NT, D])
        self.stats = sb("ln_stats", [P, NT, 6])
        self.mean = sb("ln_mean", [P, NT])
        self.rstd = sb("ln_rstd", [P, NT])
        self.tmp = sb("ln_tmp", [P, 4, NT])
        self.ident = sb("ident", [P, P])
        self.moved = [[ctx.enter_context(nc.semaphore(f"g_{n}{layer}")) for n in
                       ("scattered", "gathered_first", "gathered_second")] for layer in range(2)]


def start_semaphores(nc, sems, from_one):
    numbers = sorted(x.num for x in sems + from_one)
    with nc.Block() as block:
        @block.sync
        def _(sp):
            start = numbers[0]
            for n, after in zip(numbers, numbers[1:] + [None]):
                if after != n + 1:
                    sp.sem_clear(range(start, n + 1))
                    start = after
            for x in from_one:
                sp.sem_inc(x, 1)


def load_x(nc, g):
    with ExitStack() as ctx:
        loaded = ctx.enter_context(nc.semaphore("x_loaded"))
        block = ctx.enter_context(nc.Block())

        @block.sync
        def _(sp):
            sp.dma_start(g.ident[:], g.io["c_ident"]).then_inc(loaded, 16)
            sp.dma_start(g.x[:], g.io["x"].rearrange("b (t p) d -> p (b t) d", p=P)).then_inc(loaded, 16)

        @block.vector
        def _(dve):
            dve.wait_ge(loaded, 32)
            for t in range(NT):
                dve.bn_stats(g.stats[:, t, :], g.x[:, t, :])


def norm_factors(dve, g, sqrt_in, sqrt_out):
    st, tmp = g.stats, g.tmp
    dve.tensor_tensor(g.mean[:], st[:, :, 1], st[:, :, 4], ALU.add)
    dve.tensor_tensor(tmp[:, 0, :], st[:, :, 1], st[:, :, 4], ALU.subtract)
    dve.tensor_tensor(tmp[:, 1, :], st[:, :, 2], st[:, :, 5], ALU.add)
    dve.drain()
    dve.tensor_scalar(g.mean[:], g.mean[:], 0.5, None, ALU.mult)
    dve.tensor_tensor(tmp[:, 0, :], tmp[:, 0, :], tmp[:, 0, :], ALU.mult)
    dve.tensor_scalar(tmp[:, 1, :], tmp[:, 1, :], 1.0 / D, EPS, ALU.mult, ALU.add)
    dve.drain()
    dve.scalar_tensor_tensor(out=tmp[:, 1, :], in0=tmp[:, 0, :], scalar=0.25, in1=tmp[:, 1, :],
                             op0=ALU.mult, op1=ALU.add).then_inc(sqrt_in, 1)
    dve.wait_ge(sqrt_out, 1)
    dve.reciprocal(g.rstd[:], tmp[:, 2, :])
    dve.drain()
    dve.tensor_tensor(tmp[:, 0, :], g.rstd[:], g.rstd[:], ALU.mult)
    dve.drain()
    dve.tensor_tensor(tmp[:, 0, :], tmp[:, 0, :], tmp[:, 1, :], ALU.mult)
    dve.drain()
    dve.tensor_scalar(tmp[:, 0, :], tmp[:, 0, :], -0.5, 1.5, ALU.mult, ALU.add)
    dve.drain()
    dve.tensor_tensor(g.rstd[:], g.rstd[:], tmp[:, 0, :], ALU.mult)
    dve.drain()


def norm_sqrt(act, g, sqrt_in, sqrt_out):
    act.wait_ge(sqrt_in, 1)
    act.activation(g.tmp[:, 2, :], g.tmp[:, 1, :], ACT.Sqrt).then_inc(sqrt_out, 1)


def normalise(dve, g, b, xn, ready):
    for t in range(TT):
        i = b * TT + t
        op = dve.tensor_scalar(xn[:, t, :], g.x[:, bass.ds(i, 1), :].rearrange("p a d -> p (a d)"),
                               g.mean[:, bass.ds(i, 1)], g.rstd[:, bass.ds(i, 1)], ALU.subtract, ALU.mult)
    if ready is not None:
        op.then_inc(ready, 1)


def add_to_x(dve, g, b, y):
    xb = g.x[:, bass.ds(b * TT, TT), :]
    op = dve.tensor_tensor(xb, xb, y, ALU.add)
    return op


def next_stats(dve, g, b):
    for t in range(TT):
        i = b * TT + t
        dve.bn_stats(g.stats[:, bass.ds(i, 1), :].rearrange("p a d -> p (a d)"),
                     g.x[:, bass.ds(i, 1), :].rearrange("p a d -> p (a d)"))


def transpose_xn(pe, g, xn, out):
    for k in range(KD):
        for t in range(TT):
            op = pe.transpose(out[:, k, t * P:(t + 1) * P], xn[:, t, k * P:(k + 1) * P], g.ident[:])
    return op


PART = {"norm": 0, "xT": 0, "q": 0, "k": 0, "v": 0, "qT": 0, "max": 1, "neg": 1, "score": 1, "weigh": 1,
        "gate": 2, "y": 2}


def plan(NQ, NKB, NV, SU, HO, CO, router):
    maxima = [("max", u) for u in range(SU)]
    order = [maxima[0], ("norm", 0), maxima[1]] + ([("gate", 0)] if router else []) + [("y", 0), ("xT", 0)]
    between = [("q", i) for i in range(NQ)] + [("k", i) for i in range(NKB)] + [("v", i) for i in range(NV)]
    late = max(1, NV // 2)
    between, late = between[:-late], between[-late:]
    rest = maxima[2:]
    for n, m in enumerate(rest):
        order += between[len(between) * n // len(rest):len(between) * (n + 1) // len(rest)] + [m]
    order += [("neg", 0)] + late
    done = 0
    for u in range(SU):
        order.append(("score", u))
        while done < 2 * u // HO:
            order.append(("weigh", done))
            done += 1
    return order + ([("qT", 0)] if router else []) + [("weigh", c) for c in range(done, CO)]


def attention(nc, g, name, hd, w, kv_from_x=False, shared_kv=False, causal=False, bias=False, router=False,
              interleave=False):
    io = g.io
    CQ = H * hd // P
    CK = 1 if shared_kv else CQ
    HC = P // hd
    HP = 32 if hd == 16 else 64
    HO = P // HP
    CO = H // HO
    KH = HC if shared_kv else H
    VH = 1 if shared_kv else H
    scale = float(hd) ** -0.5
    NQ = max(1, CQ // 2)
    NKB = max(1, CK // 2)
    NV = 1 if shared_kv else max(1, H * hd // D)
    SU = H // 2
    order = plan(NQ, NKB, NV, SU, HO, CO, router)
    gp = StepBanks([(f"{what}{i}" if what in "qkv" else what, PART[what]) for what, i in order
                    if what not in ("norm", "max", "score", "weigh")])
    sc = Banks([("max", u) for u in range(SU)] + [("exp", u) for u in range(SU)])
    ot = Banks(list(range(CO)))

    with ExitStack() as ctx:
        sb = lambda n, s, t=F32: ctx.enter_context(nc.sbuf_tensor(f"{name}_sb_{n}", s, t))
        sems, from_one = [], []

        def sem(n, one=False):
            s = ctx.enter_context(nc.semaphore(f"{name}_{n}"))
            (from_one if one else sems).append(s)
            return s
        wq = sb("wq", [P, KD, H * hd])
        wk = sb("wk", [P, KD, CK * P])
        wv = sb("wv", [P, KD, VH * hd])
        wo = sb("wo", [P, CO, D])
        mask = sb("mask", [P, HC])
        sel = sb("sel", [P, H, P], BF16)
        xn = sb("xn", [P, TT, D])
        xnT = sb("xnT", [P, KD, S])
        kvT = xnT if kv_from_x else sb("kvT", [P, KD, S])
        qT2 = sb("qT", [P, 2, CQ, S])
        kT = sb("kT", [P, CK, S])
        kM2 = sb("kM", [P, 2, KH, S])
        qR2 = sb("q_rounded", [P, 2, CQ, S], ROUNDED)
        kR2 = sb("k_rounded", [P, 2, KH, S], ROUNDED)
        v2 = sb("v", [P, 2, TT, VH, HP])
        ones = sb("ones", [P, HP])
        mx = sb("mx", [P, TT, H])
        negT = sb("negT", [P, S], BF16)
        rest = sb("rest", [H, S])
        probs = sb("probs", [P, 2, HO, TT, S])
        rden = sb("rden", [P, 2, S])
        oT = sb("oT", [P, CO, S])
        if causal:
            eye = sb("eye", [P, P], BF16)
            neg_qk = sb("neg_qk", [P, P], BF16)
            neg_kq = sb("neg_kq", [P, P], BF16)
        if bias:
            bq = sb("bq", [P, CQ])
            bk = sb("bk", [P, CK])
            bv = sb("bv", [P, D])
            bo = sb("bo", [P, D])
        if router:
            bqt = sb("bqt", [P, D])
            qe = sb("qe", [P, D])
            sp_t = sb("sp_t", [P, 4, H])
            spq = sb("spq", [P, H])
            qtm = sb("qtm", [P, TT, D])
            qsq = sb("qsq", [P, TT, D])
            qn = sb("qn", [P, 3, TT, H])
            wr = sb("wr", [P, CO, H + 1])
            br = sb("br", [P, H + 1])
            lg = sb("lg", [P, TT, 24])
            le = sb("le", [P, TT, 24])
            top = sb("top", [P, TT, 8])
            sm = sb("sm", [P, TT, 8])
            yt = sb("yt", [P, TT, D])
        GP = [ctx.enter_context(nc.psum_tensor(f"{name}_gp{i}", [P, 2, S], F32)) for i in range(2)]
        SC = [ctx.enter_context(nc.psum_tensor(f"{name}_sc{i}", [P, 2, 2, S], F32)) for i in range(2)]
        OT = [ctx.enter_context(nc.psum_tensor(f"{name}_ot{i}", [P, 2, S], F32)) for i in range(2)]

        weights_in = sem("weights_in")
        kv_in = sem("kv_in")
        sqrt_in, sqrt_out = sem("sqrt_in"), sem("sqrt_out")
        fixed = sem("fixed")
        xn_ready = sem("xn_ready")
        q_sums = sem("q_sums")
        q_roots = sem("q_roots")
        q_scaled = sem("q_scaled")
        softplus = sem("softplus")
        gate_in, gate_exp = sem("gate_in"), sem("gate_exp")
        km_ready = sem("km_ready")
        act_step = sem("act_step")
        gp_full = [sem(f"gp_full{i}", one=True) for i in range(2)]
        gp_read = [sem(f"gp_read{i}", one=True) for i in range(2)]
        sc_full = [sem(f"sc_full{i}", one=True) for i in range(2)]
        sc_read = [sem(f"sc_read{i}", one=True) for i in range(2)]
        ot_full = [sem(f"ot_full{i}", one=True) for i in range(2)]
        ot_read = [sem(f"ot_read{i}", one=True) for i in range(2)]

        def gp_wait(eng, sems, st, u, after):
            eng.wait_ge(sems[gp.bank[u]], gp.after(st, u) if after else gp.before(st, u))

        loads = [(wq, w["wq"].rearrange("(k p) n -> p k n", p=P)),
                 (wk, w["wk"].rearrange("(k p) n -> p k n", p=P)),
                 (wv, w["wv"].rearrange("(k p) n -> p k n", p=P)),
                 (wo, w["wo"].rearrange("(c p) n -> p c n", p=P)),
                 (mask, io[f"c_mask{hd}"]), (sel, io["c_sel"])]
        if causal:
            loads += [(eye, io["c_eye"]), (neg_qk, io["c_neg_qk"]), (neg_kq, io["c_neg_kq"])]
        if bias:
            loads += [(bk, w["bk"]),
                      (bv, w["bv"].rearrange("(a n) -> a n", a=1).broadcast_to([P, D])),
                      (bo, w["bo"].rearrange("(a n) -> a n", a=1).broadcast_to([P, D]))]
            if not router:
                loads += [(bq, w["bq"])]
        if router:
            loads += [(bqt, w["bq"].rearrange("(a n) -> a n", a=1).broadcast_to([P, D])),
                      (qe, w["qe"].rearrange("(a n) -> a n", a=1).broadcast_to([P, D])),
                      (sp_t[:, 0, :], w["temp"].rearrange("(a n) -> a n", a=1).broadcast_to([P, H])),
                      (wr, w["wr"].rearrange("(c p) n -> p c n", p=P)),
                      (br, w["br"].rearrange("(a n) -> a n", a=1).broadcast_to([P, H + 1]))]
        all_in = 16 * len(loads)

        start_semaphores(nc, sems, from_one)
        block = ctx.enter_context(nc.Block())

        @block.sync
        def _(sp):
            for dst, src in loads:
                sp.dma_start(dst if isinstance(dst, bass.AP) else dst[:], src).then_inc(weights_in, 16)
            if not kv_from_x:
                u = f"v{NV - 1}"

                def load_context(b):
                    sp.dma_start(kvT[:], io["ctxT"][b].rearrange("(k p) s -> p k s", p=P)).then_inc(kv_in, 16)

                load_context(0)
                sp.wait_ge(gp_full[gp.bank[u]], gp.at_start(Step(1), u))
                load_context(1)
                with sp.Fori(0, B - 2) as b:
                    sp.wait_ge(gp_full[gp.bank[u]], b * gp.per(u) + gp.at_start(Step(DEPTH), u))
                    load_context(b + 2)

        @block.gpsimd
        def _(pool):
            pool.memset(v2[:], 0.0).then_inc(fixed, 1)
            pool.memset(ones[:], 1.0).then_inc(fixed, 1)
            pool.memset(negT[:], 0.0).then_inc(fixed, 1)
            pool.wait_ge(weights_in, all_in)
            def mask_k(st):
                if not st.has(0):
                    return
                for i in range(NKB):
                    gp_wait(pool, gp_read, st, f"k{i}", True)
                    for c in range(2 * i, min(2 * i + 2, CK)):
                        for out in (kM2, kR2):
                            op = pool.tensor_tensor(out[:, st.half(0), c * HC:(c + 1) * HC, :],
                                                    kT[:, c:c + 1, :].broadcast_to([P, HC, S]),
                                                    mask[:].rearrange("p (h a) -> p h a", a=1)
                                                    .broadcast_to([P, HC, S]), ALU.mult)
                op.then_inc(km_ready, 1)

            run_steps(pool, mask_k)

        @block.scalar
        def _(act):
            norm_sqrt(act, g, sqrt_in, sqrt_out)
            act.wait_ge(weights_in, all_in)
            if router:
                act.activation(sp_t[:, 1, :], sp_t[:, 0, :], ACT.Abs).then_inc(act_step, 1)
                act.wait_ge(act_step, 1)
                act.activation(sp_t[:, 1, :], sp_t[:, 1, :], ACT.Exp, scale=-1.0).then_inc(act_step, 1)
                act.wait_ge(act_step, 2)
                act.activation(sp_t[:, 2, :], sp_t[:, 1, :], ACT.Ln, bias=1.0).then_inc(softplus, 1)
            def evacuate(dsts, u, n, st, biases=None):
                gp_wait(act, gp_full, st, u, True)
                for dst in dsts:
                    if biases is None:
                        op = act.activation(dst, GP[gp.bank[u]][:, 0:n, :], ACT.Copy)
                    else:
                        for c in range(n):
                            op = act.activation(dst[:, c, :], GP[gp.bank[u]][:, c, :], ACT.Identity,
                                                bias=biases[:, c:c + 1])
                op.then_inc(gp_read[gp.bank[u]], 1)

            def step(st):
                for what, i in order:
                    if not st.has(PART[what]):
                        continue
                    if what == "xT":
                        evacuate([xnT[:]], "xT", KD, st)
                    elif what == "q" and not router:
                        evacuate([a[:, st.half(0), 2 * i:2 * i + 2, :] for a in (qT2, qR2)], f"q{i}", 2, st,
                                 bq[:, 2 * i:2 * i + 2] if bias else None)
                    elif what == "k":
                        n = min(2, CK - 2 * i)
                        evacuate([kT[:, 2 * i:2 * i + n, :]], f"k{i}", n, st, bk[:, 2 * i:2 * i + n] if bias else None)
                    elif what == "qT":
                        evacuate([a[:, st.half(0)] for a in (qT2, qR2)], "qT", CQ, st)
                    elif what == "score":
                        use = ("exp", i)
                        pair = sc.bank[use]
                        c = 2 * i // HO
                        if 2 * i % HO == 0:
                            if c >= 2:
                                act.wait_ge(ot_full[c % 2], ot.before(st.seq(1), c))
                            else:
                                act.wait_ge(ot_full[c % 2], st.seq(1) * ot.per[c % 2] + 1)
                        act.wait_ge(sc_full[pair], sc.after(st.seq(1), use))
                        h0 = 2 * i % HO
                        pr = probs[:, c % 2, h0:h0 + 2]
                        if causal:
                            act.activation(pr[:, :, 0, :], SC[pair][:, :, 0, :], ACT.Exp, scale=scale)
                            act.activation(pr[:, :, 1, P:S], SC[pair][:, :, 1, P:S], ACT.Exp, scale=scale)\
                               .then_inc(sc_read[pair], 1)
                        else:
                            act.activation(pr, SC[pair][:], ACT.Exp, scale=scale).then_inc(sc_read[pair], 1)
                        if router and i == 1 and st.has(0):
                            head_norms(st)
                    elif what == "gate":
                        act.wait_ge(gate_in, st.seq(2) + 1)
                        act.activation(le[:, :, 0:H + 1], lg[:, :, 0:H + 1], ACT.Exp).then_inc(gate_exp, 1)
                    if what == "k" and router and not st.has(1):
                        head_norms(st)

            def head_norms(st):
                act.wait_ge(q_sums, st.seq(0) + 1)
                act.activation(qn[:, 1], qn[:, 0], ACT.Sqrt).then_inc(q_roots, 1)

            run_steps(act, step)

        @block.tensor
        def _(pe):
            pe.wait_ge(weights_in, all_in)
            pe.wait_ge(fixed, 3)
            def transposed(src, st, u):
                gp_wait(pe, gp_read, st, u, False)
                transpose_xn(pe, g, src, GP[gp.bank[u]]).then_inc(gp_full[gp.bank[u]], 1)

            def features(st, u, wgt, cols, rhs, n0):
                gp_wait(pe, gp_read, st, u, False)
                for c in range(cols):
                    for k in range(KD):
                        op = pe.matmul(GP[gp.bank[u]][:, c, :], wgt[:, k, (n0 + c) * P:(n0 + c + 1) * P],
                                       rhs[:, k, :], start=(k == 0), stop=(k == KD - 1))
                op.then_inc(gp_full[gp.bank[u]], 1)

            def tokens(st, u, lhs, wgt, n0, n):
                gp_wait(pe, gp_read, st, u, False)
                for t in range(TT):
                    for k in range(KD):
                        op = pe.matmul(GP[gp.bank[u]][:, t, 0:n], lhs[:, k, t * P:(t + 1) * P], wgt[:, k, n0:n0 + n],
                                       start=(k == 0), stop=(k == KD - 1))
                op.then_inc(gp_full[gp.bank[u]], 1)

            def row_scores(st, u):
                qR, kR = qR2[:, st.half(1)], kR2[:, st.half(1)]
                use = ("max", u)
                pair = sc.bank[use]
                pe.wait_ge(sc_read[pair], sc.before(st.seq(1), use))
                for j in range(2):
                    h = 2 * u + j
                    for t in range(TT):
                        keys = (t + 1) * P if causal else S
                        op = pe.matmul(SC[pair][:, j, t, 0:keys], qR[:, h // HC, t * P:(t + 1) * P],
                                       kR[:, h % KH, 0:keys], start=True, stop=True)
                        if causal:
                            op = pe.matmul(SC[pair][:, j, t, t * P:keys], eye[:], neg_qk[:],
                                           start=False, stop=True, skip_group_check=True)
                op.then_inc(sc_full[pair], 1)

            def negated_maxima(st):
                gp_wait(pe, gp_read, st, "neg", False)
                for pair in range(2):
                    pe.wait_ge(sc_read[pair], sc.after(st.seq(1), ("max", SU - 2 + pair)))
                for t in range(TT):
                    op = pe.transpose(GP[gp.bank["neg"]][0:H, 0, t * P:(t + 1) * P], mx[:, t, :], g.ident[:])
                op.then_inc(gp_full[gp.bank["neg"]], 1)

            def scores(st, u):
                qT, kM = qT2[:, st.half(1)], kM2[:, st.half(1)]
                use = ("exp", u)
                pair = sc.bank[use]
                pe.wait_ge(sc_read[pair], sc.before(st.seq(1), use))
                for j in range(2):
                    h = 2 * u + j
                    for t in range(TT):
                        q0 = t * P if causal else 0
                        out = SC[pair][:, j, t, q0:S]
                        pe.matmul(out, kM[:, h % KH, t * P:(t + 1) * P], qT[:, h // HC, q0:S],
                                  start=True, stop=False)
                        op = pe.matmul(out, sel[:, h, :], negT[:, q0:S], start=False, stop=True)
                        if causal:
                            op = pe.matmul(SC[pair][:, j, t, t * P:(t + 1) * P], eye[:], neg_kq[:],
                                           start=False, stop=True, skip_group_check=True)
                op.then_inc(sc_full[pair], 1)

            def weigh(st, c):
                v = v2[:, st.half(1)]
                for u in range(c * HO // 2, (c + 1) * HO // 2):
                    use = ("exp", u)
                    pe.wait_ge(sc_read[sc.bank[use]], sc.after(st.seq(1), use))
                pe.wait_ge(ot_read[c % 2], ot.before(st.seq(1), c))
                for what in range(2):
                    for j, t in [(j, t) for j in range(HO) for t in range(TT)] if interleave else \
                            [(j, t) for t in range(TT) for j in range(HO)]:
                        h = c * HO + j
                        q0 = t * P if causal else 0
                        lhs = v[:, t, h % VH, :] if what == 0 else ones[:]
                        if interleave:
                            for par in range(2):
                                op = pe.matmul(OT[c % 2][par * HP:(par + 1) * HP, what, j * P + q0 // 2:(j + 1) * P],
                                               lhs, probs[:, c % 2, j, t, q0 + par:S:2],
                                               start=(t == 0), stop=(t == TT - 1))
                        else:
                            op = pe.matmul(OT[c % 2][j * HP:(j + 1) * HP, what, q0:S], lhs,
                                           probs[:, c % 2, j, t, q0:S], start=(t == 0), stop=(t == TT - 1))
                op.then_inc(ot_full[c % 2], 1)

            def heads_out(st, u, wgt, n):
                for i in range(2):
                    pe.wait_ge(ot_read[i], ot.after(st.seq(2), CO - 2 + i))
                gp_wait(pe, gp_read, st, u, False)
                for t in range(TT):
                    for c in range(CO):
                        if interleave:
                            lhs = oT[:].rearrange("p c (j i r) -> p r (c j) i", j=HO, r=CO)[:, c, 8 * t:8 * t + 8, :]
                        else:
                            lhs = oT[:, c, t * P:(t + 1) * P]
                        op = pe.matmul(GP[gp.bank[u]][:, t, 0:n], lhs, wgt[:, c, :],
                                       start=(c == 0), stop=(c == CO - 1))
                op.then_inc(gp_full[gp.bank[u]], 1)

            def step(st):
                for what, i in order:
                    if not st.has(PART[what]):
                        continue
                    if what == "xT":
                        pe.wait_ge(xn_ready, st.seq(0) + 1)
                        transposed(xn, st, "xT")
                    elif what == "q":
                        gp_wait(pe, gp_read, st, "xT", True)
                        if router:
                            tokens(st, "q0", xnT, wq, 0, D)
                        else:
                            features(st, f"q{i}", wq, 2, xnT, 2 * i)
                    elif what == "k":
                        if not kv_from_x:
                            pe.wait_ge(kv_in, st.seq(0) * 16 + 16)
                        features(st, f"k{i}", wk, min(2, CK), kvT, 2 * i)
                    elif what == "v":
                        n = min(VH * hd, D)
                        tokens(st, f"v{i}", kvT, wv, i * n, n)
                    elif what == "qT":
                        pe.wait_ge(q_scaled, st.seq(0) + 1)
                        transposed(qtm, st, "qT")
                    elif what == "max":
                        if i == 0:
                            pe.wait_ge(km_ready, st.seq(1) + 1)
                            u = "qT" if router else f"q{NQ - 1}"
                            pe.wait_ge(gp_read[gp.bank[u]], gp.at_start(st, u))
                        row_scores(st, i)
                    elif what == "neg":
                        negated_maxima(st)
                    elif what == "score":
                        if i == 0:
                            gp_wait(pe, gp_read, st, "neg", True)
                        scores(st, i)
                    elif what == "weigh":
                        if i == 0:
                            pe.wait_ge(gp_read[gp.bank[f"v{NV - 1}"]], gp.at_start(st, f"v{NV - 1}"))
                        weigh(st, i)
                    elif what == "gate":
                        heads_out(st, "gate", wr, H + 1)
                    elif what == "y":
                        heads_out(st, "y", wo, D)

            run_steps(pe, step)

        @block.vector
        def _(dve):
            over_tokens = lambda row: row[:].rearrange("p (a n) -> p a n", a=1).broadcast_to([P, TT, D])

            def gate_logits(st):
                gp_wait(dve, gp_full, st, "gate", True)
                dve.tensor_tensor(lg[:, :, 0:H + 1], GP[gp.bank["gate"]][:, :, 0:H + 1],
                                  br[:].rearrange("p (a n) -> p a n", a=1).broadcast_to([P, TT, H + 1]), ALU.add)\
                   .then_inc(gp_read[gp.bank["gate"]], 1)
                dve.drain()
                for i, (lo, hi) in enumerate(((0, H - 1), (H - 1, H + 1))):
                    dve.tensor_reduce(sm[:, :, i], lg[:, :, lo:hi], AX.X, ALU.max)
                dve.drain()
                for i, (lo, hi) in enumerate(((0, H - 1), (H - 1, H + 1))):
                    op = dve.tensor_tensor(lg[:, :, lo:hi], lg[:, :, lo:hi],
                                           sm[:, :, i:i + 1].broadcast_to([P, TT, hi - lo]), ALU.subtract)
                op.then_inc(gate_in, 1)

            def gate_factor(st):
                dve.wait_ge(gate_exp, st.seq(2) + 1)
                for i, (lo, hi) in enumerate(((0, H - 1), (H - 1, H + 1))):
                    dve.tensor_reduce(sm[:, :, i], le[:, :, lo:hi], AX.X, ALU.add)
                for t in range(TT):
                    dve.max(top[:, t, :], le[:, t, 0:H - 1])
                dve.drain()
                dve.tensor_reduce(sm[:, :, 2], top[:, :, 0:3], AX.X, ALU.add)
                dve.reciprocal(sm[:, :, 3:5], sm[:, :, 0:2])
                dve.drain()
                dve.tensor_tensor(sm[:, :, 2], sm[:, :, 2], sm[:, :, 3], ALU.mult)
                dve.tensor_tensor(sm[:, :, 5:7], le[:, :, H - 1:H + 1], sm[:, :, 4:5].broadcast_to([P, TT, 2]), ALU.mult)
                dve.drain()
                dve.tensor_tensor(sm[:, :, 0], sm[:, :, 5], sm[:, :, 6], ALU.add)
                dve.tensor_tensor(sm[:, :, 1], sm[:, :, 6], sm[:, :, 2], ALU.mult)
                dve.drain()
                dve.tensor_tensor(sm[:, :, 0], sm[:, :, 0], sm[:, :, 5], ALU.mult)
                dve.tensor_scalar(sm[:, :, 1], sm[:, :, 1], 3.0, None, ALU.mult)
                dve.drain()
                dve.tensor_tensor(sm[:, :, 0], sm[:, :, 0], sm[:, :, 1], ALU.add)
                dve.drain()
                dve.tensor_scalar(sm[:, :, 7], sm[:, :, 0], 2.0, None, ALU.mult)
                dve.drain()

            norm_factors(dve, g, sqrt_in, sqrt_out)
            dve.wait_ge(weights_in, all_in)
            dve.wait_ge(fixed, 3)
            if router:
                dve.wait_ge(softplus, 1)
                dve.tensor_scalar(sp_t[:, 3, :], sp_t[:, 0, :], 0.0, None, ALU.max)
                dve.drain()
                dve.tensor_tensor(spq[:], sp_t[:, 3, :], sp_t[:, 2, :], ALU.add)
                dve.drain()
                qeh = qe[:].rearrange("p (h d) -> p h d", d=hd)
                dve.tensor_tensor(qeh, qeh, spq[:].rearrange("p (h a) -> p h a", a=1).broadcast_to([P, H, hd]), ALU.mult)
                dve.drain()
            def tokens_q(st):
                gp_wait(dve, gp_full, st, "q0", True)
                dve.tensor_tensor(qtm[:], GP[gp.bank["q0"]][:], over_tokens(bqt), ALU.add)\
                   .then_inc(gp_read[gp.bank["q0"]], 1)

            def square_q(st):
                dve.drain()
                dve.tensor_tensor(qsq[:], qtm[:], qtm[:], ALU.mult)
                dve.drain()
                dve.tensor_reduce(qn[:, 0], qsq[:].rearrange("p t (h d) -> p t h d", d=hd), AX.X, ALU.add)\
                   .then_inc(q_sums, 1)

            def scale_q(st):
                dve.wait_ge(q_roots, st.seq(0) + 1)
                dve.reciprocal(qn[:, 2], qn[:, 1])
                dve.drain()
                dve.tensor_tensor(qn[:, 1], qn[:, 2], qn[:, 2], ALU.mult)
                dve.drain()
                dve.tensor_tensor(qn[:, 1], qn[:, 1], qn[:, 0], ALU.mult)
                dve.drain()
                dve.tensor_scalar(qn[:, 1], qn[:, 1], -0.5, 1.5, ALU.mult, ALU.add)
                dve.drain()
                dve.tensor_tensor(qn[:, 2], qn[:, 2], qn[:, 1], ALU.mult)
                dve.drain()
                dve.tensor_tensor(qn[:, 2], qn[:, 2],
                                  spq[:].rearrange("p (a h) -> p a h", a=1).broadcast_to([P, TT, H]), ALU.mult)
                dve.drain()
                qh = qtm[:].rearrange("p t (h d) -> p t h d", d=hd)
                dve.tensor_tensor(qh, qh, qn[:, 2].rearrange("p t (h a) -> p t h a", a=1)
                                  .broadcast_to([P, TT, H, hd]), ALU.mult)
                dve.drain()
                dve.tensor_tensor(qtm[:], qtm[:], over_tokens(qe), ALU.add).then_inc(q_scaled, 1)

            def copy_v(st, i):
                v, u = v2[:, st.half(0)], f"v{i}"
                gp_wait(dve, gp_full, st, u, True)
                if shared_kv:
                    op = dve.tensor_copy(v[:, :, 0, 0:hd], GP[gp.bank[u]][:, :, 0:hd])
                else:
                    hv = D // hd
                    src = GP[gp.bank[u]][:].rearrange("p t (h d) -> p t h d", d=hd)
                    for t in range(TT):
                        dst = v[:, t, i * hv:(i + 1) * hv, 0:hd]
                        if bias:
                            op = dve.tensor_tensor(dst, src[:, t], bv[:].rearrange("p (h d) -> p h d", d=hd), ALU.add)
                        else:
                            op = dve.tensor_copy(dst, src[:, t])
                op.then_inc(gp_read[gp.bank[u]], 1)

            def row_maxima(st, u):
                use = ("max", u)
                pair = sc.bank[use]
                dve.wait_ge(sc_full[pair], sc.after(st.seq(1), use))
                for t in range(TT):
                    keys = (t + 1) * P if causal else S
                    op = dve.tensor_reduce(mx[:, t, 2 * u:2 * u + 2], SC[pair][:, :, t, 0:keys], AX.X, ALU.max,
                                           negate=True)
                op.then_inc(sc_read[pair], 1)

            def split_maxima(st):
                gp_wait(dve, gp_full, st, "neg", True)
                src = GP[gp.bank["neg"]][0:H, 0, :]
                dve.tensor_copy(negT[0:H, :], src)
                dve.drain()
                dve.tensor_tensor(rest[:], src, negT[0:H, :], ALU.subtract)
                dve.drain()
                dve.tensor_copy(negT[32:32 + H, :], rest[:])
                dve.drain()
                dve.tensor_tensor(negT[64:64 + H, :], rest[:], negT[32:32 + H, :], ALU.subtract)\
                   .then_inc(gp_read[gp.bank["neg"]], 1)

            def divide(st, c):
                dve.wait_ge(ot_full[c % 2], ot.after(st.seq(1), c))
                dve.reciprocal(rden[:, c % 2], OT[c % 2][:, 1, :])
                dve.drain()
                dve.tensor_tensor(oT[:, c, :], OT[c % 2][:, 0, :], rden[:, c % 2], ALU.mult).then_inc(ot_read[c % 2], 1)

            def add_y(st):
                gp_wait(dve, gp_full, st, "y", True)
                if router:
                    for t in range(TT):
                        op = dve.scalar_tensor_tensor(out=yt[:, t], in0=GP[gp.bank["y"]][:, t], scalar=sm[:, t, 7:8],
                                                      in1=bo[:], op0=ALU.mult, op1=ALU.add)
                    op.then_inc(gp_read[gp.bank["y"]], 1)
                    dve.drain()
                    add_to_x(dve, g, st.seq(2), yt[:])
                else:
                    add_to_x(dve, g, st.seq(2), GP[gp.bank["y"]][:]).then_inc(gp_read[gp.bank["y"]], 1)
                    if bias:
                        dve.drain()
                        add_to_x(dve, g, st.seq(2), over_tokens(bo))
                dve.drain()
                next_stats(dve, g, st.seq(2))

            def step(st):
                for what, i in order:
                    if not st.has(PART[what]):
                        continue
                    if what == "norm":
                        normalise(dve, g, st.seq(0), xn, xn_ready)
                    elif what == "q" and router:
                        tokens_q(st)
                    elif what == "v":
                        copy_v(st, i)
                    elif what == "max":
                        row_maxima(st, i)
                    elif what == "neg":
                        split_maxima(st)
                        if router and st.has(0):
                            square_q(st)
                    elif what == "qT":
                        if not st.has(1):
                            square_q(st)
                        scale_q(st)
                    elif what == "weigh":
                        divide(st, i)
                    elif what == "gate":
                        gate_logits(st)
                        gate_factor(st)
                    elif what == "y":
                        add_y(st)
                dve.drain()

            run_steps(dve, step)


def root(dve, out, square, inverse, half):
    dve.tensor_tensor(half, inverse, inverse, ALU.mult)
    dve.drain()
    dve.tensor_tensor(half, half, square, ALU.mult)
    dve.drain()
    dve.tensor_scalar(half, half, -0.5, 1.5, ALU.mult, ALU.add)
    dve.drain()
    dve.tensor_tensor(out, inverse, half, ALU.mult)
    dve.drain()


RETENTION = [("score", 0), ("norm", 0), ("score", 1), ("aT", 0), ("xT", 0), ("score", 2), ("weigh", 0), ("k", 0),
             ("score", 3), ("y", 0), ("score", 4), ("weigh", 1), ("kr", 0), ("q", 0), ("score", 5), ("score", 6),
             ("weigh", 2), ("qr", 0), ("score", 7), ("weigh", 3), ("T0", 0), ("T1", 0), ("group", 0), ("v", 0),
             ("g", 0)]
RETENTION_PART = {"norm": 0, "xT": 0, "q": 0, "k": 0, "qr": 0, "kr": 0, "v": 0, "g": 0,
                  "score": 1, "weigh": 1, "T0": 1, "T1": 1, "group": 1, "aT": 2, "y": 2}


def retention(nc, g, name, w):
    io = g.io
    hd = 16
    CQ, HC, HP, HO, CO = 2, 8, 32, 4, 4
    SU = H // 2
    part_of = RETENTION_PART
    gp = StepBanks([(what, part_of[what]) for what, _ in RETENTION
                    if what not in ("norm", "score", "weigh", "group")])
    sc = Banks(list(range(SU)))
    ot = Banks(list(range(CO)))
    with ExitStack() as ctx:
        sb = lambda n, s, t=F32: ctx.enter_context(nc.sbuf_tensor(f"{name}_sb_{n}", s, t))
        sems, from_one = [], []

        def sem(n, one=False):
            s = ctx.enter_context(nc.semaphore(f"{name}_{n}"))
            (from_one if one else sems).append(s)
            return s
        wq, wk, wv, wg, wo = (sb(n, [P, KD, D]) for n in ("wq", "wk", "wv", "wg", "wo"))
        turn = sb("turn", [P, P])
        mask = sb("mask", [P, HC])
        tri = sb("tri", [P, P])
        tables = sb("tables", [P, 4, CQ, S])
        gb, bo = sb("gb", [P, D]), sb("bo", [P, D])
        xn = sb("xn", [P, TT, D])
        xnT = sb("xnT", [P, KD, S])
        kvT = sb("kvT", [P, KD, S])
        raw = sb("raw", [P, 2, CQ, S])
        qk2 = sb("qk", [P, 2, 2, CQ, S])
        part = sb("part", [P, 2, CQ, S])
        kM2 = sb("kM", [P, 2, H, S])
        v2 = sb("v", [P, 2, TT, H, HP])
        sim = sb("sim", [P, 2, HO, TT, S])
        oraw = sb("oraw", [P, CO, S])
        ret = sb("ret", [P, TT, D])
        sq = sb("sq", [P, TT, D])
        gn = sb("gn", [P, 4, TT, H])
        gz = sb("gz", [P, TT, D])
        gate2 = sb("gate", [P, 2, TT, D])
        aT = sb("aT", [P, KD, S])
        GP = [ctx.enter_context(nc.psum_tensor(f"{name}_gp{i}", [P, 2, S], F32)) for i in range(2)]
        SC = [ctx.enter_context(nc.psum_tensor(f"{name}_sc{i}", [P, 2, 2, S], F32)) for i in range(2)]
        OT = [ctx.enter_context(nc.psum_tensor(f"{name}_ot{i}", [P, 2, S], F32)) for i in range(2)]

        weights_in, kv_in = sem("weights_in"), sem("kv_in")
        sqrt_in, sqrt_out, fixed = sem("sqrt_in"), sem("sqrt_out"), sem("fixed")
        xn_ready, turned, km_ready = sem("xn_ready"), sem("turned"), sem("km_ready")
        gate_z, gate_ready = sem("gate_z"), sem("gate_ready")
        variance, deviation, ret_ready = sem("variance"), sem("deviation"), sem("ret_ready")
        gp_full = [sem(f"gp_full{i}", one=True) for i in range(2)]
        gp_read = [sem(f"gp_read{i}", one=True) for i in range(2)]
        sc_full = [sem(f"sc_full{i}", one=True) for i in range(2)]
        sc_read = [sem(f"sc_read{i}", one=True) for i in range(2)]
        ot_full = [sem(f"ot_full{i}", one=True) for i in range(2)]
        ot_read = [sem(f"ot_read{i}", one=True) for i in range(2)]

        def full(eng, st, u):
            eng.wait_ge(gp_full[gp.bank[u]], gp.after(st, u))

        def free(eng, st, u):
            eng.wait_ge(gp_read[gp.bank[u]], gp.before(st, u))

        def read(eng, st, u):
            eng.wait_ge(gp_read[gp.bank[u]], gp.after(st, u))

        def entries(st):
            return [e for e in RETENTION if st.has(part_of[e[0]])]

        row = lambda a: a.rearrange("(a n) -> a n", a=1).broadcast_to([P, D])
        loads = [(t[:], w[n].rearrange("(k p) n -> p k n", p=P))
                 for t, n in ((wq, "wq"), (wk, "wk"), (wv, "wv"), (wg, "wg"), (wo, "wo"))]
        loads += [(turn[:], io["c_turn"]), (mask[:], io["c_mask16"]), (tri[:], io["c_tri"]),
                  (tables[:], io["c_tables"]), (gb[:], row(w["gb"])), (bo[:], row(w["bo"]))]
        all_in = 16 * len(loads)
        start_semaphores(nc, sems, from_one)
        block = ctx.enter_context(nc.Block())

        @block.sync
        def _(sp):
            for dst, src in loads:
                sp.dma_start(dst, src).then_inc(weights_in, 16)

            def load_context(b):
                sp.dma_start(kvT[:], io["ctxT"][b].rearrange("(k p) s -> p k s", p=P)).then_inc(kv_in, 16)

            load_context(0)
            sp.wait_ge(gp_full[gp.bank["v"]], gp.at_start(Step(1), "v"))
            load_context(1)
            with sp.Fori(0, B - 2) as b:
                sp.wait_ge(gp_full[gp.bank["v"]], b * gp.per("v") + gp.at_start(Step(DEPTH), "v"))
                load_context(b + 2)

        @block.gpsimd
        def _(pool):
            pool.memset(v2[:], 0.0).then_inc(fixed, 1)
            pool.wait_ge(weights_in, all_in)

            def step(st):
                if st.has(0):
                    pool.wait_ge(turned, st.seq(0) * 2 + 1)
                    for c in range(CQ):
                        op = pool.tensor_tensor(kM2[:, st.half(0), c * HC:(c + 1) * HC, :],
                                                qk2[:, st.half(0), 1, c:c + 1, :].broadcast_to([P, HC, S]),
                                                mask[:].rearrange("p (h a) -> p h a", a=1).broadcast_to([P, HC, S]),
                                                ALU.mult)
                    op.then_inc(km_ready, 1)

            run_steps(pool, step)

        @block.scalar
        def _(act):
            norm_sqrt(act, g, sqrt_in, sqrt_out)
            act.wait_ge(fixed, 1)

            def evacuate(dst, st, u):
                full(act, st, u)
                act.activation(dst, GP[gp.bank[u]][:], ACT.Copy).then_inc(gp_read[gp.bank[u]], 1)

            def step(st):
                for what, c in entries(st):
                    if what == "xT":
                        evacuate(xnT[:], st, "xT")
                    elif what == "q":
                        evacuate(raw[:, 0], st, "q")
                    elif what == "k":
                        evacuate(raw[:, 1], st, "k")
                    elif what == "v":
                        full(act, st, "v")
                        for t in range(TT):
                            op = act.activation(v2[:, st.half(0), t, :, 0:hd],
                                                GP[gp.bank["v"]][:, t, :].rearrange("p (h d) -> p h d", d=hd), ACT.Copy)
                        op.then_inc(gp_read[gp.bank["v"]], 1)
                    elif what == "g":
                        act.wait_ge(gate_z, st.seq(0) + 1)
                        act.activation(gate2[:, st.half(0)], gz[:], ACT.Silu).then_inc(gate_ready, 1)
                    elif what == "weigh":
                        act.wait_ge(ot_full[c % 2], ot.after(st.seq(1), c))
                        act.activation(oraw[:, c, :], OT[c % 2][:, 0, :], ACT.Copy).then_inc(ot_read[c % 2], 1)
                    elif what == "group":
                        act.wait_ge(variance, st.seq(1) + 1)
                        act.activation(gn[:, 1], gn[:, 0], ACT.Sqrt).then_inc(deviation, 1)
                    elif what == "aT":
                        evacuate(aT[:], st, "aT")

            run_steps(act, step)

        @block.tensor
        def _(pe):
            pe.wait_ge(weights_in, all_in)
            pe.wait_ge(fixed, 1)

            def feature_major(st, u, wgt, rhs):
                free(pe, st, u)
                for c in range(CQ):
                    for k in range(KD):
                        op = pe.matmul(GP[gp.bank[u]][:, c, :], wgt[:, k, c * P:(c + 1) * P], rhs[:, k, :],
                                       start=(k == 0), stop=(k == KD - 1))
                op.then_inc(gp_full[gp.bank[u]], 1)

            def token_major(st, u, act_T, wgt):
                free(pe, st, u)
                for t in range(TT):
                    for k in range(KD):
                        op = pe.matmul(GP[gp.bank[u]][:, t, :], act_T[:, k, t * P:(t + 1) * P], wgt[:, k, :],
                                       start=(k == 0), stop=(k == KD - 1))
                op.then_inc(gp_full[gp.bank[u]], 1)

            def turn_pairs(st, u, i):
                free(pe, st, u)
                for c in range(CQ):
                    op = pe.matmul(GP[gp.bank[u]][:, c, :], turn[:], raw[:, i, c, :], start=True, stop=True)
                op.then_inc(gp_full[gp.bank[u]], 1)

            def transposed(st, u, src):
                free(pe, st, u)
                transpose_xn(pe, g, src, GP[gp.bank[u]]).then_inc(gp_full[gp.bank[u]], 1)

            def scores(st, u):
                b = st.seq(1)
                pe.wait_ge(sc_read[sc.bank[u]], sc.before(b, u))
                for j in range(2):
                    h = 2 * u + j
                    for t in range(TT):
                        op = pe.matmul(SC[sc.bank[u]][:, j, t, t * P:S], kM2[:, st.half(1), h, t * P:(t + 1) * P],
                                       qk2[:, st.half(1), 0, h // HC, t * P:S], start=True, stop=True)
                op.then_inc(sc_full[sc.bank[u]], 1)

            def weigh(st, c):
                b = st.seq(1)
                for u in (2 * c, 2 * c + 1):
                    pe.wait_ge(sc_read[sc.bank[u]], sc.after(b, u))
                pe.wait_ge(ot_read[c % 2], ot.before(b, c))
                for t in range(TT):
                    for j in range(HO):
                        op = pe.matmul(OT[c % 2][j * HP:(j + 1) * HP, 0, t * P:S], v2[:, st.half(1), t, c * HO + j, :],
                                       sim[:, c % 2, j, t, t * P:S], start=(t == 0), stop=(t == TT - 1))
                op.then_inc(ot_full[c % 2], 1)

            def retained(st, t):
                u = f"T{t}"
                free(pe, st, u)
                flat = GP[gp.bank[u]][:].rearrange("p a n -> p (a n)")
                for c in range(CO):
                    op = pe.transpose(flat[:, c * P:(c + 1) * P], oraw[:, c, t * P:(t + 1) * P], g.ident[:])
                op.then_inc(gp_full[gp.bank[u]], 1)

            def step(st):
                for what, i in entries(st):
                    if what == "xT":
                        pe.wait_ge(xn_ready, st.seq(0) + 1)
                        transposed(st, "xT", xn)
                    elif what == "q":
                        read(pe, st, "xT")
                        feature_major(st, "q", wq, xnT)
                    elif what == "k":
                        pe.wait_ge(kv_in, st.seq(0) * 16 + 16)
                        feature_major(st, "k", wk, kvT)
                    elif what == "kr":
                        read(pe, st, "k")
                        turn_pairs(st, "kr", 1)
                    elif what == "qr":
                        read(pe, st, "q")
                        turn_pairs(st, "qr", 0)
                    elif what == "v":
                        token_major(st, "v", kvT, wv)
                    elif what == "g":
                        token_major(st, "g", xnT, wg)
                    elif what == "score":
                        if i == 0:
                            pe.wait_ge(km_ready, st.seq(1) + 1)
                            pe.wait_ge(turned, st.seq(1) * 2 + 2)
                        scores(st, i)
                    elif what == "weigh":
                        if i == 0:
                            pe.wait_ge(gp_read[gp.bank["v"]], gp.at_start(st, "v"))
                        weigh(st, i)
                    elif what == "T0":
                        for c in (CO - 2, CO - 1):
                            pe.wait_ge(ot_read[c % 2], ot.after(st.seq(1), c))
                        retained(st, 0)
                    elif what == "T1":
                        retained(st, 1)
                    elif what == "aT":
                        pe.wait_ge(ret_ready, st.seq(2) + 1)
                        transposed(st, "aT", ret)
                    elif what == "y":
                        read(pe, st, "aT")
                        token_major(st, "y", aT, wo)

            run_steps(pe, step)

        @block.vector
        def _(dve):
            rows = lambda a: a[:].rearrange("p (a n) -> p a n", a=1).broadcast_to([P, TT, D])
            heads = lambda a: a[:].rearrange("p t (h d) -> p (t h) d", d=hd)
            per_head = lambda a: a.rearrange("p t (h a) -> p (t h) a", a=1).broadcast_to([P, TT * H, hd])
            norm_factors(dve, g, sqrt_in, sqrt_out)
            dve.wait_ge(weights_in, all_in)
            dve.wait_ge(fixed, 1)

            def turn(st, i, u, src):
                read(dve, st, src)
                dve.tensor_tensor(part[:, 0], raw[:, i], tables[:, 2 * i], ALU.mult)
                full(dve, st, u)
                dve.tensor_tensor(part[:, 1], GP[gp.bank[u]][:], tables[:, 2 * i + 1], ALU.mult)\
                   .then_inc(gp_read[gp.bank[u]], 1)
                dve.drain()
                dve.tensor_tensor(qk2[:, st.half(0), i], part[:, 0], part[:, 1], ALU.add).then_inc(turned, 1)
                dve.drain()

            def keep_triangle(st, u):
                b, c = st.seq(1), u // 2
                if u % 2 == 0:
                    dve.wait_ge(ot_full[c % 2], ot.before(b, c))
                dve.wait_ge(sc_full[sc.bank[u]], sc.after(b, u))
                dst = sim[:, c % 2, 2 * (u % 2):2 * (u % 2) + 2]
                src = SC[sc.bank[u]]
                for t in range(TT):
                    dve.tensor_tensor(dst[:, :, t, t * P:(t + 1) * P], src[:, :, t, t * P:(t + 1) * P],
                                      tri[:].rearrange("p (a n) -> p a n", a=1).broadcast_to([P, 2, P]), ALU.mult)
                dve.tensor_copy(dst[:, :, 0, P:S], src[:, :, 0, P:S]).then_inc(sc_read[sc.bank[u]], 1)
                dve.drain()

            def group_norm(st):
                dve.drain()
                dve.tensor_reduce(gn[:, 0].rearrange("p t h -> p (t h)"), heads(ret), AX.X, ALU.add)
                dve.drain()
                dve.tensor_scalar(gn[:, 0], gn[:, 0], 1.0 / hd, None, ALU.mult)
                dve.drain()
                dve.tensor_tensor(heads(ret), heads(ret), per_head(gn[:, 0]), ALU.subtract)
                dve.drain()
                dve.tensor_tensor(sq[:], ret[:], ret[:], ALU.mult)
                dve.drain()
                dve.tensor_reduce(gn[:, 0].rearrange("p t h -> p (t h)"), heads(sq), AX.X, ALU.add)
                dve.drain()
                dve.tensor_scalar(gn[:, 0], gn[:, 0], 1.0 / hd, EPS, ALU.mult, ALU.add).then_inc(variance, 1)
                dve.wait_ge(deviation, st.seq(1) + 1)
                dve.reciprocal(gn[:, 2], gn[:, 1])
                dve.drain()
                root(dve, gn[:, 2], gn[:, 0], gn[:, 2], gn[:, 3])
                dve.tensor_tensor(heads(ret), heads(ret), per_head(gn[:, 2]), ALU.mult)
                dve.drain()
                dve.wait_ge(gate_ready, st.seq(1) + 1)
                dve.tensor_tensor(ret[:], ret[:], gate2[:, st.half(1)], ALU.mult).then_inc(ret_ready, 1)

            def step(st):
                for what, i in entries(st):
                    if what == "norm":
                        normalise(dve, g, st.seq(0), xn, xn_ready)
                    elif what == "kr":
                        turn(st, 1, "kr", "k")
                    elif what == "qr":
                        turn(st, 0, "qr", "q")
                    elif what == "g":
                        full(dve, st, "g")
                        dve.tensor_tensor(gz[:], GP[gp.bank["g"]][:], rows(gb), ALU.add)\
                           .then_inc(gp_read[gp.bank["g"]], 1)
                        dve.drain()
                        dve.sem_inc(gate_z, 1)
                    elif what == "score":
                        keep_triangle(st, i)
                    elif what in ("T0", "T1"):
                        full(dve, st, what)
                        src = GP[gp.bank[what]][:].rearrange("p a n -> p (a n)")
                        src = src.rearrange("p (h e) -> p h e", e=HP)[:, :, 0:hd]
                        dve.tensor_copy(ret[:, int(what[1]), :].rearrange("p (h d) -> p h d", d=hd), src)\
                           .then_inc(gp_read[gp.bank[what]], 1)
                    elif what == "group":
                        group_norm(st)
                    elif what == "y":
                        full(dve, st, "y")
                        add_to_x(dve, g, st.seq(2), GP[gp.bank["y"]][:]).then_inc(gp_read[gp.bank["y"]], 1)
                        dve.drain()
                        add_to_x(dve, g, st.seq(2), rows(bo))
                        dve.drain()
                        next_stats(dve, g, st.seq(2))
                dve.drain()

            run_steps(dve, step)


def top_rank(dve, rank, cmp, eq, s, earlier, t, n):
    other = s[:, t, 0:n].rearrange("p (a n) -> p a n", a=1).broadcast_to([P, n, n])
    own = s[:, t, 0:n].rearrange("p (n a) -> p n a", a=1).broadcast_to([P, n, n])
    dve.tensor_tensor(cmp, other, own, ALU.is_gt)
    dve.tensor_tensor(eq, other, own, ALU.is_equal)
    dve.drain()
    dve.tensor_tensor(eq, eq, earlier, ALU.mult)
    dve.drain()
    dve.tensor_tensor(cmp, cmp, eq, ALU.add)
    dve.drain()
    dve.tensor_reduce(rank[:, t, 0:n], cmp, AX.X, ALU.add)
    dve.drain()


def experts(nc, g, name, w, gated):
    io = g.io
    E = 16 if gated else 8
    SH = 2 if gated else 1
    HX = 2 if gated else 1
    gp = Banks(["xT", "logits", "cT"])
    n_h = E + SH
    hb = Banks(list(range(n_h)))
    cb = Banks(list(range(SH, n_h)))
    with ExitStack() as ctx:
        sb = lambda n, s, t=F32: ctx.enter_context(nc.sbuf_tensor(f"{name}_sb_{n}", s, t))
        sems, from_one = [], []

        def sem(n, one=False):
            s = ctx.enter_context(nc.semaphore(f"{name}_{n}"))
            (from_one if one else sems).append(s)
            return s
        w1 = sb("w1", [P, n_h, KD, P])
        w2 = sb("w2", [P, n_h, D])
        wr = sb("wr", [P, KD, E])
        sel = sb("sel", [P, H, P], BF16)
        earlier = sb("earlier", [P, H, H])
        if gated:
            w3 = sb("w3", [P, n_h, KD, P])
            b1, b3 = sb("b1", [P, n_h]), sb("b3", [P, n_h])
            br = sb("br", [P, E])
            b2 = sb("b2", [P, D])
            bs = sb("bs", [P, D])
            pairs = sb("pairs", [P, TT, 4, 6])
            gs = sb("gs", [P, TT, 4])
            grank = sb("grank", [P, TT, 4])
        xn = sb("xn", [P, TT, D])
        xnT = sb("xnT", [P, KD, S])
        lg = sb("lg", [P, TT, E])
        ex = sb("ex", [P, TT, E])
        red = sb("red", [P, 2, TT])
        score = sb("score", [P, TT, E])
        cmp, eq = sb("cmp", [P, E, E]), sb("eq", [P, E, E])
        rank = sb("rank", [P, TT, E])
        top = sb("top", [P, TT, 8])
        c = sb("c", [P, TT, E])
        cT = sb("cT", [P, S])
        cTb = sb("cTb", [P, S], BF16)
        rest = sb("rest", [E, S])
        act_out = sb("act_out", [P, 2, S])
        hT = sb("hT", [P, 2, S])
        hc = sb("hc", [P, 2, S])
        yt = sb("yt", [P, TT, D])
        GP = [ctx.enter_context(nc.psum_tensor(f"{name}_gp{i}", [P, 2, S], F32)) for i in range(2)]
        HB = [ctx.enter_context(nc.psum_tensor(f"{name}_hb{i}", [P, 2, S], F32)) for i in range(2)]
        CB = [ctx.enter_context(nc.psum_tensor(f"{name}_cb{i}", [P, 2, S], F32)) for i in range(2)]
        YB = [ctx.enter_context(nc.psum_tensor(f"{name}_yb{i}", [P, 2, S], F32)) for i in range(TT)]

        weights_in, sqrt_in, sqrt_out, fixed = sem("weights_in"), sem("sqrt_in"), sem("sqrt_out"), sem("fixed")
        xn_ready, logits_ready, exp_ready, c_ready = (sem("xn_ready"), sem("logits_ready"), sem("exp_ready"),
                                                      sem("c_ready"))
        gp_full = [sem(f"gp_full{i}", one=True) for i in range(2)]
        gp_read = [sem(f"gp_read{i}", one=True) for i in range(2)]
        hb_full = [sem(f"hb_full{i}", one=True) for i in range(2)]
        act_ready = [sem(f"act_ready{i}", one=True) for i in range(2)]
        hb_read = [sem(f"hb_read{i}", one=True) for i in range(2)]
        cb_full = [sem(f"cb_full{i}", one=True) for i in range(2)]
        h_ready = [sem(f"h_ready{i}", one=True) for i in range(2)]
        h_used = [sem(f"h_used{i}", one=True) for i in range(2)]
        y_full, y_read = sem("y_full"), sem("y_read", one=True)

        def full(eng, b, u):
            eng.wait_ge(gp_full[gp.bank[u]], gp.after(b, u))

        def free(eng, b, u):
            eng.wait_ge(gp_read[gp.bank[u]], gp.before(b, u))

        def read(eng, b, u):
            eng.wait_ge(gp_read[gp.bank[u]], gp.after(b, u))

        row = lambda a, n: a.rearrange("(a n) -> a n", a=1).broadcast_to([P, n])
        loads = [(w1[:], w["w1"]), (w2[:], w["w2"]), (wr[:], w["wr"].rearrange("(k p) n -> p k n", p=P)),
                 (sel[:], io["c_sel"]), (earlier[:], io["c_earlier"])]
        if gated:
            loads += [(w3[:], w["w3"]), (b1[:], w["b1"]), (b3[:], w["b3"]), (br[:], row(w["br"], E)),
                      (b2[:], w["b2"]), (bs[:], row(w["bs"], D))]
        all_in = 16 * len(loads)
        start_semaphores(nc, sems, from_one)
        block = ctx.enter_context(nc.Block())

        @block.sync
        def _(sp):
            for dst, src in loads:
                sp.dma_start(dst, src).then_inc(weights_in, 16)

        @block.gpsimd
        def _(pool):
            pool.memset(cT[:], 0.0).then_inc(fixed, 1)
            pool.memset(cTb[:], 0.0).then_inc(fixed, 1)

        @block.scalar
        def _(act):
            norm_sqrt(act, g, sqrt_in, sqrt_out)
            act.wait_ge(weights_in, all_in)
            with act.Fori(0, B) as b:
                full(act, b, "xT")
                act.activation(xnT[:], GP[gp.bank["xT"]][:], ACT.Copy).then_inc(gp_read[gp.bank["xT"]], 1)
                act.wait_ge(logits_ready, b + 1)
                act.activation(ex[:], lg[:], ACT.Exp).then_inc(exp_ready, 1)
                for e in range(n_h):
                    i = e % 2
                    act.wait_ge(hb_full[i], hb.after(b, e))
                    act.wait_ge(hb_read[i], hb.before(b, e))
                    if gated:
                        act.activation(act_out[:, i], HB[i][:, 0], ACT.Silu, bias=b1[:, e:e + 1]).then_inc(act_ready[i], 1)
                    else:
                        act.activation(act_out[:, i], HB[i][:, 0], ACT.Relu).then_inc(act_ready[i], 1)

        @block.tensor
        def _(pe):
            pe.wait_ge(weights_in, all_in)
            pe.wait_ge(fixed, 2)
            with pe.Fori(0, B) as b:
                pe.wait_ge(xn_ready, b + 1)
                free(pe, b, "xT")
                transpose_xn(pe, g, xn, GP[gp.bank["xT"]]).then_inc(gp_full[gp.bank["xT"]], 1)
                read(pe, b, "xT")
                free(pe, b, "logits")
                for t in range(TT):
                    for k in range(KD):
                        op = pe.matmul(GP[gp.bank["logits"]][:, t, 0:E], xnT[:, k, t * P:(t + 1) * P], wr[:, k, :],
                                       start=(k == 0), stop=(k == KD - 1))
                op.then_inc(gp_full[gp.bank["logits"]], 1)

                def hidden(e):
                    i = e % 2
                    pe.wait_ge(hb_read[i], hb.before(b, e))
                    for x, wgt in enumerate((w1, w3) if gated else (w1,)):
                        for k in range(KD):
                            op = pe.matmul(HB[i][:, x], wgt[:, e, k, :], xnT[:, k, :], start=(k == 0), stop=(k == KD - 1))
                    op.then_inc(hb_full[i], 1)

                def spread(e):
                    i = cb.bank[e]
                    if e - 2 >= SH:
                        pe.wait_ge(h_ready[e % 2], hb.after(b, e - 2))
                    pe.matmul(CB[i][:, 0], sel[:, e - SH, :], cTb[:], start=True, stop=True).then_inc(cb_full[i], 1)

                def out(e):
                    i = e % 2
                    pe.wait_ge(h_ready[i], hb.after(b, e))
                    for t in range(TT):
                        op = pe.matmul(YB[t][:, 0], hT[:, i, t * P:(t + 1) * P], w2[:, e, :], start=(e == 0),
                                       stop=(e == n_h - 1))
                    op.then_inc(h_used[i], 1)

                hidden(0)
                hidden(1)
                pe.wait_ge(c_ready, b + 1)
                free(pe, b, "cT")
                for t in range(TT):
                    op = pe.transpose(GP[gp.bank["cT"]][0:E, 0, t * P:(t + 1) * P], c[:, t, :], g.ident[:])
                op.then_inc(gp_full[gp.bank["cT"]], 1)
                read(pe, b, "cT")
                for e in range(SH, 2):
                    spread(e)
                pe.wait_ge(y_read, b + 1)
                for e in range(2, n_h):
                    spread(e)
                    hidden(e)
                    out(e - 2)
                out(n_h - 2)
                out(n_h - 1)
                if gated:
                    for t in range(TT):
                        op = pe.matmul(YB[t][:, 0], cT[:, t * P:(t + 1) * P], b2[:], start=False, stop=True,
                                       skip_group_check=True)
                    op.then_inc(y_full, 1)

        @block.vector
        def _(dve):
            norm_factors(dve, g, sqrt_in, sqrt_out)
            dve.wait_ge(weights_in, all_in)
            dve.wait_ge(fixed, 2)
            wide = lambda a, n: a.rearrange("p (t a) -> p t a", a=1).broadcast_to([P, TT, n])
            with dve.Fori(0, B) as b:
                normalise(dve, g, b, xn, xn_ready)
                full(dve, b, "logits")
                src = GP[gp.bank["logits"]][:, :, 0:E]
                if gated:
                    dve.tensor_reduce(red[:, 0], src, AX.X, ALU.max)
                    dve.drain()
                    dve.tensor_tensor(lg[:], src, wide(red[:, 0], E), ALU.subtract).then_inc(gp_read[gp.bank["logits"]], 1)
                    dve.drain()
                    dve.sem_inc(logits_ready, 1)
                    dve.wait_ge(exp_ready, b + 1)
                    dve.tensor_reduce(red[:, 0], ex[:], AX.X, ALU.add)
                    dve.drain()
                    dve.reciprocal(red[:, 1], red[:, 0])
                    dve.drain()
                    dve.tensor_tensor(ex[:], ex[:], wide(red[:, 1], E), ALU.mult)
                    dve.drain()
                    dve.tensor_tensor(score[:], ex[:], br[:].rearrange("p (a n) -> p a n", a=1)
                                      .broadcast_to([P, TT, E]), ALU.add)
                    dve.drain()
                    sg = score[:].rearrange("p t (g e) -> p t g e", e=4)
                    dve.tensor_tensor(pairs[:, :, :, 0:3], sg[:, :, :, 0:3], sg[:, :, :, 1:4], ALU.add)
                    dve.tensor_tensor(pairs[:, :, :, 3:5], sg[:, :, :, 0:2], sg[:, :, :, 2:4], ALU.add)
                    dve.tensor_tensor(pairs[:, :, :, 5:6], sg[:, :, :, 0:1], sg[:, :, :, 3:4], ALU.add)
                    dve.drain()
                    dve.tensor_reduce(gs[:], pairs[:], AX.X, ALU.max)
                    dve.drain()
                    for t in range(TT):
                        top_rank(dve, grank, cmp[:, 0:4, 0:4], eq[:, 0:4, 0:4], gs, earlier[:, 0:4, 0:4], t, 4)
                    dve.tensor_scalar(grank[:], grank[:], 1.5, None, ALU.is_lt)
                    dve.drain()
                    dve.tensor_scalar(gs[:], grank[:], 1e30, -1e30, ALU.mult, ALU.add)
                    for t in range(TT):
                        dve.tensor_tensor(score[:, t].rearrange("p (g e) -> p g e", e=4),
                                          score[:, t].rearrange("p (g e) -> p g e", e=4),
                                          grank[:, t].rearrange("p (g a) -> p g a", a=1).broadcast_to([P, 4, 4]), ALU.mult)
                    dve.drain()
                    for t in range(TT):
                        dve.tensor_tensor(score[:, t].rearrange("p (g e) -> p g e", e=4),
                                          score[:, t].rearrange("p (g e) -> p g e", e=4),
                                          gs[:, t].rearrange("p (g a) -> p g a", a=1).broadcast_to([P, 4, 4]), ALU.add)
                    dve.drain()
                    for t in range(TT):
                        top_rank(dve, rank, cmp[:], eq[:], score, earlier[:], t, E)
                    dve.tensor_scalar(rank[:], rank[:], 1.5, None, ALU.is_lt)
                    dve.drain()
                    dve.tensor_tensor(c[:], rank[:], ex[:], ALU.mult).then_inc(c_ready, 1)
                else:
                    dve.tensor_copy(score[:], src).then_inc(gp_read[gp.bank["logits"]], 1)
                    dve.drain()
                    for t in range(TT):
                        dve.max(top[:, t, :], score[:, t, :])
                    dve.drain()
                    dve.tensor_tensor(lg[:], top[:], top[:, :, 0:1].broadcast_to([P, TT, 8]), ALU.subtract)
                    dve.drain()
                    dve.sem_inc(logits_ready, 1)
                    dve.wait_ge(exp_ready, b + 1)
                    dve.tensor_scalar(red[:, 0], ex[:, :, 1], 1.0, None, ALU.add)
                    dve.drain()
                    dve.reciprocal(red[:, 1], red[:, 0])
                    dve.drain()
                    dve.tensor_scalar(red[:, 1], red[:, 1], 1.0, None, ALU.is_ge)
                    dve.tensor_tensor(c[:], score[:], top[:, :, 0:1].broadcast_to([P, TT, 8]), ALU.is_ge)
                    dve.drain()
                    dve.tensor_tensor(c[:], c[:], wide(red[:, 1], E), ALU.mult).then_inc(c_ready, 1)

                def hidden(e, routed):
                    i = e % 2
                    dve.wait_ge(act_ready[i], hb.after(b, e))
                    dve.wait_ge(h_used[i], hb.before(b, e))
                    dst = hc[:, i] if routed else hT[:, i]
                    if gated:
                        op = dve.scalar_tensor_tensor(out=dst, in0=HB[i][:, 1], scalar=b3[:, e:e + 1],
                                                      in1=act_out[:, i], op0=ALU.add, op1=ALU.mult)
                    else:
                        op = dve.scalar_tensor_tensor(out=dst, in0=HB[i][:, 0], scalar=0.0,
                                                      in1=act_out[:, i], op0=ALU.max, op1=ALU.mult)
                    op.then_inc(hb_read[i], 1)
                    if not routed:
                        dve.drain()
                        dve.sem_inc(h_ready[i], 1)
                        return
                    dve.drain()
                    dve.wait_ge(cb_full[cb.bank[e]], cb.after(b, e))
                    dve.tensor_tensor(hT[:, i], hc[:, i], CB[cb.bank[e]][:, 0], ALU.mult).then_inc(h_ready[i], 1)

                full(dve, b, "cT")
                src = GP[gp.bank["cT"]][0:E, 0, :]
                dve.tensor_copy(cT[0:E, :], src)
                dve.tensor_copy(cTb[0:E, :], src)
                dve.drain()
                dve.tensor_tensor(rest[:], src, cTb[0:E, :], ALU.subtract)
                dve.drain()
                dve.tensor_copy(cTb[32:32 + E, :], rest[:])
                dve.drain()
                dve.tensor_tensor(cTb[64:64 + E, :], rest[:], cTb[32:32 + E, :], ALU.subtract)\
                   .then_inc(gp_read[gp.bank["cT"]], 1)
                for e in range(n_h):
                    hidden(e, e >= SH)
                if gated:
                    dve.wait_ge(y_full, b + 1)
                else:
                    dve.wait_ge(h_used[(n_h - 1) % 2], hb.after(b, n_h - 1))
                for t in range(TT):
                    if gated:
                        op = dve.tensor_tensor(yt[:, t], YB[t][:, 0], bs[:], ALU.add)
                    else:
                        op = dve.tensor_copy(yt[:, t], YB[t][:, 0])
                op.then_inc(y_read, 1)
                dve.drain()
                add_to_x(dve, g, b, yt[:])
                dve.drain()
                next_stats(dve, g, b)
                dve.drain()


def pick_two(dve, s, descending, tmp, red, picked):
    wide = lambda a: a.rearrange("p (t a) -> p t a", a=1).broadcast_to(list(s.shape))
    order = descending.rearrange("p (a n) -> p a n", a=1).broadcast_to(list(s.shape))
    for r in range(2):
        dve.tensor_reduce(red[:, 0], s, AX.X, ALU.max)
        dve.drain()
        dve.tensor_tensor(tmp, s, wide(red[:, 0]), ALU.is_ge)
        dve.drain()
        dve.tensor_tensor(tmp, tmp, order, ALU.mult)
        dve.drain()
        dve.tensor_reduce(red[:, 1], tmp, AX.X, ALU.max)
        dve.drain()
        dve.tensor_tensor(picked[r], tmp, wide(red[:, 1]), ALU.is_equal)
        dve.drain()
        if r == 0:
            dve.scalar_tensor_tensor(out=s, in0=picked[0], scalar=-3e38, in1=s, op0=ALU.mult, op1=ALU.add)
            dve.drain()


def sorted_gated_experts(nc, g, name, w):
    io = g.io
    E, G, SH = 16, 4, 2
    NS = 48
    U = 4
    PAIRS = U // 2
    ST = NT
    with ExitStack() as ctx:
        sb = lambda n, s, t=F32: ctx.enter_context(nc.sbuf_tensor(f"{name}_sb_{n}", s, t))
        sems, from_one = [], []

        def sem(n, one=False):
            s = ctx.enter_context(nc.semaphore(f"{name}_{n}"))
            (from_one if one else sems).append(s)
            return s
        x_slots = nc.dram_tensor(f"{name}_x_slots", (NS * P, D), F32).ap()
        y_slots = nc.dram_tensor(f"{name}_y_slots", (NS * P, D), F32).ap()
        wr, br = sb("wr", [P, KD, E]), sb("br", [P, E])
        w13 = sb("w13", [P, E, KD, 2 * P])
        w2 = sb("w2", [P, E, D])
        b13, b2 = sb("b13", [P, E, 2 * P]), sb("b2", [P, E, D])
        ws13 = sb("ws13", [P, SH, 2, KD, P])
        ws2 = sb("ws2", [P, SH, D])
        bs1, bs3, bs2 = sb("bs1", [P, SH]), sb("bs3", [P, SH]), sb("bs2", [P, D])
        before_p, ones = sb("before_p", [P, P]), sb("ones", [P, P])
        earlier = sb("earlier", [P, E, E])
        descending = sb("descending", [P, E])
        steps = sb("steps", [P, ST])
        zero = sb("zero", [P, D])
        xn = sb("xn", [P, NT, D])
        xnT = sb("xnT", [P, KD, B * S])
        rows = [xn[:], xnT[:].rearrange("p k s -> p (k s)").rearrange("p (t d) -> p t d", d=D)]
        lg, ex, score, tmp = (sb(n, [P, NT, E]) for n in ("lg", "ex", "score", "tmp"))
        red, red2 = sb("red", [P, 2, NT]), sb("red2", [P, 2, NT * G])
        pairs = sb("pairs", [P, NT * G, 6])
        gs, gtmp, keep = sb("gs", [P, NT, G]), sb("gtmp", [P, NT, G]), sb("keep", [P, 2, NT, G])
        picked = sb("picked", [P, 2, NT, E])
        both = sb("both", [P, NT, E])
        weight = sb("weight", [P, 2, NT])
        pre, tot, run = sb("pre", [P, NT, E]), sb("tot", [P, NT, E]), sb("run", [P, 2, NT, E])
        tiles = sb("tiles", [P, 3, E])
        cmp2, cmp3, cmp4 = sb("cmp2", [P, E, ST]), sb("cmp3", [P, NS, E]), sb("cmp4", [P, E, E])
        posf = sb("posf", [P, 2, NT])
        pos = sb("pos", [P, 2, NT], mybir.dt.int32)
        slotf, slot = sb("slotf", [P, NS]), sb("slot", [P, NS], mybir.dt.int32)
        s_act, s_lin, s_hT = sb("s_act", [P, SH, S]), sb("s_lin", [P, SH, S]), sb("s_hT", [P, SH, S])
        s_y = sb("s_y", [P, TT, D])
        xs, xsT = sb("xs", [P, U, D]), sb("xsT", [P, U, KD * P])
        hb, ha, hm, hmT = sb("hb", [P, U, 2 * P]), sb("ha", [P, U, P]), sb("hm", [P, U, P]), sb("hmT", [P, U, P])
        ys = sb("ys", [P, U, D])
        ps = lambda n: ctx.enter_context(nc.psum_tensor(f"{name}_{n}", [P, 2, S], F32))
        GP, HB, YB = [ps("gp0"), ps("gp1")], [ps("hb0"), ps("hb1")], [ps("yb0"), ps("yb1")]
        HT = LG, CT = ps("lg"), ps("ct")

        router_in, shared_in, experts_in = sem("router_in"), sem("shared_in"), sem("experts_in")
        sqrt_in, sqrt_out, fixed, cleared = sem("sqrt_in"), sem("sqrt_out"), sem("fixed"), sem("cleared")
        xn_ready, xn_turned, xnT_ready = sem("xn_ready"), sem("xn_turned"), sem("xnT_ready")
        logits_full, shifted, exp_ready = sem("logits_full"), sem("shifted"), sem("exp_ready")
        both_ready, counted, routed = sem("both_ready"), sem("counted"), sem("routed")
        s_full = [sem(f"s_full{e}") for e in range(SH)]
        s_evacuated = [sem(f"s_evacuated{e}", one=True) for e in range(SH)]
        s_product = [sem(f"s_product{e}", one=True) for e in range(SH)]
        s_y_full, s_y_copied, s_y_added = (sem("s_y_full", one=True), sem("s_y_copied", one=True),
                                           sem("s_y_added", one=True))
        scattered, gathered = g.moved[0][0], g.moved[0][1:]
        each = lambda n, one=False: [sem(f"{n}{q}", one) for q in range(PAIRS)]
        x_in, xT_ready, h_full, h_biased, h_act, h_ready, hT_full, hT_ready, y_full = (
            each(n) for n in ("x_in", "xT_ready", "h_full", "h_biased", "h_act", "h_ready", "hT_full", "hT_ready",
                              "y_full"))
        turned, y_ready, y_stored = (each(n, one=True) for n in ("turned", "y_ready", "y_stored"))
        start_semaphores(nc, sems, from_one)
        block = ctx.enter_context(nc.Block())
        row = lambda a, n: a.rearrange("(a n) -> a n", a=1).broadcast_to([P, n])
        table = lambda a: a.rearrange("(a e) n -> a e n", a=1).broadcast_to([P, E, 2 * P])
        slots = lambda a, i, q: a[bass.ds((i * U + 2 * q) * P, 2 * P), :].rearrange("(j p) d -> p j d", p=P)

        @block.sync
        def _(sp):
            for dst, src in ((wr, w["wr"].rearrange("(k p) n -> p k n", p=P)), (br, row(w["br"], E)),
                             (before_p, io["c_before"]), (descending, io["c_descending"]),
                             (earlier, io["c_earlier"]), (steps, io["c_steps"][:, 0:ST])):
                sp.dma_start(dst[:], src).then_inc(router_in, 16)
            for dst, src in ((ws13, w["ws13"]), (ws2, w["ws2"]), (bs1, w["bs1"]), (bs3, w["bs3"]),
                             (bs2, row(w["bs2"], D))):
                sp.dma_start(dst[:], src).then_inc(shared_in, 16)
            sp.wait_ge(fixed, 1)
            sp.dma_start(x_slots.rearrange("(n p) d -> p n d", p=P),
                         zero[:].rearrange("p (a d) -> p a d", a=1).broadcast_to([P, NS, D])).then_inc(cleared, 16)
            for dst, src in ((w13, w["w13"]), (w2, w["w2"]), (b13, table(w["b13"])), (b2, table(w["b2"]))):
                sp.dma_start(dst[:], src).then_inc(experts_in, 16)
            sp.wait_ge(scattered, 16 * 2 * NT)
            with sp.Fori(0, NS // U) as i:
                for q in range(PAIRS):
                    sp.wait_ge(turned[q], i + 1)
                    sp.dma_start(xs[:, 2 * q:2 * q + 2, :], slots(x_slots, i, q)).then_inc(x_in[q], 16)

        @block.gpsimd
        def _(pool):
            pool.memset(zero[:], 0.0).then_inc(fixed, 1)
            pool.memset(ones[:], 1.0).then_inc(fixed, 1)
            with pool.Fori(0, B) as b:
                for e in range(SH):
                    pool.wait_ge(s_evacuated[e], b + 2)
                    pool.wait_ge(s_y_full, b + 1)
                    pool.tensor_tensor(s_hT[:, e], s_act[:, e], s_lin[:, e], ALU.mult).then_inc(s_product[e], 1)
                pool.wait_ge(s_y_copied, b + 2)
                xb = g.x[:, bass.ds(b * TT, TT), :]
                pool.tensor_tensor(xb, xb, s_y[:], ALU.add).then_inc(s_y_added, 1)
            pool.wait_ge(cleared, 16)
            pool.wait_ge(routed, 1)
            for i in range(2):
                for t in range(NT):
                    pool.indirect_dma_start(x_slots, bass.IndirectOffsetOnAxis(pos[:, i, t:t + 1], 0), xn[:, t, :], None)\
                        .then_inc(scattered, 16)
            for q in range(PAIRS):
                pool.wait_ge(y_stored[q], 16 * (NS // U) + 1)
            for half_ in range(2):
                for t in range(half_ * NT // 2, (half_ + 1) * NT // 2):
                    for i in range(2):
                        pool.indirect_dma_start(rows[i][:, t, :], None, y_slots,
                                                bass.IndirectOffsetOnAxis(pos[:, i, t:t + 1], 0))\
                            .then_inc(gathered[half_], 16)

        @block.scalar
        def _(act):
            norm_sqrt(act, g, sqrt_in, sqrt_out)
            for b in range(B):
                act.wait_ge(xn_turned, b + 1)
                act.activation(xnT[:, :, b * S:(b + 1) * S], GP[b % 2][:], ACT.Copy).then_inc(xnT_ready, 1)
            act.wait_ge(shifted, 1)
            act.activation(ex[:], lg[:], ACT.Exp).then_inc(exp_ready, 1)
            act.wait_ge(shared_in, 16 * 5)
            with act.Fori(0, B) as b:
                for e in range(SH):
                    act.wait_ge(s_full[e], b + 1)
                    act.wait_ge(s_product[e], b + 1)
                    act.activation(s_act[:, e], HB[e][:, 0], ACT.Silu, bias=bs1[:, e:e + 1])
                    act.activation(s_lin[:, e], HB[e][:, 1], ACT.Identity, bias=bs3[:, e:e + 1])\
                       .then_inc(s_evacuated[e], 1)
                act.wait_ge(s_y_full, b + 2)
                act.wait_ge(s_y_added, b + 1)
                for t in range(TT):
                    op = act.activation(s_y[:, t], YB[t][:, 0], ACT.Copy)
                op.then_inc(s_y_copied, 1)
            with act.Fori(0, NS // U) as i:
                for q in range(PAIRS):
                    act.wait_ge(turned[q], i + 2)
                    act.activation(xsT[:, 2 * q:2 * q + 2], GP[q][:], ACT.Copy).then_inc(xT_ready[q], 1)
                for q in range(PAIRS):
                    act.wait_ge(h_biased[q], i + 1)
                    act.activation(ha[:, 2 * q:2 * q + 2], hb[:, 2 * q:2 * q + 2, 0:P], ACT.Silu).then_inc(h_act[q], 1)
                for q in range(PAIRS):
                    act.wait_ge(hT_full[q], i + 1)
                    act.activation(hmT[:, 2 * q:2 * q + 2], HT[q][:, 0, :].rearrange("p (j n) -> p j n", n=P), ACT.Copy)\
                       .then_inc(hT_ready[q], 1)
                for q in range(PAIRS):
                    act.wait_ge(y_ready[q], i + 2)
                    act.dma_start(slots(y_slots, i, q), ys[:, 2 * q:2 * q + 2, :]).then_inc(y_stored[q], 16)

        @block.tensor
        def _(pe):
            pe.wait_ge(router_in, 16 * 6)
            logits = LG[:].rearrange("p a n -> p (a n)")
            for b in range(B + 1):
                if b < B:
                    pe.wait_ge(xn_ready, b + 1)
                    if b >= 2:
                        pe.wait_ge(xnT_ready, b - 1)
                    transpose_xn(pe, g, xn[:, b * TT:(b + 1) * TT, :], GP[b % 2]).then_inc(xn_turned, 1)
                if b:
                    pe.wait_ge(xnT_ready, b)
                    for t in range((b - 1) * TT, b * TT):
                        for k in range(KD):
                            op = pe.matmul(logits[:, t * E:(t + 1) * E], xnT[:, k, t * P:(t + 1) * P], wr[:, k, :],
                                           start=(k == 0), stop=(k == KD - 1))
            op.then_inc(logits_full, 1)
            pe.wait_ge(shared_in, 16 * 5)

            def shared(b):
                for e in range(SH):
                    pe.wait_ge(s_evacuated[e], b + 1)
                    for x in range(2):
                        for k in range(KD):
                            op = pe.matmul(HB[e][:, x], ws13[:, e, x, k, :], xnT[:, k, bass.ds(b * S, S)],
                                           start=(k == 0), stop=(k == KD - 1))
                    op.then_inc(s_full[e], 1)
                pe.wait_ge(s_y_copied, b + 1)
                for e in range(SH):
                    pe.wait_ge(s_product[e], b + 2)
                    for t in range(TT):
                        op = pe.matmul(YB[t][:, 0], s_hT[:, e, t * P:(t + 1) * P], ws2[:, e, :],
                                       start=(e == 0), stop=(e == SH - 1))
                op.then_inc(s_y_full, 1)

            with pe.Fori(0, B // 2) as b:
                shared(b)
            pe.wait_ge(both_ready, 1)
            pe.wait_ge(fixed, 2)
            flat = both[:].rearrange("p t e -> p (t e)")
            pe.matmul(CT[:, 0, :], before_p[:], flat, start=True, stop=True)
            pe.matmul(CT[:, 1, :], ones[:], flat, start=True, stop=True).then_inc(counted, 1)
            with pe.Fori(B // 2, B) as b:
                shared(b)
            pe.wait_ge(s_y_copied, B + 1)
            pe.wait_ge(experts_in, 16 * 4)
            pe.wait_ge(routed, 1)
            with pe.Fori(0, NS // U) as i:
                e = [pe.value_load(slot[0:1, bass.ds(i * U + j, 1)], min_val=0, max_val=E - 1) for j in range(U)]
                for q in range(PAIRS):
                    pe.wait_ge(x_in[q], i * 16 + 16)
                    for j in range(2):
                        for k in range(KD):
                            op = pe.transpose(GP[q][:, j, k * P:(k + 1) * P], xs[:, 2 * q + j, k * P:(k + 1) * P], g.ident[:])
                    op.then_inc(turned[q], 1)
                for q in range(PAIRS):
                    pe.wait_ge(xT_ready[q], i + 1)
                    for j in range(2):
                        for k in range(KD):
                            op = pe.matmul(HB[q][:, j], xsT[:, 2 * q + j, k * P:(k + 1) * P],
                                           w13[:, bass.ds(e[2 * q + j], 1), k, :].rearrange("p a n -> p (a n)"),
                                           start=(k == 0), stop=(k == KD - 1))
                    op.then_inc(h_full[q], 1)
                for q in range(PAIRS):
                    pe.wait_ge(h_ready[q], i + 1)
                    for j in range(2):
                        op = pe.transpose(HT[q][:, 0, j * P:(j + 1) * P], hm[:, 2 * q + j], g.ident[:])
                    op.then_inc(hT_full[q], 1)
                for q in range(PAIRS):
                    pe.wait_ge(hT_ready[q], i + 1)
                    pe.wait_ge(y_ready[q], i + 1)
                    for j in range(2):
                        op = pe.matmul(YB[q][:, j], hmT[:, 2 * q + j],
                                       w2[:, bass.ds(e[2 * q + j], 1), :].rearrange("p a n -> p (a n)"),
                                       start=True, stop=True)
                    op.then_inc(y_full[q], 1)

        @block.vector
        def _(dve):
            wide = lambda a, n: a.rearrange("p (t a) -> p t a", a=1).broadcast_to([P, NT, n])
            norm_factors(dve, g, sqrt_in, sqrt_out)
            for t in range(NT):
                op = dve.tensor_scalar(xn[:, t, :], g.x[:, t, :], g.mean[:, t:t + 1], g.rstd[:, t:t + 1],
                                       ALU.subtract, ALU.mult)
                if t % TT == TT - 1:
                    op.then_inc(xn_ready, 1)
            dve.wait_ge(router_in, 16 * 6)
            dve.wait_ge(logits_full, 1)
            src = LG[:].rearrange("p a n -> p (a n)")[:, 0:NT * E].rearrange("p (t e) -> p t e", e=E)
            dve.tensor_reduce(red[:, 0], src, AX.X, ALU.max)
            dve.drain()
            dve.tensor_tensor(lg[:], src, wide(red[:, 0], E), ALU.subtract).then_inc(shifted, 1)
            dve.wait_ge(exp_ready, 1)
            dve.tensor_reduce(red[:, 0], ex[:], AX.X, ALU.add)
            dve.drain()
            dve.reciprocal(red[:, 1], red[:, 0])
            dve.drain()
            dve.tensor_tensor(ex[:], ex[:], wide(red[:, 1], E), ALU.mult)
            dve.drain()
            dve.tensor_tensor(score[:], ex[:], br[:].rearrange("p (a n) -> p a n", a=1).broadcast_to([P, NT, E]), ALU.add)
            dve.drain()
            per_group = E // G
            sg = score[:].rearrange("p t (g e) -> p (t g) e", e=per_group)
            dve.tensor_tensor(pairs[:, :, 0:3], sg[:, :, 0:3], sg[:, :, 1:4], ALU.add)
            dve.tensor_tensor(pairs[:, :, 3:5], sg[:, :, 0:2], sg[:, :, 2:4], ALU.add)
            dve.tensor_tensor(pairs[:, :, 5:6], sg[:, :, 0:1], sg[:, :, 3:4], ALU.add)
            dve.drain()
            dve.tensor_reduce(gs[:].rearrange("p t g -> p (t g)"), pairs[:], AX.X, ALU.max)
            dve.drain()
            pick_two(dve, gs[:], descending[:, 0:G], gtmp[:], red, [keep[:, 0], keep[:, 1]])
            dve.tensor_tensor(gs[:], keep[:, 0], keep[:, 1], ALU.add)
            dve.drain()
            dve.tensor_scalar(gtmp[:], gs[:], 1e30, -1e30, ALU.mult, ALU.add)
            over = lambda a: a.rearrange("p t (g a) -> p (t g) a", a=1).broadcast_to([P, NT * G, per_group])
            dve.tensor_tensor(sg, sg, over(gs[:]), ALU.mult)
            dve.drain()
            dve.tensor_tensor(sg, sg, over(gtmp[:]), ALU.add)
            dve.drain()
            pick_two(dve, score[:], descending[:], tmp[:], red, [picked[:, 0], picked[:, 1]])
            dve.tensor_tensor(both[:], picked[:, 0], picked[:, 1], ALU.add).then_inc(both_ready, 1)
            for i in range(2):
                dve.tensor_tensor(tmp[:], picked[:, i], ex[:], ALU.mult)
                dve.drain()
                dve.tensor_reduce(weight[:, i], tmp[:], AX.X, ALU.add)
                dve.drain()
            dve.wait_ge(counted, 1)
            counts = [CT[:, i, :].rearrange("p (t e) -> p t e", e=E) for i in range(2)]
            dve.tensor_copy(pre[:], counts[0])
            dve.tensor_copy(tot[:], counts[1])
            dve.tensor_copy(run[:, 0], counts[1])
            dve.drain()
            a, d = 0, 1
            while d < NT:
                dve.tensor_copy(run[:, 1 - a, 0:d], run[:, a, 0:d])
                dve.tensor_tensor(run[:, 1 - a, d:NT], run[:, a, d:NT], run[:, a, 0:NT - d], ALU.add)
                dve.drain()
                a, d = 1 - a, 2 * d
            dve.tensor_tensor(pre[:], pre[:], tot[:], ALU.subtract)
            dve.tensor_tensor(cmp2[:], steps[:].rearrange("p (a n) -> p a n", a=1).broadcast_to([P, E, ST]),
                              run[:, a, NT - 1, :].rearrange("p (e a) -> p e a", a=1).broadcast_to([P, E, ST]), ALU.is_lt)
            dve.drain()
            dve.tensor_tensor(pre[:], pre[:], run[:, a], ALU.add)
            dve.tensor_reduce(tiles[:, 0], cmp2[:], AX.X, ALU.add)
            dve.drain()
            dve.tensor_tensor(cmp4[:], tiles[:, 0:1, :].broadcast_to([P, E, E]), earlier[:], ALU.mult)
            dve.drain()
            dve.tensor_reduce(tiles[:, 1], cmp4[:], AX.X, ALU.add)
            dve.drain()
            dve.tensor_scalar(tiles[:, 2], tiles[:, 1], float(P), None, ALU.mult)
            dve.tensor_tensor(tiles[:, 0], tiles[:, 0], tiles[:, 1], ALU.add)
            dve.drain()
            dve.tensor_tensor(pre[:], pre[:], tiles[:, 2:3, :].broadcast_to([P, NT, E]), ALU.add)
            dve.drain()
            for i in range(2):
                dve.tensor_tensor(picked[:, i], pre[:], picked[:, i], ALU.mult)
            dve.drain()
            for i in range(2):
                dve.tensor_reduce(posf[:, i], picked[:, i], AX.X, ALU.add)
            for sl in range(NS):
                dve.tensor_scalar(cmp3[:, sl, :], tiles[:, 0, :], float(sl), None, ALU.is_le)
            dve.drain()
            dve.tensor_copy(pos[:], posf[:])
            dve.tensor_reduce(slotf[:], cmp3[:], AX.X, ALU.add)
            dve.drain()
            dve.tensor_scalar(slotf[:], slotf[:], float(E - 1), None, ALU.min)
            dve.drain()
            dve.tensor_copy(slot[:], slotf[:]).then_inc(routed, 1)
            dve.wait_ge(s_y_added, B + 1)
            dve.wait_ge(shared_in, 16 * 5)
            dve.tensor_tensor(g.x[:], g.x[:], bs2[:].rearrange("p (a n) -> p a n", a=1).broadcast_to([P, NT, D]), ALU.add)
            dve.wait_ge(experts_in, 16 * 4)
            dve.drain()
            with dve.Fori(0, NS // U) as i:
                e = [dve.value_load(slot[0:1, bass.ds(i * U + j, 1)], min_val=0, max_val=E - 1) for j in range(U)]
                of = lambda table_, j: table_[:, bass.ds(e[j], 1), :].rearrange("p a n -> p (a n)")
                for q in range(PAIRS):
                    dve.wait_ge(h_full[q], i + 1)
                    for j in range(2):
                        op = dve.tensor_tensor(hb[:, 2 * q + j], HB[q][:, j], of(b13, 2 * q + j), ALU.add)
                    op.then_inc(h_biased[q], 1)
                dve.drain()
                for q in range(PAIRS):
                    dve.wait_ge(h_act[q], i + 1)
                    dve.tensor_tensor(hm[:, 2 * q:2 * q + 2], ha[:, 2 * q:2 * q + 2], hb[:, 2 * q:2 * q + 2, P:2 * P],
                                      ALU.mult).then_inc(h_ready[q], 1)
                for q in range(PAIRS):
                    dve.wait_ge(y_full[q], i + 1)
                    dve.wait_ge(y_stored[q], i * 16 + 1)
                    for j in range(2):
                        op = dve.tensor_tensor(ys[:, 2 * q + j], YB[q][:, j], of(b2, 2 * q + j), ALU.add)
                    op.then_inc(y_ready[q], 1)
                dve.drain()
            for h in range(2):
                dve.wait_ge(gathered[h], 16 * NT)
                for t in range(h * NT // 2, (h + 1) * NT // 2):
                    for i in range(2):
                        dve.scalar_tensor_tensor(out=g.x[:, t, :], in0=rows[i][:, t, :], scalar=weight[:, i, t:t + 1],
                                                 in1=g.x[:, t, :], op0=ALU.mult, op1=ALU.add)
                        dve.drain()
                    dve.bn_stats(g.stats[:, t, :], g.x[:, t, :])
            dve.drain()


def sorted_experts(nc, g, name, w):
    io = g.io
    E, F = 8, 1024
    FC = F // P
    NS = 24
    U = 4
    WROW = KD * F + FC * D + FC
    with ExitStack() as ctx:
        sb = lambda n, s, t=F32: ctx.enter_context(nc.sbuf_tensor(f"{name}_sb_{n}", s, t))
        sems, from_one = [], []

        def sem(n, one=False):
            s = ctx.enter_context(nc.semaphore(f"{name}_{n}"))
            (from_one if one else sems).append(s)
            return s
        x_slots = nc.dram_tensor(f"{name}_x_slots", (NS * P, D), F32).ap()
        y_slots = nc.dram_tensor(f"{name}_y_slots", (NS * P, D), F32).ap()
        wr = sb("wr", [P, KD, E])
        br = sb("br", [P, E])
        before_p = sb("before_p", [P, P])
        ones = sb("ones", [P, P])
        earlier = sb("earlier", [P, H, H])
        steps = sb("steps", [P, NS])
        xn = sb("xn", [P, TT, D])
        xnT = sb("xnT", [P, KD, S])
        lg = sb("lg", [P, NT, E])
        sc = sb("sc", [P, NT, E])
        red = sb("red", [P, NT])
        cmp, eq = sb("cmp", [P, NT, E, E]), sb("eq", [P, NT, E, E])
        rank = sb("rank", [P, NT, E])
        win = sb("win", [P, NT, E])
        pre = sb("pre", [P, NT, E])
        tot = sb("tot", [P, NT, E])
        run = sb("run", [P, 2, NT, E])
        tiles = sb("tiles", [P, 3, E])
        cmp2 = sb("cmp2", [P, E, NT])
        cmp3 = sb("cmp3", [P, NS, E])
        cmp4 = sb("cmp4", [P, E, E])
        posf = sb("posf", [P, NT])
        pos = sb("pos", [P, NT], mybir.dt.int32)
        slotf = sb("slotf", [P, NS])
        slot = sb("slot", [P, NS], mybir.dt.int32)
        rw = sb("rw", [P, NT])
        rows = sb("rows", [P, NT, D])
        zero = sb("zero", [P, D])
        wb = sb("wb", [P, U, WROW])
        b2 = sb("b2", [P, U, D])
        xs = sb("xs", [P, U, D])
        xsT = sb("xsT", [P, U, KD, P])
        hT = sb("hT", [P, U, FC, P])
        ys = sb("ys", [P, U, D])
        GP = [ctx.enter_context(nc.psum_tensor(f"{name}_gp{i}", [P, 2, S], F32)) for i in range(2)]
        HB = [[ctx.enter_context(nc.psum_tensor(f"{name}_hb{j}{i}", [P, FC // 2, P], F32)) for i in range(2)]
              for j in range(2)]
        YB = [ctx.enter_context(nc.psum_tensor(f"{name}_yb{j}", [P, 2, S], F32)) for j in range(2)]

        weights_in, sqrt_in, sqrt_out = sem("weights_in"), sem("sqrt_in"), sem("sqrt_out")
        fixed, cleared = sem("fixed"), sem("cleared")
        xn_ready, xn_turned, xnT_ready = sem("xn_ready"), sem("xn_turned", one=True), sem("xnT_ready")
        logits_full, logits_read = sem("logits_full"), sem("logits_read", one=True)
        shifted, exp_ready = sem("shifted"), sem("exp_ready")
        win_ready, counted = sem("win_ready"), sem("counted")
        slots_known, rows_ready = sem("slots_known"), sem("rows_ready")
        scattered, gathered = g.moved[1][0], g.moved[1][1:]
        each = lambda n, one=False: [sem(f"{n}{j}", one) for j in range(U)]
        w_in, x_in, xT_ready, h_full, h_act, h_dve, y_full = (
            each(n) for n in ("w_in", "x_in", "xT_ready", "h_full", "h_act", "h_dve", "y_full"))
        turned, y_ready, y_stored = (each(n, one=True) for n in ("turned", "y_ready", "y_stored"))
        start_semaphores(nc, sems, from_one)
        block = ctx.enter_context(nc.Block())
        w1 = lambda j, k, c: wb[:, j, k * F + c * P:k * F + (c + 1) * P]
        w2 = lambda j, c: wb[:, j, KD * F + c * D:KD * F + (c + 1) * D]
        b1 = lambda j, c: wb[:, j, KD * F + FC * D + c:KD * F + FC * D + c + 1]

        @block.sync
        def _(sp):
            for dst, src in ((wr, w["wr"].rearrange("(k p) n -> p k n", p=P)),
                             (br, w["br"].rearrange("(a n) -> a n", a=1).broadcast_to([P, E])),
                             (before_p, io["c_before"]), (earlier, io["c_earlier"]), (steps, io["c_steps"])):
                sp.dma_start(dst[:], src).then_inc(weights_in, 16)
            sp.wait_ge(fixed, 2)
            for i in range(NS):
                sp.dma_start(x_slots[i * P:(i + 1) * P, :], zero[:]).then_inc(cleared, 16)
            sp.wait_ge(slots_known, 1)
            with sp.Fori(0, NS // U) as i:
                for j in range(U):
                    e = sp.value_load(slot[0:1, bass.ds(U * i + j, 1)], min_val=0, max_val=E - 1)
                    sp.wait_ge(y_ready[j], i + 1)
                    sp.dma_start(wb[:, j, :], w["w"][bass.ds(e, 1), :, :].rearrange("a p n -> p (a n)"))\
                      .then_inc(w_in[j], 16)
                    sp.dma_start(b2[:, j, :], w["b2"][bass.ds(e, 1), :].broadcast_to([P, D])).then_inc(w_in[j], 16)
                    sp.wait_ge(scattered, 16 * NT)
                    sp.wait_ge(turned[j], i + 1)
                    sp.dma_start(xs[:, j, :], x_slots[bass.ds((U * i + j) * P, P), :]).then_inc(x_in[j], 16)

        @block.gpsimd
        def _(pool):
            pool.memset(ones[:], 1.0).then_inc(fixed, 1)
            pool.memset(zero[:], 0.0).then_inc(fixed, 1)
            pool.wait_ge(cleared, 16 * NS)
            for t in range(NT):
                pool.wait_ge(rows_ready, t + 1)
                pool.indirect_dma_start(x_slots, bass.IndirectOffsetOnAxis(pos[:, t:t + 1], 0), rows[:, t, :], None)\
                    .then_inc(scattered, 16)
            for j in range(U):
                pool.wait_ge(y_stored[j], 16 * (NS // U) + 1)
            pool.wait_ge(scattered, 16 * NT)
            for t in range(NT):
                pool.indirect_dma_start(rows[:, t, :], None, y_slots, bass.IndirectOffsetOnAxis(pos[:, t:t + 1], 0))\
                    .then_inc(gathered[2 * t // NT], 16)

        @block.scalar
        def _(act):
            norm_sqrt(act, g, sqrt_in, sqrt_out)
            with act.Fori(0, B) as b:
                act.wait_ge(xn_turned, b + 2)
                act.activation(xnT[:], GP[0][:], ACT.Copy).then_inc(xnT_ready, 1)
            act.wait_ge(shifted, 1)
            act.activation(sc[:], lg[:], ACT.Exp).then_inc(exp_ready, 1)
            with act.Fori(0, NS // U) as i:
                for pair in ((0, 1), (2, 3)):
                    for j in pair:
                        act.wait_ge(turned[j], i + 2)
                        act.activation(xsT[:, j], GP[j % 2][:, :, 0:P], ACT.Copy).then_inc(xT_ready[j], 1)
                    for j in pair:
                        act.wait_ge(h_full[j], i + 1)
                        for c in range(FC // 2):
                            op = act.activation(hT[:, j, c, :], HB[j % 2][0][:, c, :], ACT.Relu, bias=b1(j, c))
                        op.then_inc(h_act[j], 1)
                    for j in pair:
                        act.wait_ge(y_ready[j], i + 2)
                        act.dma_start(y_slots[bass.ds((U * i + j) * P, P), :], ys[:, j, :]).then_inc(y_stored[j], 16)

        @block.tensor
        def _(pe):
            pe.wait_ge(weights_in, 16 * 5)
            with pe.Fori(0, B) as b:
                pe.wait_ge(xn_ready, b + 1)
                transpose_xn(pe, g, xn, GP[0]).then_inc(xn_turned, 1)
                pe.wait_ge(xnT_ready, b + 1)
                pe.wait_ge(logits_read, b + 1)
                for t in range(TT):
                    for k in range(KD):
                        op = pe.matmul(GP[1][:, t, 0:E], xnT[:, k, t * P:(t + 1) * P], wr[:, k, :],
                                       start=(k == 0), stop=(k == KD - 1))
                op.then_inc(logits_full, 1)
            pe.wait_ge(win_ready, 1)
            pe.wait_ge(fixed, 2)
            flat = win[:].rearrange("p t e -> p (t e)")
            pe.matmul(HB[0][0][:, 0, :], before_p[:], flat, start=True, stop=True)
            pe.matmul(HB[0][1][:, 0, :], ones[:], flat, start=True, stop=True).then_inc(counted, 1)
            with pe.Fori(0, NS // U) as i:
                for pair in ((0, 1), (2, 3)):
                    for j in pair:
                        pe.wait_ge(x_in[j], 16 * i + 16)
                        for k in range(KD):
                            op = pe.transpose(GP[j % 2][:, k, 0:P], xs[:, j, k * P:(k + 1) * P], g.ident[:])
                        op.then_inc(turned[j], 1)
                    for j in pair:
                        pe.wait_ge(xT_ready[j], i + 1)
                        pe.wait_ge(w_in[j], 32 * i + 32)
                        for c in range(FC):
                            for k in range(KD):
                                op = pe.matmul(HB[j % 2][c // (FC // 2)][:, c % (FC // 2), :], w1(j, k, c), xsT[:, j, k, :],
                                               start=(k == 0), stop=(k == KD - 1))
                        op.then_inc(h_full[j], 1)
                    for j in pair:
                        pe.wait_ge(h_act[j], i + 1)
                        pe.wait_ge(h_dve[j], i + 1)
                        pe.wait_ge(y_ready[(j + 2) % U], i + 1 + j // 2)
                        for c in range(FC):
                            op = pe.matmul(YB[j % 2][:, 0], hT[:, j, c, :], w2(j, c), start=(c == 0), stop=(c == FC - 1))
                        op.then_inc(y_full[j], 1)

        @block.vector
        def _(dve):
            wide = lambda a: a[:].rearrange("p (t a) -> p t a", a=1).broadcast_to([P, NT, E])
            norm_factors(dve, g, sqrt_in, sqrt_out)
            dve.wait_ge(weights_in, 16 * 5)
            with dve.Fori(0, B) as b:
                dve.wait_ge(xn_turned, b + 1)
                normalise(dve, g, b, xn, xn_ready)
                dve.wait_ge(logits_full, b + 1)
                dve.tensor_tensor(lg[:, bass.ds(b * TT, TT), :], GP[1][:, :, 0:E],
                                  br[:].rearrange("p (a n) -> p a n", a=1).broadcast_to([P, TT, E]), ALU.add)\
                   .then_inc(logits_read, 1)
            dve.drain()
            dve.tensor_reduce(red[:], lg[:], AX.X, ALU.max)
            dve.drain()
            dve.tensor_tensor(lg[:], lg[:], wide(red), ALU.subtract).then_inc(shifted, 1)
            dve.wait_ge(exp_ready, 1)
            dve.tensor_reduce(red[:], sc[:], AX.X, ALU.add)
            dve.drain()
            dve.reciprocal(red[:], red[:])
            dve.drain()
            dve.tensor_tensor(sc[:], sc[:], wide(red), ALU.mult)
            dve.drain()
            for t in range(NT):
                other = sc[:, t, :].rearrange("p (a n) -> p a n", a=1).broadcast_to([P, E, E])
                own = sc[:, t, :].rearrange("p (n a) -> p n a", a=1).broadcast_to([P, E, E])
                dve.tensor_tensor(cmp[:, t], other, own, ALU.is_gt)
                dve.tensor_tensor(eq[:, t], other, own, ALU.is_equal)
            dve.drain()
            early = earlier[:, 0:E, 0:E].rearrange("p (a i) j -> p a i j", a=1).broadcast_to([P, NT, E, E])
            dve.tensor_tensor(eq[:], eq[:], early, ALU.mult)
            dve.drain()
            dve.tensor_tensor(cmp[:], cmp[:], eq[:], ALU.add)
            dve.drain()
            dve.tensor_reduce(rank[:], cmp[:], AX.X, ALU.add)
            dve.drain()
            dve.tensor_scalar(rank[:], rank[:], 1.5, None, ALU.is_lt)
            dve.tensor_scalar(win[:], sc[:], 0.0, None, ALU.is_gt)
            dve.drain()
            dve.tensor_tensor(rank[:], rank[:], win[:], ALU.mult)
            dve.drain()
            for t in range(NT):
                dve.tensor_tensor(cmp[:, t], rank[:, t, :].rearrange("p (n a) -> p n a", a=1).broadcast_to([P, E, E]),
                                  earlier[:, 0:E, 0:E], ALU.mult)
            dve.drain()
            dve.tensor_reduce(win[:], cmp[:].rearrange("p t j i -> p t i j"), AX.X, ALU.add)
            dve.drain()
            dve.tensor_scalar(win[:], win[:], 0.5, None, ALU.is_lt)
            dve.drain()
            dve.tensor_tensor(win[:], win[:], rank[:], ALU.mult).then_inc(win_ready, 1)
            dve.drain()
            dve.tensor_tensor(sc[:], sc[:], win[:], ALU.mult)
            dve.drain()
            dve.tensor_reduce(rw[:], sc[:], AX.X, ALU.add)
            dve.drain()
            dve.tensor_tensor(rw[:], rw[:], g.rstd[:], ALU.mult)
            dve.wait_ge(counted, 1)
            dve.tensor_copy(pre[:], HB[0][0][:, 0, :].rearrange("p (t e) -> p t e", e=E))
            dve.tensor_copy(tot[:], HB[0][1][:, 0, :].rearrange("p (t e) -> p t e", e=E))
            dve.tensor_copy(run[:, 0], HB[0][1][:, 0, :].rearrange("p (t e) -> p t e", e=E))
            dve.drain()
            a, d = 0, 1
            while d < NT:
                dve.tensor_copy(run[:, 1 - a, 0:d], run[:, a, 0:d])
                dve.tensor_tensor(run[:, 1 - a, d:NT], run[:, a, d:NT], run[:, a, 0:NT - d], ALU.add)
                dve.drain()
                a, d = 1 - a, 2 * d
            dve.tensor_tensor(pre[:], pre[:], tot[:], ALU.subtract)
            for e in range(E):
                dve.tensor_scalar(cmp2[:, e, :], steps[:, 0:NT], run[:, a, NT - 1, e:e + 1], None, ALU.is_lt)
            dve.drain()
            dve.tensor_tensor(pre[:], pre[:], run[:, a], ALU.add)
            dve.tensor_reduce(tiles[:, 0], cmp2[:], AX.X, ALU.add)
            dve.drain()
            dve.tensor_tensor(cmp4[:], tiles[:, 0:1, :].broadcast_to([P, E, E]), earlier[:, 0:E, 0:E], ALU.mult)
            dve.drain()
            dve.tensor_reduce(tiles[:, 1], cmp4[:], AX.X, ALU.add)
            dve.drain()
            dve.tensor_tensor(tiles[:, 0], tiles[:, 0], tiles[:, 1], ALU.add)
            dve.tensor_scalar(tiles[:, 2], tiles[:, 1], float(P), None, ALU.mult)
            dve.drain()
            dve.tensor_tensor(pre[:], pre[:], tiles[:, 2:3, :].broadcast_to([P, NT, E]), ALU.add)
            for sl in range(NS):
                dve.tensor_scalar(cmp3[:, sl, :], tiles[:, 0, :], float(sl), None, ALU.is_le)
            dve.drain()
            dve.tensor_tensor(pre[:], pre[:], win[:], ALU.mult)
            dve.tensor_reduce(slotf[:], cmp3[:], AX.X, ALU.add)
            dve.drain()
            dve.tensor_reduce(posf[:], pre[:], AX.X, ALU.add)
            dve.tensor_scalar(slotf[:], slotf[:], float(E - 1), None, ALU.min)
            dve.drain()
            dve.tensor_copy(pos[:], posf[:])
            dve.tensor_copy(slot[:], slotf[:]).then_inc(slots_known, 1)
            dve.drain()
            for t in range(NT):
                dve.tensor_scalar(rows[:, t, :], g.x[:, t, :], g.mean[:, t:t + 1], rw[:, t:t + 1],
                                  ALU.subtract, ALU.mult).then_inc(rows_ready, 1)
            with dve.Fori(0, NS // U) as i:
                for pair in ((0, 1), (2, 3)):
                    for j in pair:
                        dve.wait_ge(h_full[j], i + 1)
                        for c in range(FC // 2):
                            op = dve.tensor_scalar(hT[:, j, FC // 2 + c, :], HB[j % 2][1][:, c, :], b1(j, FC // 2 + c), 0.0,
                                                   ALU.add, ALU.max)
                        op.then_inc(h_dve[j], 1)
                    for j in pair:
                        dve.wait_ge(y_full[j], i + 1)
                        dve.wait_ge(y_stored[j], 16 * i + 1)
                        dve.tensor_tensor(ys[:, j, :], YB[j % 2][:, 0], b2[:, j, :], ALU.add).then_inc(y_ready[j], 1)
            for h in range(2):
                dve.wait_ge(gathered[h], 16 * NT // 2)
                own = slice(h * NT // 2, (h + 1) * NT // 2)
                dve.tensor_tensor(g.x[:, own, :], g.x[:, own, :], rows[:, own, :], ALU.add)
                dve.drain()
                for t in range(own.start, own.stop):
                    dve.bn_stats(g.stats[:, t, :], g.x[:, t, :])
            dve.drain()


def store_x(nc, g):
    with ExitStack() as ctx:
        stored = ctx.enter_context(nc.semaphore("x_stored"))
        start_semaphores(nc, [stored], [])
        block = ctx.enter_context(nc.Block())

        @block.sync
        def _(sp):
            sp.dma_start(g.io["out"].rearrange("b (t p) d -> p (b t) d", p=P), g.x[:]).then_inc(stored, 16)
            sp.wait_ge(stored, 16)


def constants():
    bf = lambda a: (np.ascontiguousarray(a, np.float32).view(np.uint32) >> 16).astype(np.uint16)
    c = {"c_ident": np.eye(P, dtype=np.float32), "c_eye": bf(np.eye(P))}
    for hd in (16, 64):
        m = np.zeros((P, P // hd), np.float32)
        for h in range(P // hd):
            m[h * hd:(h + 1) * hd, h] = 1
        c[f"c_mask{hd}"] = m
    sel = np.zeros((P, H, P), np.float32)
    for part in range(3):
        for h in range(H):
            sel[32 * part + h, h, :] = 1
    c["c_sel"] = bf(sel)
    c["c_earlier"] = np.broadcast_to(np.tril(np.ones((H, H), np.float32), -1), (P, H, H)).copy()
    c["c_descending"] = np.broadcast_to(np.arange(H, 0, -1, dtype=np.float32), (P, H)).copy()
    c["c_before"] = np.triu(np.ones((P, P), np.float32), 1)
    c["c_steps"] = np.broadcast_to(np.arange(24, dtype=np.float32) * P, (P, 24)).copy()
    turn = np.zeros((P, P), np.float32)
    for i in range(0, P, 2):
        turn[i + 1, i], turn[i, i + 1] = -1, 1
    c["c_turn"] = turn
    c["c_tri"] = np.triu(np.ones((P, P), np.float32))
    hd = 16
    half = hd // 2
    base = (np.arange(0, hd, 2) + 0.4 * hd) / (1.4 * hd)
    power = (np.arange(-(S // 2), -(S // 2) + S) / 512.0)[:, None]
    length = base[None, :] ** power
    angle = np.arange(S)[:, None] / 10000.0 ** (np.arange(half) / half)[None, :]
    gammas = 1.0 - np.exp(np.linspace(np.log(1 / 32), np.log(1 / 512), H))
    tables = np.zeros((4, H, hd, S))
    for i, (f, sign) in enumerate(((np.cos, 1), (np.sin, 1), (np.cos, -1), (np.sin, -1))):
        t = np.repeat(f(angle) * length ** sign, 2, axis=-1).T
        tables[i] = t[None] * gammas[:, None, None] ** (sign * np.arange(S))[None, None, :]
    c["c_tables"] = tables.reshape(4, 2, P, S).transpose(2, 0, 1, 3).astype(np.float32)
    q, k = np.arange(P)[:, None], np.arange(P)[None, :]
    c["c_neg_qk"] = bf(np.where(k > q, -8e9, 0.0))
    c["c_neg_kq"] = np.ascontiguousarray(c["c_neg_qk"].T)
    return c


def pad_heads(w, hp):
    out = np.zeros((H, hp) + w.shape[1:], w.dtype)
    out[:, :w.shape[0] // H] = w.reshape((H, w.shape[0] // H) + w.shape[1:])
    return out.reshape((H * hp,) + w.shape[1:])


def layouts(i):
    T = lambda a: np.ascontiguousarray(np.asarray(a).T)
    a = {"x": i["x"], "ctxT": np.ascontiguousarray(np.asarray(i["ctx_1024"]).transpose(0, 2, 1))}
    wkv = np.asarray(i["L0_xattn_w_kv"])
    a["a0_wq"] = i["L0_xattn_w_q"]
    a["a0_wk"] = np.tile(wkv[:, :16], (1, 8))
    a["a0_wv"] = wkv[:, 16:]
    a["a0_wo"] = pad_heads(np.asarray(i["L0_xattn_w_concat"]), 32)
    E, I = 16, 128
    first = lambda w, ws: np.concatenate(
        [np.asarray(ws).reshape(KD, P, -1, P).transpose(1, 2, 0, 3),
         np.asarray(w).reshape(-1, KD, P, P).transpose(2, 0, 1, 3)], 1)
    second = lambda w, ws: np.concatenate(
        [np.asarray(ws).reshape(-1, P, D).transpose(1, 0, 2), np.asarray(w).transpose(1, 0, 2)], 1)
    rows_of = lambda n: np.asarray(i[f"L0_ffn_We{n}"]).reshape(E, KD, P, I).transpose(2, 0, 1, 3)
    a["f0_w13"] = np.concatenate([rows_of(1), rows_of(3)], 3)
    a["f0_w2"] = np.asarray(i["L0_ffn_We2"]).transpose(1, 0, 2)
    a["f0_b13"], a["f0_b2"] = np.concatenate([i["L0_ffn_be1"], i["L0_ffn_be3"]], 1), i["L0_ffn_be2"]
    a["f0_ws13"] = np.stack([np.asarray(i[f"L0_ffn_ws{n}"]).reshape(KD, P, -1, P).transpose(1, 2, 0, 3) for n in (1, 3)], 2)
    a["f0_ws2"] = np.asarray(i["L0_ffn_ws2"]).reshape(-1, P, D).transpose(1, 0, 2)
    for n in "13":
        a[f"f0_bs{n}"] = T(np.asarray(i[f"L0_ffn_bs{n}"]).reshape(-1, P))
    a["f0_bs2"] = i["L0_ffn_bs2"]
    a["f0_wr"], a["f0_br"] = T(i["L0_ffn_gate_w"]), i["L0_ffn_gate_b"]
    per_partition = lambda n: np.asarray(i[f"L1_ffn_{n}"]).reshape(8, -1, P, i[f"L1_ffn_{n}"].shape[-1])\
        .transpose(0, 2, 1, 3).reshape(8, P, -1)
    a["f1_w"] = np.concatenate([per_partition("w1"), per_partition("w2"),
                                np.asarray(i["L1_ffn_b1"]).reshape(8, -1, P).transpose(0, 2, 1)], 2)
    a["f1_b2"], a["f1_wr"], a["f1_br"] = i["L1_ffn_b2"], i["L1_ffn_gate_w"], i["L1_ffn_gate_b"]
    a["f3_w1"] = first(i["L3_ffn_W1"], i["L3_ffn_Ws1"])
    a["f3_w2"] = second(i["L3_ffn_W2"], i["L3_ffn_Ws2"])
    a["f3_wr"] = i["L3_ffn_Wr"]
    for n in "QKV":
        a[f"a1_w{n.lower()}"] = np.asarray(i[f"L1_xattn_W_{n}"]).transpose(1, 0, 2).reshape(D, D)
    a["a1_wg"], a["a1_wo"] = T(i["L1_xattn_g_w"]), T(i["L1_xattn_out_w"])
    a["a1_gb"], a["a1_bo"] = i["L1_xattn_g_b"], i["L1_xattn_out_b"]
    a["a2_wq"], a["a2_wk"], a["a2_wv"] = (T(i[f"L2_xattn_w{n}"]) for n in "qkv")
    a["a2_wo"] = pad_heads(T(i["L2_xattn_wo"]), 32)
    for n in ("bq", "bk"):
        a[f"a2_{n}"] = T(np.asarray(i[f"L2_xattn_{n}"]).reshape(-1, P))
    for n in ("bv", "bo"):
        a[f"a2_{n}"] = i[f"L2_xattn_{n}"]
    for n in "qkv":
        a[f"f2_w{n}"] = T(i[f"L2_ffn_W{n}"])
    a["f2_wo"] = pad_heads(T(i["L2_ffn_Wp"]), 32)
    a["f2_bq"], a["f2_bv"], a["f2_bo"] = (i[f"L2_ffn_b{n}"] for n in "qvp")
    a["f2_bk"] = T(np.asarray(i["L2_ffn_bk"]).reshape(-1, P))
    a["f2_wr"] = pad_heads(np.concatenate([T(i["L2_ffn_Wr"]), T(i["L2_ffn_Ws"])], 1), 32)
    a["f2_br"] = np.concatenate([np.asarray(i["L2_ffn_br"]), np.asarray(i["L2_ffn_bs"])])
    a["f2_qe"] = np.asarray(i["L2_ffn_query_embedding"]).reshape(-1)
    a["f2_temp"] = np.asarray(i["L2_ffn_temperature"]).reshape(-1)
    for n in "qkv":
        w = np.asarray(i[f"L3_xattn_W{n}"])
        a[f"a3_w{n}"] = w.transpose(1, 0, 2).reshape(D, -1)
    a["a3_wo"] = i["L3_xattn_Wo"]
    a.update(constants())
    return {k: np.ascontiguousarray(v) for k, v in a.items()}


def sub(a, pre):
    return {n[len(pre):]: v for n, v in a.items() if n.startswith(pre)}


STAGES = ["a0", "f0", "a1", "f1", "a2", "f2", "a3", "f3"]


def program(nc, io, stages):
    for n in ("c_eye", "c_sel", "c_neg_qk", "c_neg_kq"):
        io[n] = io[n].bitcast(BF16)
    with ExitStack() as ctx:
        g = Common(nc, ctx, io)
        load_x(nc, g)
        for s in stages:
            w = sub(io, s + "_")
            if s == "a0":
                attention(nc, g, s, 16, w, shared_kv=True)
            elif s == "f0":
                sorted_gated_experts(nc, g, s, w)
            elif s == "f3":
                experts(nc, g, s, w, False)
            elif s == "f1":
                sorted_experts(nc, g, s, w)
            elif s == "a1":
                retention(nc, g, s, w)
            elif s == "a2":
                attention(nc, g, s, 16, w, bias=True)
            elif s == "a3":
                attention(nc, g, s, 64, w, causal=True, interleave=True)
            elif s == "f2":
                attention(nc, g, s, 16, w, bias=True, kv_from_x=True, router=True)
        store_x(nc, g)


def kernel(**inputs):
    import concourse.bacc as bacc
    from concourse.bass_utils import run_bass_kernel_spmd

    nc = bacc.Bacc("TRN2", target_bir_lowering=False, num_devices=1)
    arrays = layouts(inputs)
    io = {n: nc.dram_tensor(n, a.shape, mybir.dt.from_np(a.dtype), kind="ExternalInput").ap()
          for n, a in arrays.items()}
    io["out"] = nc.dram_tensor("out", (B, S, D), F32, kind="ExternalOutput").ap()
    program(nc, io, STAGES)
    result = run_bass_kernel_spmd(nc, [arrays], core_ids=[0])
    return result.results[0]["out"]
```

```python
from contextlib import ExitStack

import numpy as np
import concourse.bass as bass
from concourse import mybir

F32 = mybir.dt.float32
BF16 = mybir.dt.bfloat16
F32R = mybir.dt.float32r
ALU = mybir.AluOpType
ACT = mybir.ActivationFunctionType
AX = mybir.AxisListType

P = 128
B, S, D = 8, 256, 256
TT = S // P
KD = D // P
NT = B * TT
H = 16
EPS = 1e-5


class Banks:

    def __init__(self, uses, n=2):
        self.bank = {u: i % n for i, u in enumerate(uses)}
        self.nth = {u: i // n for i, u in enumerate(uses)}
        self.per = [sum(1 for u in uses if self.bank[u] == k) for k in range(n)]

    def before(self, b, u):
        return b * self.per[self.bank[u]] + self.nth[u] + 1

    def after(self, b, u):
        return self.before(b, u) + 1


DEPTH = 2


class Step:

    def __init__(self, s=None, i=None, j=0):
        self.s, self.i, self.j = s, i, j

    def has(self, part):
        return self.i is not None or 0 <= self.s - part < B

    def seq(self, part):
        return self.s - part if self.i is None else self.i * 2 + (DEPTH + self.j - part)

    def half(self, part):
        return (self.s - part if self.i is None else DEPTH + self.j - part) % 2


def run_steps(eng, body):
    for s in range(DEPTH):
        body(Step(s))
    with eng.Fori(0, (B - DEPTH) // 2) as i:
        for j in range(2):
            body(Step(i=i, j=j))
    for s in range(B, B + DEPTH):
        body(Step(s))


class StepBanks:

    def __init__(self, uses, n=2):
        self.uses = uses
        self.bank = {u: i % n for i, (u, _) in enumerate(uses)}

    def in_step(self, st, k, until=None):
        n = 0
        for u, part in self.uses:
            if u == until:
                break
            n += self.bank[u] == k and st.has(part)
        return n

    def before(self, st, u):
        k = self.bank[u]
        count = self.in_step(st, k, u) + 1
        if st.i is None:
            return count + sum(self.in_step(Step(s), k) for s in range(st.s))
        per = self.in_step(Step(DEPTH), k)
        count += sum(self.in_step(Step(s), k) for s in range(DEPTH)) + st.j * per
        return st.i * (2 * per) + count

    def after(self, st, u):
        return self.before(st, u) + 1

    def at_start(self, st, u):
        return self.before(st, next(v for v, _ in self.uses if self.bank[v] == self.bank[u]))

    def per(self, u):
        return self.in_step(Step(DEPTH), self.bank[u])


class Common:

    def __init__(self, nc, ctx, io):
        self.nc, self.io = nc, io
        sb = lambda n, s, t=F32: ctx.enter_context(nc.sbuf_tensor(f"g_{n}", s, t))
        self.x = sb("x_all", [P, NT, D])
        self.stats = sb("ln_stats", [P, NT, 6])
        self.mean = sb("ln_mean", [P, NT])
        self.rstd = sb("ln_rstd", [P, NT])
        self.tmp = sb("ln_tmp", [P, 4, NT])
        self.ident = sb("ident", [P, P])
        self.moved = [[ctx.enter_context(nc.semaphore(f"g_{n}{layer}")) for n in
                       ("scattered", "gathered_first", "gathered_second")] for layer in range(2)]


def start_semaphores(nc, sems, from_one):
    numbers = sorted(x.num for x in sems + from_one)
    with nc.Block() as block:
        @block.sync
        def _(sp):
            start = numbers[0]
            for n, after in zip(numbers, numbers[1:] + [None]):
                if after != n + 1:
                    sp.sem_clear(range(start, n + 1))
                    start = after
            for x in from_one:
                sp.sem_inc(x, 1)


def load_x(nc, g):
    with ExitStack() as ctx:
        loaded = ctx.enter_context(nc.semaphore("x_loaded"))
        block = ctx.enter_context(nc.Block())

        @block.sync
        def _(sp):
            sp.dma_start(g.ident[:], g.io["c_ident"]).then_inc(loaded, 16)
            sp.dma_start(g.x[:], g.io["x"].rearrange("b (t p) d -> p (b t) d", p=P)).then_inc(loaded, 16)

        @block.vector
        def _(dve):
            dve.wait_ge(loaded, 32)
            for t in range(NT):
                dve.bn_stats(g.stats[:, t, :], g.x[:, t, :])


def norm_factors(dve, g, sqrt_in, sqrt_out):
    st, tmp = g.stats, g.tmp
    dve.tensor_tensor(g.mean[:], st[:, :, 1], st[:, :, 4], ALU.add)
    dve.tensor_tensor(tmp[:, 0, :], st[:, :, 1], st[:, :, 4], ALU.subtract)
    dve.tensor_tensor(tmp[:, 1, :], st[:, :, 2], st[:, :, 5], ALU.add)
    dve.drain()
    dve.tensor_scalar(g.mean[:], g.mean[:], 0.5, None, ALU.mult)
    dve.tensor_tensor(tmp[:, 0, :], tmp[:, 0, :], tmp[:, 0, :], ALU.mult)
    dve.tensor_scalar(tmp[:, 1, :], tmp[:, 1, :], 1.0 / D, EPS, ALU.mult, ALU.add)
    dve.drain()
    dve.scalar_tensor_tensor(out=tmp[:, 1, :], in0=tmp[:, 0, :], scalar=0.25, in1=tmp[:, 1, :],
                             op0=ALU.mult, op1=ALU.add).then_inc(sqrt_in, 1)
    dve.wait_ge(sqrt_out, 1)
    dve.reciprocal(g.rstd[:], tmp[:, 2, :])
    dve.drain()
    dve.tensor_tensor(tmp[:, 0, :], g.rstd[:], g.rstd[:], ALU.mult)
    dve.drain()
    dve.tensor_tensor(tmp[:, 0, :], tmp[:, 0, :], tmp[:, 1, :], ALU.mult)
    dve.drain()
    dve.tensor_scalar(tmp[:, 0, :], tmp[:, 0, :], -0.5, 1.5, ALU.mult, ALU.add)
    dve.drain()
    dve.tensor_tensor(g.rstd[:], g.rstd[:], tmp[:, 0, :], ALU.mult)
    dve.drain()


def norm_sqrt(act, g, sqrt_in, sqrt_out):
    act.wait_ge(sqrt_in, 1)
    act.activation(g.tmp[:, 2, :], g.tmp[:, 1, :], ACT.Sqrt).then_inc(sqrt_out, 1)


def normalise(dve, g, b, xn, ready):
    for t in range(TT):
        i = b * TT + t
        op = dve.tensor_scalar(xn[:, t, :], g.x[:, bass.ds(i, 1), :].rearrange("p a d -> p (a d)"),
                               g.mean[:, bass.ds(i, 1)], g.rstd[:, bass.ds(i, 1)], ALU.subtract, ALU.mult)
    if ready is not None:
        op.then_inc(ready, 1)


def add_to_x(dve, g, b, y):
    xb = g.x[:, bass.ds(b * TT, TT), :]
    op = dve.tensor_tensor(xb, xb, y, ALU.add)
    return op


def next_stats(dve, g, b):
    for t in range(TT):
        i = b * TT + t
        dve.bn_stats(g.stats[:, bass.ds(i, 1), :].rearrange("p a d -> p (a d)"),
                     g.x[:, bass.ds(i, 1), :].rearrange("p a d -> p (a d)"))


def transpose_xn(pe, g, xn, out):
    for k in range(KD):
        for t in range(TT):
            op = pe.transpose(out[:, k, t * P:(t + 1) * P], xn[:, t, k * P:(k + 1) * P], g.ident[:])
    return op


PART = {"norm": 0, "xT": 0, "q": 0, "k": 0, "v": 0, "qT": 0, "max": 1, "neg": 1, "score": 1, "weigh": 1,
        "gate": 2, "y": 2, "logits": 2, "finish": 2, "scale": 0}


def plan(NQ, NKB, NV, SU, HO, CO, router):
    maxima = [("max", u) for u in range(SU)]
    order = [maxima[0], ("norm", 0), maxima[1]] + ([("gate", 0)] if router else []) + [("y", 0), ("xT", 0)]
    between = [("q", i) for i in range(NQ)] + [("k", i) for i in range(NKB)] + [("v", i) for i in range(NV)]
    late = max(1, NV // 2)
    between, late = between[:-late], between[-late:]
    rest = maxima[2:]
    for n, m in enumerate(rest):
        order += between[len(between) * n // len(rest):len(between) * (n + 1) // len(rest)] + [m]
    order += [("neg", 0)] + late
    done = 0
    for u in range(SU):
        if u == 1:
            order.append(("logits", 0) if router else ("finish", 0))
        if u == SU // 2 and router:
            order.append(("scale", 0))
        if u == SU - 2 and router:
            order.append(("finish", 0))
        order.append(("score", u))
        while done < 2 * u // HO:
            order.append(("weigh", done))
            done += 1
    return order + ([("qT", 0)] if router else []) + [("weigh", c) for c in range(done, CO)]


def attention(nc, g, name, hd, w, kv_from_x=False, shared_kv=False, causal=False, bias=False, router=False,
              interleave=False):
    io = g.io
    CQ = H * hd // P
    CK = 1 if shared_kv else CQ
    HC = P // hd
    HP = 32 if hd == 16 else 64
    HO = P // HP
    CO = H // HO
    KH = HC if shared_kv else H
    VH = 1 if shared_kv else H
    scale = float(hd) ** -0.5
    NQ = max(1, CQ // 2)
    NKB = max(1, CK // 2)
    NV = 1 if shared_kv else max(1, H * hd // D)
    SU = H // 2
    order = plan(NQ, NKB, NV, SU, HO, CO, router)
    gp = StepBanks([(f"{what}{i}" if what in "qkv" else what, PART[what]) for what, i in order
                    if what not in ("norm", "max", "score", "weigh", "logits", "finish", "scale")])
    sc = Banks([("max", u) for u in range(SU)] + [("exp", u) for u in range(SU)])
    ot = Banks(list(range(CO)))

    with ExitStack() as ctx:
        sb = lambda n, s, t=F32: ctx.enter_context(nc.sbuf_tensor(f"{name}_sb_{n}", s, t))
        sems, from_one = [], []

        def sem(n, one=False):
            s = ctx.enter_context(nc.semaphore(f"{name}_{n}"))
            (from_one if one else sems).append(s)
            return s
        wq = sb("wq", [P, KD, H * hd])
        wk = sb("wk", [P, KD, CK * P])
        wv = sb("wv", [P, KD, VH * hd])
        wo = sb("wo", [P, CO, D])
        mask = sb("mask", [P, HC])
        sel = sb("sel", [P, H, P], BF16)
        xn = sb("xn", [P, TT, D])
        xnT = sb("xnT", [P, KD, S])
        kvT = xnT if kv_from_x else sb("kvT", [P, KD, S])
        qT = sb("qT", [P, CQ, S])
        kT = sb("kT", [P, CK, S])
        q_hi2, q_lo2 = (sb(f"q_{part}", [P, 2, CQ, S], F32R) for part in ("hi", "lo"))
        k_hi2, k_lo2 = (sb(f"k_{part}", [P, 2, KH, S], F32R) for part in ("hi", "lo"))
        v2 = sb("v", [P, 2, TT, VH, HP])
        ones = sb("ones", [P, HP])
        mx = sb("mx", [P, TT, H])
        negT = sb("negT", [P, S], BF16)
        rest = sb("rest", [H, S])
        probs = sb("probs", [P, 2, HO, TT, S])
        rden = sb("rden", [P, 2, S])
        oT = sb("oT", [P, CO, S])
        yt = sb("yt", [P, TT, D]) if router else rden
        if causal:
            eye = sb("eye", [P, P], BF16)
            neg_qk = sb("neg_qk", [P, P], BF16)
        if bias:
            bq = sb("bq", [P, CQ])
            bk = sb("bk", [P, CK])
            bv = sb("bv", [P, D])
            bo = sb("bo", [P, D])
        if router:
            bqt = sb("bqt", [P, D])
            qe = sb("qe", [P, D])
            sp_t = sb("sp_t", [P, 4, H])
            spq = sb("spq", [P, H])
            qtm = sb("qtm", [P, TT, D])
            qsq = sb("qsq", [P, TT, D])
            qn = sb("qn", [P, 3, TT, H])
            wr = sb("wr", [P, CO, H + 1])
            br = sb("br", [P, H + 1])
            lg = sb("lg", [P, TT, 24])
            le = sb("le", [P, TT, 24])
            top = sb("top", [P, TT, 8])
            sm = sb("sm", [P, TT, 8])
            graw = sb("graw", [P, TT, H + 1])
        GP = [ctx.enter_context(nc.psum_tensor(f"{name}_gp{i}", [P, 2, S], F32)) for i in range(2)]
        SC = [ctx.enter_context(nc.psum_tensor(f"{name}_sc{i}", [P, 2, 2, S], F32)) for i in range(2)]
        OT = [ctx.enter_context(nc.psum_tensor(f"{name}_ot{i}", [P, 2, S], F32)) for i in range(2)]

        weights_in = sem("weights_in")
        kv_in = sem("kv_in")
        sqrt_in, sqrt_out = sem("sqrt_in"), sem("sqrt_out")
        fixed = sem("fixed")
        xn_ready = sem("xn_ready")
        q_sums = sem("q_sums")
        q_roots = sem("q_roots")
        q_scaled = sem("q_scaled")
        softplus = sem("softplus")
        gate_in, gate_exp = sem("gate_in"), sem("gate_exp")
        y_used = sem("y_used", one=True)
        parts_ready = sem("parts_ready")
        act_step = sem("act_step")
        gp_full = [sem(f"gp_full{i}", one=True) for i in range(2)]
        gp_read = [sem(f"gp_read{i}", one=True) for i in range(2)]
        sc_full = [sem(f"sc_full{i}", one=True) for i in range(2)]
        sc_read = [sem(f"sc_read{i}", one=True) for i in range(2)]
        ot_full = [sem(f"ot_full{i}", one=True) for i in range(2)]
        ot_read = [sem(f"ot_read{i}", one=True) for i in range(2)]

        def gp_wait(eng, sems, st, u, after):
            eng.wait_ge(sems[gp.bank[u]], gp.after(st, u) if after else gp.before(st, u))

        loads = [(wq, w["wq"].rearrange("(k p) n -> p k n", p=P)),
                 (wk, w["wk"].rearrange("(k p) n -> p k n", p=P)),
                 (wv, w["wv"].rearrange("(k p) n -> p k n", p=P)),
                 (wo, w["wo"].rearrange("(c p) n -> p c n", p=P)),
                 (mask, io[f"c_mask{hd}"]), (sel, io["c_sel"])]
        if causal:
            loads += [(eye, io["c_eye"]), (neg_qk, io["c_neg_qk"])]
        if bias:
            loads += [(bk, w["bk"]),
                      (bv, w["bv"].rearrange("(a n) -> a n", a=1).broadcast_to([P, D])),
                      (bo, w["bo"].rearrange("(a n) -> a n", a=1).broadcast_to([P, D]))]
            if not router:
                loads += [(bq, w["bq"])]
        if router:
            loads += [(bqt, w["bq"].rearrange("(a n) -> a n", a=1).broadcast_to([P, D])),
                      (qe, w["qe"].rearrange("(a n) -> a n", a=1).broadcast_to([P, D])),
                      (sp_t[:, 0, :], w["temp"].rearrange("(a n) -> a n", a=1).broadcast_to([P, H])),
                      (wr, w["wr"].rearrange("(c p) n -> p c n", p=P)),
                      (br, w["br"].rearrange("(a n) -> a n", a=1).broadcast_to([P, H + 1]))]
        all_in = 16 * len(loads)

        start_semaphores(nc, sems, from_one)
        block = ctx.enter_context(nc.Block())

        @block.sync
        def _(sp):
            for dst, src in loads:
                sp.dma_start(dst if isinstance(dst, bass.AP) else dst[:], src).then_inc(weights_in, 16)
            if not kv_from_x:
                u = f"v{NV - 1}"

                def load_context(b):
                    sp.dma_start(kvT[:], io["ctxT"][b].rearrange("(k p) s -> p k s", p=P)).then_inc(kv_in, 16)

                load_context(0)
                sp.wait_ge(gp_full[gp.bank[u]], gp.at_start(Step(1), u))
                load_context(1)
                with sp.Fori(0, B - 2) as b:
                    sp.wait_ge(gp_full[gp.bank[u]], b * gp.per(u) + gp.at_start(Step(DEPTH), u))
                    load_context(b + 2)

        @block.gpsimd
        def _(pool):
            pool.memset(v2[:], 0.0).then_inc(fixed, 1)
            pool.memset(ones[:], 1.0).then_inc(fixed, 1)
            pool.memset(negT[:], 0.0).then_inc(fixed, 1)
            pool.wait_ge(weights_in, all_in)
            def q_rest(st, u, q0, n):
                gp_wait(pool, gp_read, st, u, True)
                return pool.tensor_tensor(q_lo2[:, st.half(0), q0:q0 + n], qT[:, q0:q0 + n],
                                          q_hi2[:, st.half(0), q0:q0 + n].bitcast(F32), ALU.subtract)

            def step(st):
                if not st.has(0):
                    return
                if not router:
                    for i in range(NQ):
                        q_rest(st, f"q{i}", 2 * i, min(2, CQ - 2 * i))
                for i in range(NKB):
                    gp_wait(pool, gp_read, st, f"k{i}", True)
                    chunks = range(2 * i, min(2 * i + 2, CK))
                    part = lambda a, c: a[:, st.half(0), c * HC:(c + 1) * HC, :]
                    wide_k = lambda c: kT[:, c:c + 1, :].broadcast_to([P, HC, S])
                    own = mask[:].rearrange("p (h a) -> p h a", a=1).broadcast_to([P, HC, S])
                    for c in chunks:
                        pool.tensor_tensor(part(k_hi2, c), wide_k(c), own, ALU.mult)
                    pool.drain()
                    for c in chunks:
                        pool.tensor_tensor(part(k_lo2, c), wide_k(c), part(k_hi2, c).bitcast(F32), ALU.subtract)
                    pool.drain()
                    for c in chunks:
                        op = pool.tensor_tensor(part(k_lo2, c), part(k_lo2, c).bitcast(F32), own, ALU.mult)
                if router:
                    op = q_rest(st, "qT", 0, CQ)
                op.then_inc(parts_ready, 1)

            run_steps(pool, step)

        @block.scalar
        def _(act):
            norm_sqrt(act, g, sqrt_in, sqrt_out)
            act.wait_ge(weights_in, all_in)
            if router:
                act.activation(sp_t[:, 1, :], sp_t[:, 0, :], ACT.Abs).then_inc(act_step, 1)
                act.wait_ge(act_step, 1)
                act.activation(sp_t[:, 1, :], sp_t[:, 1, :], ACT.Exp, scale=-1.0).then_inc(act_step, 1)
                act.wait_ge(act_step, 2)
                act.activation(sp_t[:, 2, :], sp_t[:, 1, :], ACT.Ln, bias=1.0).then_inc(softplus, 1)
            def evacuate(dsts, u, n, st, biases=None):
                gp_wait(act, gp_full, st, u, True)
                for dst in dsts:
                    if biases is None:
                        op = act.activation(dst, GP[gp.bank[u]][:, 0:n, :], ACT.Copy)
                    else:
                        for c in range(n):
                            op = act.activation(dst[:, c, :], GP[gp.bank[u]][:, c, :], ACT.Identity,
                                                bias=biases[:, c:c + 1])
                op.then_inc(gp_read[gp.bank[u]], 1)

            def step(st):
                for what, i in order:
                    if not st.has(PART[what]):
                        continue
                    if what == "xT":
                        evacuate([xnT[:]], "xT", KD, st)
                    elif what == "q" and not router:
                        evacuate([qT[:, 2 * i:2 * i + 2, :], q_hi2[:, st.half(0), 2 * i:2 * i + 2, :]], f"q{i}", 2, st,
                                 bq[:, 2 * i:2 * i + 2] if bias else None)
                    elif what == "k":
                        n = min(2, CK - 2 * i)
                        evacuate([kT[:, 2 * i:2 * i + n, :]], f"k{i}", n, st, bk[:, 2 * i:2 * i + n] if bias else None)
                    elif what == "qT":
                        evacuate([qT[:], q_hi2[:, st.half(0)]], "qT", CQ, st)
                    elif what == "score":
                        use = ("exp", i)
                        pair = sc.bank[use]
                        c = 2 * i // HO
                        if 2 * i % HO == 0:
                            if c >= 2:
                                act.wait_ge(ot_full[c % 2], ot.before(st.seq(1), c))
                            else:
                                act.wait_ge(ot_full[c % 2], st.seq(1) * ot.per[c % 2] + 1)
                        act.wait_ge(sc_full[pair], sc.after(st.seq(1), use))
                        h0 = 2 * i % HO
                        pr = probs[:, c % 2, h0:h0 + 2]
                        if causal:
                            act.activation(pr[:, :, 0, :], SC[pair][:, :, 0, :], ACT.Exp, scale=scale)
                            act.activation(pr[:, :, 1, P:S], SC[pair][:, :, 1, P:S], ACT.Exp, scale=scale)\
                               .then_inc(sc_read[pair], 1)
                        else:
                            act.activation(pr, SC[pair][:], ACT.Exp, scale=scale).then_inc(sc_read[pair], 1)
                    elif what == "gate":
                        act.wait_ge(y_used, st.seq(2) + 1)
                        gp_wait(act, gp_full, st, "gate", True)
                        act.activation(graw[:], GP[gp.bank["gate"]][:, :, 0:H + 1], ACT.Copy)\
                           .then_inc(gp_read[gp.bank["gate"]], 1)
                    elif what == "y":
                        act.wait_ge(y_used, st.seq(2) + 1)
                        evacuate([yt[:]], "y", TT, st)
                    elif what == "scale":
                        head_norms(st)
                    elif what == "finish" and router:
                        act.wait_ge(gate_in, st.seq(2) + 1)
                        act.activation(le[:, :, 0:H + 1], lg[:, :, 0:H + 1], ACT.Exp).then_inc(gate_exp, 1)

            def head_norms(st):
                act.wait_ge(q_sums, st.seq(0) + 1)
                act.activation(qn[:, 1], qn[:, 0], ACT.Sqrt).then_inc(q_roots, 1)

            run_steps(act, step)

        @block.tensor
        def _(pe):
            pe.wait_ge(weights_in, all_in)
            pe.wait_ge(fixed, 3)
            def transposed(src, st, u):
                gp_wait(pe, gp_read, st, u, False)
                transpose_xn(pe, g, src, GP[gp.bank[u]]).then_inc(gp_full[gp.bank[u]], 1)

            def features(st, u, wgt, cols, rhs, n0):
                gp_wait(pe, gp_read, st, u, False)
                for c in range(cols):
                    for k in range(KD):
                        op = pe.matmul(GP[gp.bank[u]][:, c, :], wgt[:, k, (n0 + c) * P:(n0 + c + 1) * P],
                                       rhs[:, k, :], start=(k == 0), stop=(k == KD - 1))
                op.then_inc(gp_full[gp.bank[u]], 1)

            def tokens(st, u, lhs, wgt, n0, n):
                gp_wait(pe, gp_read, st, u, False)
                for t in range(TT):
                    for k in range(KD):
                        op = pe.matmul(GP[gp.bank[u]][:, t, 0:n], lhs[:, k, t * P:(t + 1) * P], wgt[:, k, n0:n0 + n],
                                       start=(k == 0), stop=(k == KD - 1))
                op.then_inc(gp_full[gp.bank[u]], 1)

            def row_scores(st, u):
                q_hi, k_hi = q_hi2[:, st.half(1)], k_hi2[:, st.half(1)]
                use = ("max", u)
                pair = sc.bank[use]
                pe.wait_ge(sc_read[pair], sc.before(st.seq(1), use))
                for j in range(2):
                    h = 2 * u + j
                    for t in range(TT):
                        keys = (t + 1) * P if causal else S
                        op = pe.matmul(SC[pair][:, j, t, 0:keys], q_hi[:, h // HC, t * P:(t + 1) * P],
                                       k_hi[:, h % KH, 0:keys], start=True, stop=True)
                        if causal:
                            op = pe.matmul(SC[pair][:, j, t, t * P:keys], eye[:], neg_qk[:],
                                           start=False, stop=True, skip_group_check=True)
                op.then_inc(sc_full[pair], 1)

            def negated_maxima(st):
                gp_wait(pe, gp_read, st, "neg", False)
                for pair in range(2):
                    pe.wait_ge(sc_read[pair], sc.after(st.seq(1), ("max", SU - 2 + pair)))
                for t in range(TT):
                    op = pe.transpose(GP[gp.bank["neg"]][0:H, 0, t * P:(t + 1) * P], mx[:, t, :], g.ident[:])
                op.then_inc(gp_full[gp.bank["neg"]], 1)

            def scores(st, u):
                (q_hi, q_lo), (k_hi, k_lo) = ([a[:, st.half(1)] for a in pair_] for pair_ in ((q_hi2, q_lo2), (k_hi2, k_lo2)))
                use = ("exp", u)
                pair = sc.bank[use]
                pe.wait_ge(sc_read[pair], sc.before(st.seq(1), use))
                for j in range(2):
                    h = 2 * u + j
                    for t in range(TT):
                        q0 = t * P if causal else 0
                        out = SC[pair][:, j, t, q0:S]
                        for n, (k_part, q_part) in enumerate(((k_hi, q_hi), (k_hi, q_lo), (k_lo, q_hi))):
                            pe.matmul(out, k_part[:, h % KH, t * P:(t + 1) * P], q_part[:, h // HC, q0:S],
                                      start=(n == 0), stop=False)
                        op = pe.matmul(out, sel[:, h, :], negT[:, q0:S], start=False, stop=True)
                        if causal:
                            op = pe.matmul(SC[pair][:, j, t, t * P:(t + 1) * P], neg_qk[:], eye[:],
                                           start=False, stop=True, skip_group_check=True)
                op.then_inc(sc_full[pair], 1)

            def weigh(st, c):
                v = v2[:, st.half(1)]
                for u in range(c * HO // 2, (c + 1) * HO // 2):
                    use = ("exp", u)
                    pe.wait_ge(sc_read[sc.bank[use]], sc.after(st.seq(1), use))
                pe.wait_ge(ot_read[c % 2], ot.before(st.seq(1), c))
                for what in range(2):
                    for j, t in [(j, t) for j in range(HO) for t in range(TT)] if interleave else \
                            [(j, t) for t in range(TT) for j in range(HO)]:
                        h = c * HO + j
                        q0 = t * P if causal else 0
                        lhs = v[:, t, h % VH, :] if what == 0 else ones[:]
                        if interleave:
                            for par in range(2):
                                op = pe.matmul(OT[c % 2][par * HP:(par + 1) * HP, what, j * P + q0 // 2:(j + 1) * P],
                                               lhs, probs[:, c % 2, j, t, q0 + par:S:2],
                                               start=(t == 0), stop=(t == TT - 1))
                        else:
                            op = pe.matmul(OT[c % 2][j * HP:(j + 1) * HP, what, q0:S], lhs,
                                           probs[:, c % 2, j, t, q0:S], start=(t == 0), stop=(t == TT - 1))
                op.then_inc(ot_full[c % 2], 1)

            def heads_out(st, u, wgt, n):
                for i in range(2):
                    pe.wait_ge(ot_read[i], ot.after(st.seq(2), CO - 2 + i))
                gp_wait(pe, gp_read, st, u, False)
                for t in range(TT):
                    for c in range(CO):
                        if interleave:
                            lhs = oT[:].rearrange("p c (j i r) -> p r (c j) i", j=HO, r=CO)[:, c, 8 * t:8 * t + 8, :]
                        else:
                            lhs = oT[:, c, t * P:(t + 1) * P]
                        op = pe.matmul(GP[gp.bank[u]][:, t, 0:n], lhs, wgt[:, c, :],
                                       start=(c == 0), stop=(c == CO - 1))
                op.then_inc(gp_full[gp.bank[u]], 1)

            def step(st):
                for what, i in order:
                    if not st.has(PART[what]):
                        continue
                    if what == "xT":
                        pe.wait_ge(xn_ready, st.seq(0) + 1)
                        transposed(xn, st, "xT")
                    elif what == "q":
                        gp_wait(pe, gp_read, st, "xT", True)
                        if router:
                            tokens(st, "q0", xnT, wq, 0, D)
                        else:
                            features(st, f"q{i}", wq, 2, xnT, 2 * i)
                    elif what == "k":
                        if not kv_from_x:
                            pe.wait_ge(kv_in, st.seq(0) * 16 + 16)
                        features(st, f"k{i}", wk, min(2, CK), kvT, 2 * i)
                    elif what == "v":
                        n = min(VH * hd, D)
                        tokens(st, f"v{i}", kvT, wv, i * n, n)
                    elif what == "qT":
                        pe.wait_ge(q_scaled, st.seq(0) + 1)
                        transposed(qtm, st, "qT")
                    elif what == "max":
                        if i == 0:
                            pe.wait_ge(parts_ready, st.seq(1) + 1)
                        row_scores(st, i)
                    elif what == "neg":
                        negated_maxima(st)
                    elif what == "score":
                        if i == 0:
                            gp_wait(pe, gp_read, st, "neg", True)
                        scores(st, i)
                    elif what == "weigh":
                        if i == 0:
                            pe.wait_ge(gp_read[gp.bank[f"v{NV - 1}"]], gp.at_start(st, f"v{NV - 1}"))
                        weigh(st, i)
                    elif what == "gate":
                        heads_out(st, "gate", wr, H + 1)
                    elif what == "y":
                        heads_out(st, "y", wo, D)

            run_steps(pe, step)

        @block.vector
        def _(dve):
            over_tokens = lambda row: row[:].rearrange("p (a n) -> p a n", a=1).broadcast_to([P, TT, D])

            def gate_logits(st):
                gp_wait(dve, gp_read, st, "gate", True)
                dve.tensor_tensor(lg[:, :, 0:H + 1], graw[:],
                                  br[:].rearrange("p (a n) -> p a n", a=1).broadcast_to([P, TT, H + 1]), ALU.add)
                dve.drain()
                for i, (lo, hi) in enumerate(((0, H - 1), (H - 1, H + 1))):
                    dve.tensor_reduce(sm[:, :, i], lg[:, :, lo:hi], AX.X, ALU.max)
                dve.drain()
                for i, (lo, hi) in enumerate(((0, H - 1), (H - 1, H + 1))):
                    op = dve.tensor_tensor(lg[:, :, lo:hi], lg[:, :, lo:hi],
                                           sm[:, :, i:i + 1].broadcast_to([P, TT, hi - lo]), ALU.subtract)
                op.then_inc(gate_in, 1)

            def gate_factor(st):
                dve.wait_ge(gate_exp, st.seq(2) + 1)
                for i, (lo, hi) in enumerate(((0, H - 1), (H - 1, H + 1))):
                    dve.tensor_reduce(sm[:, :, i], le[:, :, lo:hi], AX.X, ALU.add)
                for t in range(TT):
                    dve.max(top[:, t, :], le[:, t, 0:H - 1])
                dve.drain()
                dve.tensor_reduce(sm[:, :, 2], top[:, :, 0:3], AX.X, ALU.add)
                dve.reciprocal(sm[:, :, 3:5], sm[:, :, 0:2])
                dve.drain()
                dve.tensor_tensor(sm[:, :, 2], sm[:, :, 2], sm[:, :, 3], ALU.mult)
                dve.tensor_tensor(sm[:, :, 5:7], le[:, :, H - 1:H + 1], sm[:, :, 4:5].broadcast_to([P, TT, 2]), ALU.mult)
                dve.drain()
                dve.tensor_tensor(sm[:, :, 0], sm[:, :, 5], sm[:, :, 6], ALU.add)
                dve.tensor_tensor(sm[:, :, 1], sm[:, :, 6], sm[:, :, 2], ALU.mult)
                dve.drain()
                dve.tensor_tensor(sm[:, :, 0], sm[:, :, 0], sm[:, :, 5], ALU.mult)
                dve.tensor_scalar(sm[:, :, 1], sm[:, :, 1], 3.0, None, ALU.mult)
                dve.drain()
                dve.tensor_tensor(sm[:, :, 0], sm[:, :, 0], sm[:, :, 1], ALU.add)
                dve.drain()
                dve.tensor_scalar(sm[:, :, 7], sm[:, :, 0], 2.0, None, ALU.mult)
                dve.drain()

            norm_factors(dve, g, sqrt_in, sqrt_out)
            dve.wait_ge(weights_in, all_in)
            dve.wait_ge(fixed, 3)
            if router:
                dve.wait_ge(softplus, 1)
                dve.tensor_scalar(sp_t[:, 3, :], sp_t[:, 0, :], 0.0, None, ALU.max)
                dve.drain()
                dve.tensor_tensor(spq[:], sp_t[:, 3, :], sp_t[:, 2, :], ALU.add)
                dve.drain()
                qeh = qe[:].rearrange("p (h d) -> p h d", d=hd)
                dve.tensor_tensor(qeh, qeh, spq[:].rearrange("p (h a) -> p h a", a=1).broadcast_to([P, H, hd]), ALU.mult)
                dve.drain()
            def tokens_q(st):
                gp_wait(dve, gp_full, st, "q0", True)
                dve.tensor_tensor(qtm[:], GP[gp.bank["q0"]][:], over_tokens(bqt), ALU.add)\
                   .then_inc(gp_read[gp.bank["q0"]], 1)

            def square_q(st):
                dve.drain()
                dve.tensor_tensor(qsq[:], qtm[:], qtm[:], ALU.mult)
                dve.drain()
                dve.tensor_reduce(qn[:, 0], qsq[:].rearrange("p t (h d) -> p t h d", d=hd), AX.X, ALU.add)\
                   .then_inc(q_sums, 1)

            def scale_q(st):
                dve.wait_ge(q_roots, st.seq(0) + 1)
                dve.reciprocal(qn[:, 2], qn[:, 1])
                dve.drain()
                dve.tensor_tensor(qn[:, 1], qn[:, 2], qn[:, 2], ALU.mult)
                dve.drain()
                dve.tensor_tensor(qn[:, 1], qn[:, 1], qn[:, 0], ALU.mult)
                dve.drain()
                dve.tensor_scalar(qn[:, 1], qn[:, 1], -0.5, 1.5, ALU.mult, ALU.add)
                dve.drain()
                dve.tensor_tensor(qn[:, 2], qn[:, 2], qn[:, 1], ALU.mult)
                dve.drain()
                dve.tensor_tensor(qn[:, 2], qn[:, 2],
                                  spq[:].rearrange("p (a h) -> p a h", a=1).broadcast_to([P, TT, H]), ALU.mult)
                dve.drain()
                qh = qtm[:].rearrange("p t (h d) -> p t h d", d=hd)
                dve.tensor_tensor(qh, qh, qn[:, 2].rearrange("p t (h a) -> p t h a", a=1)
                                  .broadcast_to([P, TT, H, hd]), ALU.mult)
                dve.drain()
                dve.tensor_tensor(qtm[:], qtm[:], over_tokens(qe), ALU.add).then_inc(q_scaled, 1)

            def copy_v(st, i):
                v, u = v2[:, st.half(0)], f"v{i}"
                gp_wait(dve, gp_full, st, u, True)
                if shared_kv:
                    op = dve.tensor_copy(v[:, :, 0, 0:hd], GP[gp.bank[u]][:, :, 0:hd])
                else:
                    hv = D // hd
                    src = GP[gp.bank[u]][:].rearrange("p t (h d) -> p t h d", d=hd)
                    for t in range(TT):
                        dst = v[:, t, i * hv:(i + 1) * hv, 0:hd]
                        if bias:
                            op = dve.tensor_tensor(dst, src[:, t], bv[:].rearrange("p (h d) -> p h d", d=hd), ALU.add)
                        else:
                            op = dve.tensor_copy(dst, src[:, t])
                op.then_inc(gp_read[gp.bank[u]], 1)

            def row_maxima(st, u):
                use = ("max", u)
                pair = sc.bank[use]
                dve.wait_ge(sc_full[pair], sc.after(st.seq(1), use))
                for t in range(TT):
                    keys = (t + 1) * P if causal else S
                    op = dve.tensor_reduce(mx[:, t, 2 * u:2 * u + 2], SC[pair][:, :, t, 0:keys], AX.X, ALU.max,
                                           negate=True)
                op.then_inc(sc_read[pair], 1)

            def split_maxima(st):
                gp_wait(dve, gp_full, st, "neg", True)
                src = GP[gp.bank["neg"]][0:H, 0, :]
                dve.tensor_copy(negT[0:H, :], src)
                dve.drain()
                dve.tensor_tensor(rest[:], src, negT[0:H, :], ALU.subtract)
                dve.drain()
                dve.tensor_copy(negT[32:32 + H, :], rest[:])
                dve.drain()
                dve.tensor_tensor(negT[64:64 + H, :], rest[:], negT[32:32 + H, :], ALU.subtract)\
                   .then_inc(gp_read[gp.bank["neg"]], 1)

            def divide(st, c):
                dve.wait_ge(ot_full[c % 2], ot.after(st.seq(1), c))
                dve.reciprocal(rden[:, c % 2], OT[c % 2][:, 1, :])
                dve.drain()
                dve.tensor_tensor(oT[:, c, :], OT[c % 2][:, 0, :], rden[:, c % 2], ALU.mult).then_inc(ot_read[c % 2], 1)

            def add_y(st):
                gp_wait(dve, gp_read, st, "y", True)
                if router:
                    for t in range(TT):
                        dve.scalar_tensor_tensor(out=yt[:, t], in0=yt[:, t], scalar=sm[:, t, 7:8],
                                                 in1=bo[:], op0=ALU.mult, op1=ALU.add)
                    dve.drain()
                add_to_x(dve, g, st.seq(2), yt[:]).then_inc(y_used, 1)
                if bias and not router:
                    dve.drain()
                    add_to_x(dve, g, st.seq(2), over_tokens(bo))
                dve.drain()
                next_stats(dve, g, st.seq(2))

            def step(st):
                for what, i in order:
                    if not st.has(PART[what]):
                        continue
                    if what == "norm":
                        normalise(dve, g, st.seq(0), xn, xn_ready)
                    elif what == "q" and router:
                        tokens_q(st)
                    elif what == "v":
                        copy_v(st, i)
                    elif what == "max":
                        row_maxima(st, i)
                    elif what == "neg":
                        split_maxima(st)
                        if router and st.has(0):
                            square_q(st)
                    elif what == "scale":
                        if not st.has(1):
                            square_q(st)
                        scale_q(st)
                    elif what == "weigh":
                        divide(st, i)
                    elif what == "logits":
                        gate_logits(st)
                    elif what == "finish":
                        if router:
                            gate_factor(st)
                        add_y(st)
                dve.drain()

            run_steps(dve, step)


def root(dve, out, square, inverse, half):
    dve.tensor_tensor(half, inverse, inverse, ALU.mult)
    dve.drain()
    dve.tensor_tensor(half, half, square, ALU.mult)
    dve.drain()
    dve.tensor_scalar(half, half, -0.5, 1.5, ALU.mult, ALU.add)
    dve.drain()
    dve.tensor_tensor(out, inverse, half, ALU.mult)
    dve.drain()


RETENTION = [("score", 0), ("norm", 0), ("score", 1), ("aT", 0), ("xT", 0), ("score", 2), ("weigh", 0), ("k", 0),
             ("score", 3), ("y", 0), ("score", 4), ("weigh", 1), ("kr", 0), ("q", 0), ("score", 5), ("score", 6),
             ("weigh", 2), ("qr", 0), ("score", 7), ("weigh", 3), ("T0", 0), ("T1", 0), ("group", 0), ("v", 0),
             ("g", 0)]
RETENTION_PART = {"norm": 0, "xT": 0, "q": 0, "k": 0, "qr": 0, "kr": 0, "v": 0, "g": 0,
                  "score": 1, "weigh": 1, "T0": 1, "T1": 1, "group": 1, "aT": 2, "y": 2}


def retention(nc, g, name, w):
    io = g.io
    hd = 16
    CQ, HC, HP, HO, CO = 2, 8, 32, 4, 4
    SU = H // 2
    part_of = RETENTION_PART
    gp = StepBanks([(what, part_of[what]) for what, _ in RETENTION
                    if what not in ("norm", "score", "weigh", "group")])
    sc = Banks(list(range(SU)))
    ot = Banks(list(range(CO)))
    with ExitStack() as ctx:
        sb = lambda n, s, t=F32: ctx.enter_context(nc.sbuf_tensor(f"{name}_sb_{n}", s, t))
        sems, from_one = [], []

        def sem(n, one=False):
            s = ctx.enter_context(nc.semaphore(f"{name}_{n}"))
            (from_one if one else sems).append(s)
            return s
        wq, wk, wv, wg, wo = (sb(n, [P, KD, D]) for n in ("wq", "wk", "wv", "wg", "wo"))
        turn = sb("turn", [P, P])
        mask = sb("mask", [P, HC])
        tri = sb("tri", [P, P])
        tables = sb("tables", [P, 4, CQ, S])
        gb, bo = sb("gb", [P, D]), sb("bo", [P, D])
        xn = sb("xn", [P, TT, D])
        xnT = sb("xnT", [P, KD, S])
        kvT = sb("kvT", [P, KD, S])
        raw = sb("raw", [P, 2, CQ, S])
        qk2 = sb("qk", [P, 2, 2, CQ, S])
        part = sb("part", [P, 2, CQ, S])
        kM2 = sb("kM", [P, 2, H, S])
        v2 = sb("v", [P, 2, TT, H, HP])
        sim = sb("sim", [P, 2, HO, TT, S])
        oraw = sb("oraw", [P, CO, S])
        ret = sb("ret", [P, TT, D])
        sq = sb("sq", [P, TT, D])
        gn = sb("gn", [P, 4, TT, H])
        gz = sb("gz", [P, TT, D])
        gate2 = sb("gate", [P, 2, TT, D])
        aT = sb("aT", [P, KD, S])
        GP = [ctx.enter_context(nc.psum_tensor(f"{name}_gp{i}", [P, 2, S], F32)) for i in range(2)]
        SC = [ctx.enter_context(nc.psum_tensor(f"{name}_sc{i}", [P, 2, 2, S], F32)) for i in range(2)]
        OT = [ctx.enter_context(nc.psum_tensor(f"{name}_ot{i}", [P, 2, S], F32)) for i in range(2)]

        weights_in, kv_in = sem("weights_in"), sem("kv_in")
        sqrt_in, sqrt_out, fixed = sem("sqrt_in"), sem("sqrt_out"), sem("fixed")
        xn_ready, turned, km_ready = sem("xn_ready"), sem("turned"), sem("km_ready")
        gate_z, gate_ready = sem("gate_z"), sem("gate_ready")
        variance, deviation, ret_ready = sem("variance"), sem("deviation"), sem("ret_ready")
        gp_full = [sem(f"gp_full{i}", one=True) for i in range(2)]
        gp_read = [sem(f"gp_read{i}", one=True) for i in range(2)]
        sc_full = [sem(f"sc_full{i}", one=True) for i in range(2)]
        sc_read = [sem(f"sc_read{i}", one=True) for i in range(2)]
        ot_full = [sem(f"ot_full{i}", one=True) for i in range(2)]
        ot_read = [sem(f"ot_read{i}", one=True) for i in range(2)]

        def full(eng, st, u):
            eng.wait_ge(gp_full[gp.bank[u]], gp.after(st, u))

        def free(eng, st, u):
            eng.wait_ge(gp_read[gp.bank[u]], gp.before(st, u))

        def read(eng, st, u):
            eng.wait_ge(gp_read[gp.bank[u]], gp.after(st, u))

        def entries(st):
            return [e for e in RETENTION if st.has(part_of[e[0]])]

        row = lambda a: a.rearrange("(a n) -> a n", a=1).broadcast_to([P, D])
        loads = [(t[:], w[n].rearrange("(k p) n -> p k n", p=P))
                 for t, n in ((wq, "wq"), (wk, "wk"), (wv, "wv"), (wg, "wg"), (wo, "wo"))]
        loads += [(turn[:], io["c_turn"]), (mask[:], io["c_mask16"]), (tri[:], io["c_tri"]),
                  (tables[:], io["c_tables"]), (gb[:], row(w["gb"])), (bo[:], row(w["bo"]))]
        all_in = 16 * len(loads)
        start_semaphores(nc, sems, from_one)
        block = ctx.enter_context(nc.Block())

        @block.sync
        def _(sp):
            for dst, src in loads:
                sp.dma_start(dst, src).then_inc(weights_in, 16)

            def load_context(b):
                sp.dma_start(kvT[:], io["ctxT"][b].rearrange("(k p) s -> p k s", p=P)).then_inc(kv_in, 16)

            load_context(0)
            sp.wait_ge(gp_full[gp.bank["v"]], gp.at_start(Step(1), "v"))
            load_context(1)
            with sp.Fori(0, B - 2) as b:
                sp.wait_ge(gp_full[gp.bank["v"]], b * gp.per("v") + gp.at_start(Step(DEPTH), "v"))
                load_context(b + 2)

        @block.gpsimd
        def _(pool):
            pool.memset(v2[:], 0.0).then_inc(fixed, 1)
            pool.wait_ge(weights_in, all_in)

            def step(st):
                if st.has(0):
                    pool.wait_ge(turned, st.seq(0) * 2 + 1)
                    for c in range(CQ):
                        op = pool.tensor_tensor(kM2[:, st.half(0), c * HC:(c + 1) * HC, :],
                                                qk2[:, st.half(0), 1, c:c + 1, :].broadcast_to([P, HC, S]),
                                                mask[:].rearrange("p (h a) -> p h a", a=1).broadcast_to([P, HC, S]),
                                                ALU.mult)
                    op.then_inc(km_ready, 1)

            run_steps(pool, step)

        @block.scalar
        def _(act):
            norm_sqrt(act, g, sqrt_in, sqrt_out)
            act.wait_ge(fixed, 1)

            def evacuate(dst, st, u):
                full(act, st, u)
                act.activation(dst, GP[gp.bank[u]][:], ACT.Copy).then_inc(gp_read[gp.bank[u]], 1)

            def step(st):
                for what, c in entries(st):
                    if what == "xT":
                        evacuate(xnT[:], st, "xT")
                    elif what == "q":
                        evacuate(raw[:, 0], st, "q")
                    elif what == "k":
                        evacuate(raw[:, 1], st, "k")
                    elif what == "v":
                        full(act, st, "v")
                        for t in range(TT):
                            op = act.activation(v2[:, st.half(0), t, :, 0:hd],
                                                GP[gp.bank["v"]][:, t, :].rearrange("p (h d) -> p h d", d=hd), ACT.Copy)
                        op.then_inc(gp_read[gp.bank["v"]], 1)
                    elif what == "g":
                        act.wait_ge(gate_z, st.seq(0) + 1)
                        act.activation(gate2[:, st.half(0)], gz[:], ACT.Silu).then_inc(gate_ready, 1)
                    elif what == "weigh":
                        act.wait_ge(ot_full[c % 2], ot.after(st.seq(1), c))
                        act.activation(oraw[:, c, :], OT[c % 2][:, 0, :], ACT.Copy).then_inc(ot_read[c % 2], 1)
                    elif what == "group":
                        act.wait_ge(variance, st.seq(1) + 1)
                        act.activation(gn[:, 1], gn[:, 0], ACT.Sqrt).then_inc(deviation, 1)
                    elif what == "aT":
                        evacuate(aT[:], st, "aT")

            run_steps(act, step)

        @block.tensor
        def _(pe):
            pe.wait_ge(weights_in, all_in)
            pe.wait_ge(fixed, 1)

            def feature_major(st, u, wgt, rhs):
                free(pe, st, u)
                for c in range(CQ):
                    for k in range(KD):
                        op = pe.matmul(GP[gp.bank[u]][:, c, :], wgt[:, k, c * P:(c + 1) * P], rhs[:, k, :],
                                       start=(k == 0), stop=(k == KD - 1))
                op.then_inc(gp_full[gp.bank[u]], 1)

            def token_major(st, u, act_T, wgt):
                free(pe, st, u)
                for t in range(TT):
                    for k in range(KD):
                        op = pe.matmul(GP[gp.bank[u]][:, t, :], act_T[:, k, t * P:(t + 1) * P], wgt[:, k, :],
                                       start=(k == 0), stop=(k == KD - 1))
                op.then_inc(gp_full[gp.bank[u]], 1)

            def turn_pairs(st, u, i):
                free(pe, st, u)
                for c in range(CQ):
                    op = pe.matmul(GP[gp.bank[u]][:, c, :], turn[:], raw[:, i, c, :], start=True, stop=True)
                op.then_inc(gp_full[gp.bank[u]], 1)

            def transposed(st, u, src):
                free(pe, st, u)
                transpose_xn(pe, g, src, GP[gp.bank[u]]).then_inc(gp_full[gp.bank[u]], 1)

            def scores(st, u):
                b = st.seq(1)
                pe.wait_ge(sc_read[sc.bank[u]], sc.before(b, u))
                for j in range(2):
                    h = 2 * u + j
                    for t in range(TT):
                        op = pe.matmul(SC[sc.bank[u]][:, j, t, t * P:S], kM2[:, st.half(1), h, t * P:(t + 1) * P],
                                       qk2[:, st.half(1), 0, h // HC, t * P:S], start=True, stop=True)
                op.then_inc(sc_full[sc.bank[u]], 1)

            def weigh(st, c):
                b = st.seq(1)
                for u in (2 * c, 2 * c + 1):
                    pe.wait_ge(sc_read[sc.bank[u]], sc.after(b, u))
                pe.wait_ge(ot_read[c % 2], ot.before(b, c))
                for t in range(TT):
                    for j in range(HO):
                        op = pe.matmul(OT[c % 2][j * HP:(j + 1) * HP, 0, t * P:S], v2[:, st.half(1), t, c * HO + j, :],
                                       sim[:, c % 2, j, t, t * P:S], start=(t == 0), stop=(t == TT - 1))
                op.then_inc(ot_full[c % 2], 1)

            def retained(st, t):
                u = f"T{t}"
                free(pe, st, u)
                flat = GP[gp.bank[u]][:].rearrange("p a n -> p (a n)")
                for c in range(CO):
                    op = pe.transpose(flat[:, c * P:(c + 1) * P], oraw[:, c, t * P:(t + 1) * P], g.ident[:])
                op.then_inc(gp_full[gp.bank[u]], 1)

            def step(st):
                for what, i in entries(st):
                    if what == "xT":
                        pe.wait_ge(xn_ready, st.seq(0) + 1)
                        transposed(st, "xT", xn)
                    elif what == "q":
                        read(pe, st, "xT")
                        feature_major(st, "q", wq, xnT)
                    elif what == "k":
                        pe.wait_ge(kv_in, st.seq(0) * 16 + 16)
                        feature_major(st, "k", wk, kvT)
                    elif what == "kr":
                        read(pe, st, "k")
                        turn_pairs(st, "kr", 1)
                    elif what == "qr":
                        read(pe, st, "q")
                        turn_pairs(st, "qr", 0)
                    elif what == "v":
                        token_major(st, "v", kvT, wv)
                    elif what == "g":
                        token_major(st, "g", xnT, wg)
                    elif what == "score":
                        if i == 0:
                            pe.wait_ge(km_ready, st.seq(1) + 1)
                            pe.wait_ge(turned, st.seq(1) * 2 + 2)
                        scores(st, i)
                    elif what == "weigh":
                        if i == 0:
                            pe.wait_ge(gp_read[gp.bank["v"]], gp.at_start(st, "v"))
                        weigh(st, i)
                    elif what == "T0":
                        for c in (CO - 2, CO - 1):
                            pe.wait_ge(ot_read[c % 2], ot.after(st.seq(1), c))
                        retained(st, 0)
                    elif what == "T1":
                        retained(st, 1)
                    elif what == "aT":
                        pe.wait_ge(ret_ready, st.seq(2) + 1)
                        transposed(st, "aT", ret)
                    elif what == "y":
                        read(pe, st, "aT")
                        token_major(st, "y", aT, wo)

            run_steps(pe, step)

        @block.vector
        def _(dve):
            rows = lambda a: a[:].rearrange("p (a n) -> p a n", a=1).broadcast_to([P, TT, D])
            heads = lambda a: a[:].rearrange("p t (h d) -> p (t h) d", d=hd)
            per_head = lambda a: a.rearrange("p t (h a) -> p (t h) a", a=1).broadcast_to([P, TT * H, hd])
            norm_factors(dve, g, sqrt_in, sqrt_out)
            dve.wait_ge(weights_in, all_in)
            dve.wait_ge(fixed, 1)

            def turn(st, i, u, src):
                read(dve, st, src)
                dve.tensor_tensor(part[:, 0], raw[:, i], tables[:, 2 * i], ALU.mult)
                full(dve, st, u)
                dve.tensor_tensor(part[:, 1], GP[gp.bank[u]][:], tables[:, 2 * i + 1], ALU.mult)\
                   .then_inc(gp_read[gp.bank[u]], 1)
                dve.drain()
                dve.tensor_tensor(qk2[:, st.half(0), i], part[:, 0], part[:, 1], ALU.add).then_inc(turned, 1)
                dve.drain()

            def keep_triangle(st, u):
                b, c = st.seq(1), u // 2
                if u % 2 == 0:
                    dve.wait_ge(ot_full[c % 2], ot.before(b, c))
                dve.wait_ge(sc_full[sc.bank[u]], sc.after(b, u))
                dst = sim[:, c % 2, 2 * (u % 2):2 * (u % 2) + 2]
                src = SC[sc.bank[u]]
                for t in range(TT):
                    dve.tensor_tensor(dst[:, :, t, t * P:(t + 1) * P], src[:, :, t, t * P:(t + 1) * P],
                                      tri[:].rearrange("p (a n) -> p a n", a=1).broadcast_to([P, 2, P]), ALU.mult)
                dve.tensor_copy(dst[:, :, 0, P:S], src[:, :, 0, P:S]).then_inc(sc_read[sc.bank[u]], 1)
                dve.drain()

            def group_norm(st):
                dve.drain()
                dve.tensor_reduce(gn[:, 0].rearrange("p t h -> p (t h)"), heads(ret), AX.X, ALU.add)
                dve.drain()
                dve.tensor_scalar(gn[:, 0], gn[:, 0], 1.0 / hd, None, ALU.mult)
                dve.drain()
                dve.tensor_tensor(heads(ret), heads(ret), per_head(gn[:, 0]), ALU.subtract)
                dve.drain()
                dve.tensor_tensor(sq[:], ret[:], ret[:], ALU.mult)
                dve.drain()
                dve.tensor_reduce(gn[:, 0].rearrange("p t h -> p (t h)"), heads(sq), AX.X, ALU.add)
                dve.drain()
                dve.tensor_scalar(gn[:, 0], gn[:, 0], 1.0 / hd, EPS, ALU.mult, ALU.add).then_inc(variance, 1)
                dve.wait_ge(deviation, st.seq(1) + 1)
                dve.reciprocal(gn[:, 2], gn[:, 1])
                dve.drain()
                root(dve, gn[:, 2], gn[:, 0], gn[:, 2], gn[:, 3])
                dve.tensor_tensor(heads(ret), heads(ret), per_head(gn[:, 2]), ALU.mult)
                dve.drain()
                dve.wait_ge(gate_ready, st.seq(1) + 1)
                dve.tensor_tensor(ret[:], ret[:], gate2[:, st.half(1)], ALU.mult).then_inc(ret_ready, 1)

            def step(st):
                for what, i in entries(st):
                    if what == "norm":
                        normalise(dve, g, st.seq(0), xn, xn_ready)
                    elif what == "kr":
                        turn(st, 1, "kr", "k")
                    elif what == "qr":
                        turn(st, 0, "qr", "q")
                    elif what == "g":
                        full(dve, st, "g")
                        dve.tensor_tensor(gz[:], GP[gp.bank["g"]][:], rows(gb), ALU.add)\
                           .then_inc(gp_read[gp.bank["g"]], 1)
                        dve.drain()
                        dve.sem_inc(gate_z, 1)
                    elif what == "score":
                        keep_triangle(st, i)
                    elif what in ("T0", "T1"):
                        full(dve, st, what)
                        src = GP[gp.bank[what]][:].rearrange("p a n -> p (a n)")
                        src = src.rearrange("p (h e) -> p h e", e=HP)[:, :, 0:hd]
                        dve.tensor_copy(ret[:, int(what[1]), :].rearrange("p (h d) -> p h d", d=hd), src)\
                           .then_inc(gp_read[gp.bank[what]], 1)
                    elif what == "group":
                        group_norm(st)
                    elif what == "y":
                        full(dve, st, "y")
                        add_to_x(dve, g, st.seq(2), GP[gp.bank["y"]][:]).then_inc(gp_read[gp.bank["y"]], 1)
                        dve.drain()
                        add_to_x(dve, g, st.seq(2), rows(bo))
                        dve.drain()
                        next_stats(dve, g, st.seq(2))
                dve.drain()

            run_steps(dve, step)


def truncated_experts(nc, g, name, w):
    io = g.io
    E = 8
    hb = Banks(list(range(E)))
    with ExitStack() as ctx:
        sb = lambda n, s, t=F32: ctx.enter_context(nc.sbuf_tensor(f"{name}_sb_{n}", s, t))
        sems, from_one = [], []

        def sem(n, one=False):
            s = ctx.enter_context(nc.semaphore(f"{name}_{n}"))
            (from_one if one else sems).append(s)
            return s
        wr, ws1, ws2 = sb("wr", [P, KD, E]), sb("ws1", [P, KD, P]), sb("ws2", [P, D])
        w1, w2 = sb("w1", [P, E, KD, P]), sb("w2", [P, E, D])
        sel = sb("sel", [P, H, P], BF16)
        ones = sb("ones", [P, P])
        xn, xnT = sb("xn", [P, NT, D]), sb("xnT", [P, KD, B * S])
        logit, top, gap, ex, c = (sb(n, [P, NT, E]) for n in ("logit", "top", "gap", "ex", "c"))
        first = sb("first", [P, 2, NT])
        any_c = sb("any_c", [P, E])
        flag = sb("flag", [P, 1], mybir.dt.int32)
        s_act, s_hT = sb("s_act", [P, 2, S]), sb("s_hT", [P, 2, S])
        c_seq, cTb = sb("c_seq", [P, TT, E]), sb("cTb", [P, S], BF16)
        act_out, hc, hT = (sb(n, [P, 2, S]) for n in ("act_out", "hc", "hT"))
        ps = lambda n: ctx.enter_context(nc.psum_tensor(f"{name}_{n}", [P, 2, S], F32))
        GP, HB, YB, CB = ([ps(f"{n}{i}") for i in range(2)] for n in ("gp", "hb", "yb", "cb"))
        LG = CB[0]

        router_in, routed_in = sem("router_in"), sem("routed_in")
        sqrt_in, sqrt_out, fixed = sem("sqrt_in"), sem("sqrt_out"), sem("fixed")
        xn_ready, xn_turned, xnT_ready = sem("xn_ready"), sem("xn_turned"), sem("xnT_ready")
        logits_full, gap_ready, exp_ready = sem("logits_full"), sem("gap_ready"), sem("exp_ready")
        any_ready, any_summed = sem("any_ready"), sem("any_summed")
        two = lambda n, one=False: [sem(f"{n}{i}", one) for i in range(2)]
        s_full, s_relu, s_ready, s_y_full, s_y_read = (two("s_full", True), two("s_relu", True), two("s_ready", True),
                                                       two("s_y_full", True), two("s_y_read", True))
        c_ready, cT_full, cT_read = sem("c_ready"), sem("cT_full"), sem("cT_read")
        hb_full, act_ready, hb_read, cb_full, h_ready, h_used = (
            two(n, True) for n in ("hb_full", "act_ready", "hb_read", "cb_full", "h_ready", "h_used"))
        y_read = sem("y_read", one=True)
        start_semaphores(nc, sems, from_one)

        with nc.Block() as block:
            @block.sync
            def _(sp):
                for dst, src in ((wr, w["wr"].rearrange("(k p) n -> p k n", p=P)), (ws1, w["ws1"]), (ws2, w["ws2"])):
                    sp.dma_start(dst[:], src).then_inc(router_in, 16)

            @block.gpsimd
            def _(pool):
                pool.memset(ones[:], 1.0).then_inc(fixed, 1)
                pool.memset(cTb[:], 0.0).then_inc(fixed, 1)

            @block.scalar
            def _(act):
                norm_sqrt(act, g, sqrt_in, sqrt_out)
                for b in range(B):
                    act.wait_ge(xn_turned, b + 1)
                    act.activation(xnT[:, :, b * S:(b + 1) * S], GP[b % 2][:], ACT.Copy).then_inc(xnT_ready, 1)
                with act.Fori(0, B // 2) as i:
                    for j in range(2):
                        act.wait_ge(s_full[j], i + 2)
                        act.wait_ge(s_ready[j], i + 1)
                        act.activation(s_act[:, j], HB[j][:, 0], ACT.Relu).then_inc(s_relu[j], 1)
                act.wait_ge(gap_ready, 1)
                act.activation(ex[:], gap[:], ACT.Exp).then_inc(exp_ready, 1)

            @block.tensor
            def _(pe):
                pe.wait_ge(router_in, 16 * 3)
                logits = LG[:].rearrange("p a n -> p (a n)")
                for b in range(B + 1):
                    if b < B:
                        pe.wait_ge(xn_ready, b + 1)
                        if b >= 2:
                            pe.wait_ge(xnT_ready, b - 1)
                        transpose_xn(pe, g, xn[:, b * TT:(b + 1) * TT, :], GP[b % 2]).then_inc(xn_turned, 1)
                    if b:
                        pe.wait_ge(xnT_ready, b)
                        for t in range((b - 1) * TT, b * TT):
                            for k in range(KD):
                                op = pe.matmul(logits[:, t * E:(t + 1) * E], xnT[:, k, t * P:(t + 1) * P], wr[:, k, :],
                                               start=(k == 0), stop=(k == KD - 1))
                op.then_inc(logits_full, 1)

                def shared_hidden(b, i, j):
                    pe.wait_ge(s_ready[j], i + 1)
                    for k in range(KD):
                        op = pe.matmul(HB[j][:, 0], ws1[:, k, :], xnT[:, k, bass.ds(b * S, S)],
                                       start=(k == 0), stop=(k == KD - 1))
                    op.then_inc(s_full[j], 1)

                def shared_out(i, j):
                    pe.wait_ge(s_ready[j], i + 2)
                    pe.wait_ge(s_y_read[j], i + 1)
                    for t in range(TT):
                        op = pe.matmul(YB[j][:, t], s_hT[:, j, t * P:(t + 1) * P], ws2[:], start=True, stop=True)
                    op.then_inc(s_y_full[j], 1)

                with pe.Fori(0, B // 2) as i:
                    for j in range(2):
                        shared_hidden(i * 2 + j, i, j)
                    for j in range(2):
                        shared_out(i, j)
                pe.wait_ge(any_ready, 1)
                pe.wait_ge(fixed, 2)
                pe.matmul(GP[0][:, 0, 0:E], ones[:], any_c[:], start=True, stop=True).then_inc(any_summed, 1)

            @block.vector
            def _(dve):
                wide = lambda a: a.rearrange("p (t a) -> p t a", a=1).broadcast_to([P, NT, E])
                norm_factors(dve, g, sqrt_in, sqrt_out)
                for t in range(NT):
                    op = dve.tensor_scalar(xn[:, t, :], g.x[:, t, :], g.mean[:, t:t + 1], g.rstd[:, t:t + 1],
                                           ALU.subtract, ALU.mult)
                    if t % TT == TT - 1:
                        op.then_inc(xn_ready, 1)
                dve.wait_ge(logits_full, 1)
                dve.tensor_copy(logit[:], LG[:].rearrange("p a n -> p (a n)")[:, 0:NT * E]
                                .rearrange("p (t e) -> p t e", e=E))
                with dve.Fori(0, B // 2) as i:
                    for j in range(2):
                        dve.wait_ge(s_relu[j], i + 2)
                        dve.wait_ge(s_y_full[j], i + 1)
                        dve.scalar_tensor_tensor(out=s_hT[:, j], in0=HB[j][:, 0], scalar=0.0, in1=s_act[:, j],
                                                 op0=ALU.max, op1=ALU.mult).then_inc(s_ready[j], 1)
                    for j in range(2):
                        dve.wait_ge(s_y_full[j], i + 2)
                        add_to_x(dve, g, i * 2 + j, YB[j][:]).then_inc(s_y_read[j], 1)
                dve.drain()
                for t in range(NT):
                    dve.max(top[:, t, :], logit[:, t, :])
                dve.drain()
                dve.tensor_tensor(gap[:], top[:], top[:, :, 0:1].broadcast_to([P, NT, E]), ALU.subtract)\
                   .then_inc(gap_ready, 1)
                dve.wait_ge(exp_ready, 1)
                dve.tensor_scalar(first[:, 0], ex[:, :, 1], 1.0, None, ALU.add)
                dve.drain()
                dve.reciprocal(first[:, 1], first[:, 0])
                dve.drain()
                dve.tensor_scalar(first[:, 1], first[:, 1], 1.0, None, ALU.is_ge)
                dve.tensor_tensor(c[:], logit[:], top[:, :, 0:1].broadcast_to([P, NT, E]), ALU.is_ge)
                dve.drain()
                dve.tensor_tensor(c[:], c[:], wide(first[:, 1]), ALU.mult)
                dve.drain()
                dve.tensor_reduce(any_c[:], c[:].rearrange("p t e -> p e t"), AX.X, ALU.max).then_inc(any_ready, 1)
                dve.wait_ge(any_summed, 1)
                dve.tensor_reduce(first[:, 0, 0:1], GP[0][:, 0, 0:E], AX.X, ALU.add)
                dve.drain()
                dve.tensor_copy(flag[:], first[:, 0, 0:1])
                dve.drain()

        def any_weight(eng):
            return eng.If(eng.value_load(flag[0:1, 0:1], min_val=0, max_val=P * E) > 0)

        with nc.Block() as block:
            @block.sync
            def _(sp):
                with any_weight(sp):
                    for dst, src in ((w1, w["w1"]), (w2, w["w2"]), (sel, io["c_sel"])):
                        sp.dma_start(dst[:], src).then_inc(routed_in, 16)

            @block.scalar
            def _(act):
                with any_weight(act):
                    with act.Fori(0, B) as b:
                        for e in range(E):
                            i = e % 2
                            act.wait_ge(hb_full[i], hb.after(b, e))
                            act.wait_ge(hb_read[i], hb.before(b, e))
                            act.activation(act_out[:, i], HB[i][:, 0], ACT.Relu).then_inc(act_ready[i], 1)

            @block.tensor
            def _(pe):
                with any_weight(pe):
                    pe.wait_ge(routed_in, 16 * 3)
                    with pe.Fori(0, B) as b:
                        pe.wait_ge(c_ready, b + 1)
                        for t in range(TT):
                            op = pe.transpose(GP[0][0:E, 0, t * P:(t + 1) * P], c_seq[:, t, :], g.ident[:])
                        op.then_inc(cT_full, 1)
                        pe.wait_ge(cT_read, b + 1)

                        def out(e):
                            i = e % 2
                            pe.wait_ge(h_ready[i], hb.after(b, e))
                            for t in range(TT):
                                op = pe.matmul(YB[t][:, 0], hT[:, i, t * P:(t + 1) * P], w2[:, e, :], start=(e == 0),
                                               stop=(e == E - 1))
                            op.then_inc(h_used[i], 1)

                        for e in range(E):
                            i = e % 2
                            pe.wait_ge(h_ready[i], hb.before(b, e))
                            pe.matmul(CB[i][:, 0], sel[:, e, :], cTb[:], start=True, stop=True).then_inc(cb_full[i], 1)
                            pe.wait_ge(hb_read[i], hb.before(b, e))
                            for k in range(KD):
                                op = pe.matmul(HB[i][:, 0], w1[:, e, k, :], xnT[:, k, bass.ds(b * S, S)],
                                               start=(k == 0), stop=(k == KD - 1))
                            op.then_inc(hb_full[i], 1)
                            if e == 1:
                                pe.wait_ge(y_read, b + 1)
                            if e:
                                out(e - 1)
                        out(E - 1)

            @block.vector
            def _(dve):
                with any_weight(dve):
                    with dve.Fori(0, B) as b:
                        dve.tensor_copy(c_seq[:], c[:, bass.ds(b * TT, TT), :]).then_inc(c_ready, 1)
                        dve.wait_ge(cT_full, b + 1)
                        dve.tensor_copy(cTb[0:E, :], GP[0][0:E, 0, :]).then_inc(cT_read, 1)
                        for e in range(E):
                            i = e % 2
                            dve.wait_ge(act_ready[i], hb.after(b, e))
                            dve.scalar_tensor_tensor(out=hc[:, i], in0=HB[i][:, 0], scalar=0.0, in1=act_out[:, i],
                                                     op0=ALU.max, op1=ALU.mult).then_inc(hb_read[i], 1)
                            dve.drain()
                            dve.wait_ge(h_used[i], hb.before(b, e))
                            dve.wait_ge(cb_full[i], hb.after(b, e))
                            dve.tensor_tensor(hT[:, i], hc[:, i], CB[i][:, 0], ALU.mult).then_inc(h_ready[i], 1)
                        dve.wait_ge(h_used[(E - 1) % 2], hb.after(b, E - 1))
                        for t in range(TT):
                            xt = g.x[:, bass.ds(b * TT + t, 1), :].rearrange("p a n -> p (a n)")
                            op = dve.tensor_tensor(xt, xt, YB[t][:, 0], ALU.add)
                        op.then_inc(y_read, 1)
                        dve.drain()


def pick_two(dve, s, descending, tmp, red, picked):
    wide = lambda a: a.rearrange("p (t a) -> p t a", a=1).broadcast_to(list(s.shape))
    order = descending.rearrange("p (a n) -> p a n", a=1).broadcast_to(list(s.shape))
    for r in range(2):
        dve.tensor_reduce(red[:, 0], s, AX.X, ALU.max)
        dve.drain()
        dve.tensor_tensor(tmp, s, wide(red[:, 0]), ALU.is_ge)
        dve.drain()
        dve.tensor_tensor(tmp, tmp, order, ALU.mult)
        dve.drain()
        dve.tensor_reduce(red[:, 1], tmp, AX.X, ALU.max)
        dve.drain()
        dve.tensor_tensor(picked[r], tmp, wide(red[:, 1]), ALU.is_equal)
        dve.drain()
        if r == 0:
            dve.scalar_tensor_tensor(out=s, in0=picked[0], scalar=-3e38, in1=s, op0=ALU.mult, op1=ALU.add)
            dve.drain()


SLOT_STEPS = [("turn", 0), ("turn", 1), ("hidden", 0), ("turn", 2), ("hidden", 1), ("gate", 0), ("turn", 3),
              ("hidden", 2), ("gate", 1), ("turn_h", 0), ("hidden", 3), ("gate", 2), ("turn_h", 1), ("out", 0),
              ("gate", 3), ("turn_h", 2), ("out", 1), ("turn_h", 3), ("out", 2), ("out", 3)]


def sorted_gated_experts(nc, g, name, w):
    io = g.io
    E, G, SH = 16, 4, 2
    NS = 48
    U = 8
    PAIRS = U // 2
    ST = NT
    with ExitStack() as ctx:
        sb = lambda n, s, t=F32: ctx.enter_context(nc.sbuf_tensor(f"{name}_sb_{n}", s, t))
        sems, from_one = [], []

        def sem(n, one=False):
            s = ctx.enter_context(nc.semaphore(f"{name}_{n}"))
            (from_one if one else sems).append(s)
            return s
        x_slots = nc.dram_tensor(f"{name}_x_slots", (NS * P, D), F32).ap()
        y_slots = nc.dram_tensor(f"{name}_y_slots", (NS * P, D), F32).ap()
        wr, br = sb("wr", [P, KD, E]), sb("br", [P, E])
        w13 = sb("w13", [P, E, KD, 2 * P])
        w2 = sb("w2", [P, E, D])
        b13, b2 = sb("b13", [P, E, 2 * P]), sb("b2", [P, E, D])
        ws13 = sb("ws13", [P, SH, 2, KD, P])
        ws2 = sb("ws2", [P, SH, D])
        bs1, bs3, bs2 = sb("bs1", [P, SH]), sb("bs3", [P, SH]), sb("bs2", [P, D])
        before_p, ones = sb("before_p", [P, P]), sb("ones", [P, P])
        earlier = sb("earlier", [P, E, E])
        descending = sb("descending", [P, E])
        steps = sb("steps", [P, ST])
        zero = sb("zero", [P, D])
        xn = sb("xn", [P, NT, D])
        xnT = sb("xnT", [P, KD, B * S])
        rows = [xn[:], xnT[:].rearrange("p k s -> p (k s)").rearrange("p (t d) -> p t d", d=D)]
        lg, ex, score, tmp = (sb(n, [P, NT, E]) for n in ("lg", "ex", "score", "tmp"))
        red, red2 = sb("red", [P, 2, NT]), sb("red2", [P, 2, NT * G])
        pairs = sb("pairs", [P, NT * G, 6])
        gs, gtmp, keep = sb("gs", [P, NT, G]), sb("gtmp", [P, NT, G]), sb("keep", [P, 2, NT, G])
        picked = sb("picked", [P, 2, NT, E])
        both = sb("both", [P, NT, E])
        weight = sb("weight", [P, 2, NT])
        pre, tot, run = sb("pre", [P, NT, E]), sb("tot", [P, NT, E]), sb("run", [P, 2, NT, E])
        tiles = sb("tiles", [P, 3, E])
        cmp2, cmp3, cmp4 = sb("cmp2", [P, E, ST]), sb("cmp3", [P, NS, E]), sb("cmp4", [P, E, E])
        posf = sb("posf", [P, 2, NT])
        pos = sb("pos", [P, 2, NT], mybir.dt.int32)
        slotf, slot = sb("slotf", [P, NS]), sb("slot", [P, NS], mybir.dt.int32)
        s_act, s_lin, s_hT = sb("s_act", [P, SH, S]), sb("s_lin", [P, SH, S]), sb("s_hT", [P, SH, S])
        s_y = sb("s_y", [P, TT, D])
        xs, xsT = sb("xs", [P, U, D]), sb("xsT", [P, U, KD * P])
        hb, hm, hmT = sb("hb", [P, U, 2 * P]), sb("hm", [P, U, P]), sb("hmT", [P, U, P])
        ys = sb("ys", [P, U, D])
        ps = lambda n: ctx.enter_context(nc.psum_tensor(f"{name}_{n}", [P, 2, S], F32))
        GP, HB, YB = [ps("gp0"), ps("gp1")], [ps("hb0"), ps("hb1")], [ps("yb0"), ps("yb1")]
        HT = LG, CT = ps("lg"), ps("ct")

        router_in, shared_in, experts_in = sem("router_in"), sem("shared_in"), sem("experts_in")
        sqrt_in, sqrt_out, fixed, cleared = sem("sqrt_in"), sem("sqrt_out"), sem("fixed"), sem("cleared")
        xn_ready, xn_turned, xnT_ready = sem("xn_ready"), sem("xn_turned"), sem("xnT_ready")
        logits_full, shifted, exp_ready = sem("logits_full"), sem("shifted"), sem("exp_ready")
        both_ready, counted, routed = sem("both_ready"), sem("counted"), sem("routed")
        s_full = [sem(f"s_full{e}") for e in range(SH)]
        s_evacuated = [sem(f"s_evacuated{e}", one=True) for e in range(SH)]
        s_product = [sem(f"s_product{e}", one=True) for e in range(SH)]
        s_y_full, s_y_copied, s_y_added = (sem("s_y_full", one=True), sem("s_y_copied", one=True),
                                           sem("s_y_added", one=True))
        scattered, gathered = g.moved[0][0], g.moved[0][1:]
        each = lambda n, one=False: [sem(f"{n}{q}", one) for q in range(PAIRS)]
        x_in, xT_ready, h_full, h_biased, h_act, h_ready, hT_full, hT_ready, y_full = (
            each(n) for n in ("x_in", "xT_ready", "h_full", "h_biased", "h_act", "h_ready", "hT_full", "hT_ready",
                              "y_full"))
        turned, y_ready, y_stored = (each(n, one=True) for n in ("turned", "y_ready", "y_stored"))
        start_semaphores(nc, sems, from_one)
        block = ctx.enter_context(nc.Block())
        row = lambda a, n: a.rearrange("(a n) -> a n", a=1).broadcast_to([P, n])
        table = lambda a: a.rearrange("(a e) n -> a e n", a=1).broadcast_to([P, E, 2 * P])

        def shared_values(eng, b):
            for e in range(SH):
                eng.wait_ge(s_evacuated[e], b + 2)
                eng.wait_ge(s_y_full, b + 1)
                eng.tensor_tensor(s_hT[:, e], s_act[:, e], s_lin[:, e], ALU.mult).then_inc(s_product[e], 1)
            eng.wait_ge(s_y_copied, b + 2)
            xb = g.x[:, bass.ds(b * TT, TT), :]
            eng.tensor_tensor(xb, xb, s_y[:], ALU.add).then_inc(s_y_added, 1)

        slots = lambda a, i, q: a[bass.ds((i * U + 2 * q) * P, 2 * P), :].rearrange("(j p) d -> p j d", p=P)

        @block.sync
        def _(sp):
            for dst, src in ((wr, w["wr"].rearrange("(k p) n -> p k n", p=P)), (br, row(w["br"], E)),
                             (before_p, io["c_before"]), (descending, io["c_descending"]),
                             (earlier, io["c_earlier"]), (steps, io["c_steps"][:, 0:ST])):
                sp.dma_start(dst[:], src).then_inc(router_in, 16)
            for dst, src in ((ws13, w["ws13"]), (ws2, w["ws2"]), (bs1, w["bs1"]), (bs3, w["bs3"]),
                             (bs2, row(w["bs2"], D))):
                sp.dma_start(dst[:], src).then_inc(shared_in, 16)
            sp.wait_ge(fixed, 1)
            sp.dma_start(x_slots.rearrange("(n p) d -> p n d", p=P),
                         zero[:].rearrange("p (a d) -> p a d", a=1).broadcast_to([P, NS, D])).then_inc(cleared, 16)
            for dst, src in ((w13, w["w13"]), (w2, w["w2"]), (b13, table(w["b13"])), (b2, table(w["b2"]))):
                sp.dma_start(dst[:], src).then_inc(experts_in, 16)
            sp.wait_ge(scattered, 16 * 2 * NT)
            with sp.Fori(0, NS // U) as i:
                for q in range(PAIRS):
                    sp.wait_ge(turned[q], i + 1)
                    sp.dma_start(xs[:, 2 * q:2 * q + 2, :], slots(x_slots, i, q)).then_inc(x_in[q], 16)

        @block.gpsimd
        def _(pool):
            pool.memset(zero[:], 0.0).then_inc(fixed, 1)
            pool.memset(ones[:], 1.0).then_inc(fixed, 1)
            with pool.Fori(0, B // 2) as b:
                shared_values(pool, b)
            pool.wait_ge(cleared, 16)
            pool.wait_ge(routed, 1)
            for i in range(2):
                for t in range(NT):
                    pool.indirect_dma_start(x_slots, bass.IndirectOffsetOnAxis(pos[:, i, t:t + 1], 0), xn[:, t, :], None)\
                        .then_inc(scattered, 16)
            for q in range(PAIRS):
                pool.wait_ge(y_stored[q], 16 * (NS // U) + 1)
            for half_ in range(2):
                for t in range(half_ * NT // 2, (half_ + 1) * NT // 2):
                    for i in range(2):
                        pool.indirect_dma_start(rows[i][:, t, :], None, y_slots,
                                                bass.IndirectOffsetOnAxis(pos[:, i, t:t + 1], 0))\
                            .then_inc(gathered[half_], 16)

        @block.scalar
        def _(act):
            norm_sqrt(act, g, sqrt_in, sqrt_out)
            for b in range(B):
                act.wait_ge(xn_turned, b + 1)
                act.activation(xnT[:, :, b * S:(b + 1) * S], GP[b % 2][:], ACT.Copy).then_inc(xnT_ready, 1)
            act.wait_ge(shifted, 1)
            act.activation(ex[:], lg[:], ACT.Exp).then_inc(exp_ready, 1)
            act.wait_ge(shared_in, 16 * 5)
            with act.Fori(0, B) as b:
                for e in range(SH):
                    act.wait_ge(s_full[e], b + 1)
                    act.wait_ge(s_product[e], b + 1)
                    act.activation(s_act[:, e], HB[e][:, 0], ACT.Silu, bias=bs1[:, e:e + 1])
                    act.activation(s_lin[:, e], HB[e][:, 1], ACT.Identity, bias=bs3[:, e:e + 1])\
                       .then_inc(s_evacuated[e], 1)
                act.wait_ge(s_y_full, b + 2)
                act.wait_ge(s_y_added, b + 1)
                for t in range(TT):
                    op = act.activation(s_y[:, t], YB[t][:, 0], ACT.Copy)
                op.then_inc(s_y_copied, 1)
            with act.Fori(0, NS // U) as i:
                for what, q in SLOT_STEPS:
                    pair = slice(2 * q, 2 * q + 2)
                    if what == "turn":
                        act.wait_ge(turned[q], i + 2)
                        act.activation(xsT[:, pair], GP[q % 2][:], ACT.Copy).then_inc(xT_ready[q], 1)
                    elif what == "gate":
                        act.wait_ge(h_biased[q], i + 1)
                        act.activation(hm[:, pair], hb[:, pair, 0:P], ACT.Silu).then_inc(h_act[q], 1)
                    elif what == "turn_h":
                        act.wait_ge(hT_full[q], i + 1)
                        act.activation(hmT[:, pair], HT[q % 2][:, 0, :].rearrange("p (j n) -> p j n", n=P), ACT.Copy)\
                           .then_inc(hT_ready[q], 1)
                for q in range(PAIRS):
                    act.wait_ge(y_ready[q], i + 2)
                    act.dma_start(slots(y_slots, i, q), ys[:, 2 * q:2 * q + 2, :]).then_inc(y_stored[q], 16)

        @block.tensor
        def _(pe):
            pe.wait_ge(router_in, 16 * 6)
            logits = LG[:].rearrange("p a n -> p (a n)")
            for b in range(B + 1):
                if b < B:
                    pe.wait_ge(xn_ready, b + 1)
                    if b >= 2:
                        pe.wait_ge(xnT_ready, b - 1)
                    transpose_xn(pe, g, xn[:, b * TT:(b + 1) * TT, :], GP[b % 2]).then_inc(xn_turned, 1)
                if b:
                    pe.wait_ge(xnT_ready, b)
                    for t in range((b - 1) * TT, b * TT):
                        for k in range(KD):
                            op = pe.matmul(logits[:, t * E:(t + 1) * E], xnT[:, k, t * P:(t + 1) * P], wr[:, k, :],
                                           start=(k == 0), stop=(k == KD - 1))
            op.then_inc(logits_full, 1)
            pe.wait_ge(shared_in, 16 * 5)

            def shared(b):
                for e in range(SH):
                    pe.wait_ge(s_evacuated[e], b + 1)
                    for x in range(2):
                        for k in range(KD):
                            op = pe.matmul(HB[e][:, x], ws13[:, e, x, k, :], xnT[:, k, bass.ds(b * S, S)],
                                           start=(k == 0), stop=(k == KD - 1))
                    op.then_inc(s_full[e], 1)
                pe.wait_ge(s_y_copied, b + 1)
                for e in range(SH):
                    pe.wait_ge(s_product[e], b + 2)
                    for t in range(TT):
                        op = pe.matmul(YB[t][:, 0], s_hT[:, e, t * P:(t + 1) * P], ws2[:, e, :],
                                       start=(e == 0), stop=(e == SH - 1))
                op.then_inc(s_y_full, 1)

            with pe.Fori(0, B // 4) as b:
                shared(b)
            pe.wait_ge(both_ready, 1)
            pe.wait_ge(fixed, 2)
            flat = both[:].rearrange("p t e -> p (t e)")
            pe.matmul(CT[:, 0, :], before_p[:], flat, start=True, stop=True)
            pe.matmul(CT[:, 1, :], ones[:], flat, start=True, stop=True).then_inc(counted, 1)
            with pe.Fori(B // 4, B) as b:
                shared(b)
            pe.wait_ge(s_y_copied, B + 1)
            pe.wait_ge(experts_in, 16 * 4)
            pe.wait_ge(routed, 1)
            with pe.Fori(0, NS // U) as i:
                for what, q in SLOT_STEPS:
                    if what == "turn":
                        pe.wait_ge(x_in[q], i * 16 + 16)
                        if q >= 2:
                            pe.wait_ge(xT_ready[q - 2], i + 1)
                        for j in range(2):
                            for k in range(KD):
                                op = pe.transpose(GP[q % 2][:, j, k * P:(k + 1) * P],
                                                  xs[:, 2 * q + j, k * P:(k + 1) * P], g.ident[:])
                        op.then_inc(turned[q], 1)
                        if q == 1:
                            e = [pe.value_load(slot[0:1, bass.ds(i * U + j, 1)], min_val=0, max_val=E - 1)
                                 for j in range(U)]
                    elif what == "hidden":
                        pe.wait_ge(xT_ready[q], i + 1)
                        if q >= 2:
                            pe.wait_ge(h_biased[q - 2], i + 1)
                        for j in range(2):
                            for k in range(KD):
                                op = pe.matmul(HB[q % 2][:, j], xsT[:, 2 * q + j, k * P:(k + 1) * P],
                                               w13[:, bass.ds(e[2 * q + j], 1), k, :].rearrange("p a n -> p (a n)"),
                                               start=(k == 0), stop=(k == KD - 1))
                        op.then_inc(h_full[q], 1)
                    elif what == "turn_h":
                        pe.wait_ge(h_ready[q], i + 1)
                        if q >= 2:
                            pe.wait_ge(hT_ready[q - 2], i + 1)
                        for j in range(2):
                            op = pe.transpose(HT[q % 2][:, 0, j * P:(j + 1) * P], hm[:, 2 * q + j], g.ident[:])
                        op.then_inc(hT_full[q], 1)
                    elif what == "out":
                        pe.wait_ge(hT_ready[q], i + 1)
                        pe.wait_ge(y_ready[(q + 2) % PAIRS], i + 1 + q // 2)
                        for j in range(2):
                            op = pe.matmul(YB[q % 2][:, j], hmT[:, 2 * q + j],
                                           w2[:, bass.ds(e[2 * q + j], 1), :].rearrange("p a n -> p (a n)"),
                                           start=True, stop=True)
                        op.then_inc(y_full[q], 1)

        @block.vector
        def _(dve):
            wide = lambda a, n: a.rearrange("p (t a) -> p t a", a=1).broadcast_to([P, NT, n])
            norm_factors(dve, g, sqrt_in, sqrt_out)
            for t in range(NT):
                op = dve.tensor_scalar(xn[:, t, :], g.x[:, t, :], g.mean[:, t:t + 1], g.rstd[:, t:t + 1],
                                       ALU.subtract, ALU.mult)
                if t % TT == TT - 1:
                    op.then_inc(xn_ready, 1)
            dve.wait_ge(router_in, 16 * 6)
            dve.wait_ge(logits_full, 1)
            src = LG[:].rearrange("p a n -> p (a n)")[:, 0:NT * E].rearrange("p (t e) -> p t e", e=E)
            dve.tensor_reduce(red[:, 0], src, AX.X, ALU.max)
            dve.drain()
            dve.tensor_tensor(lg[:], src, wide(red[:, 0], E), ALU.subtract).then_inc(shifted, 1)
            dve.wait_ge(exp_ready, 1)
            dve.tensor_reduce(red[:, 0], ex[:], AX.X, ALU.add)
            dve.drain()
            dve.reciprocal(red[:, 1], red[:, 0])
            dve.drain()
            dve.tensor_tensor(ex[:], ex[:], wide(red[:, 1], E), ALU.mult)
            dve.drain()
            dve.tensor_tensor(score[:], ex[:], br[:].rearrange("p (a n) -> p a n", a=1).broadcast_to([P, NT, E]), ALU.add)
            dve.drain()
            per_group = E // G
            sg = score[:].rearrange("p t (g e) -> p (t g) e", e=per_group)
            dve.tensor_tensor(pairs[:, :, 0:3], sg[:, :, 0:3], sg[:, :, 1:4], ALU.add)
            dve.tensor_tensor(pairs[:, :, 3:5], sg[:, :, 0:2], sg[:, :, 2:4], ALU.add)
            dve.tensor_tensor(pairs[:, :, 5:6], sg[:, :, 0:1], sg[:, :, 3:4], ALU.add)
            dve.drain()
            dve.tensor_reduce(gs[:].rearrange("p t g -> p (t g)"), pairs[:], AX.X, ALU.max)
            dve.drain()
            pick_two(dve, gs[:], descending[:, 0:G], gtmp[:], red, [keep[:, 0], keep[:, 1]])
            dve.tensor_tensor(gs[:], keep[:, 0], keep[:, 1], ALU.add)
            dve.drain()
            dve.tensor_scalar(gtmp[:], gs[:], 1e30, -1e30, ALU.mult, ALU.add)
            over = lambda a: a.rearrange("p t (g a) -> p (t g) a", a=1).broadcast_to([P, NT * G, per_group])
            dve.tensor_tensor(sg, sg, over(gs[:]), ALU.mult)
            dve.drain()
            dve.tensor_tensor(sg, sg, over(gtmp[:]), ALU.add)
            dve.drain()
            pick_two(dve, score[:], descending[:], tmp[:], red, [picked[:, 0], picked[:, 1]])
            dve.tensor_tensor(both[:], picked[:, 0], picked[:, 1], ALU.add).then_inc(both_ready, 1)
            for i in range(2):
                dve.tensor_tensor(tmp[:], picked[:, i], ex[:], ALU.mult)
                dve.drain()
                dve.tensor_reduce(weight[:, i], tmp[:], AX.X, ALU.add)
                dve.drain()
            dve.wait_ge(counted, 1)
            counts = [CT[:, i, :].rearrange("p (t e) -> p t e", e=E) for i in range(2)]
            dve.tensor_copy(pre[:], counts[0])
            dve.tensor_copy(tot[:], counts[1])
            dve.tensor_copy(run[:, 0], counts[1])
            dve.drain()
            a, d = 0, 1
            while d < NT:
                dve.tensor_copy(run[:, 1 - a, 0:d], run[:, a, 0:d])
                dve.tensor_tensor(run[:, 1 - a, d:NT], run[:, a, d:NT], run[:, a, 0:NT - d], ALU.add)
                dve.drain()
                a, d = 1 - a, 2 * d
            dve.tensor_tensor(pre[:], pre[:], tot[:], ALU.subtract)
            dve.tensor_tensor(cmp2[:], steps[:].rearrange("p (a n) -> p a n", a=1).broadcast_to([P, E, ST]),
                              run[:, a, NT - 1, :].rearrange("p (e a) -> p e a", a=1).broadcast_to([P, E, ST]), ALU.is_lt)
            dve.drain()
            dve.tensor_tensor(pre[:], pre[:], run[:, a], ALU.add)
            dve.tensor_reduce(tiles[:, 0], cmp2[:], AX.X, ALU.add)
            dve.drain()
            dve.tensor_tensor(cmp4[:], tiles[:, 0:1, :].broadcast_to([P, E, E]), earlier[:], ALU.mult)
            dve.drain()
            dve.tensor_reduce(tiles[:, 1], cmp4[:], AX.X, ALU.add)
            dve.drain()
            dve.tensor_scalar(tiles[:, 2], tiles[:, 1], float(P), None, ALU.mult)
            dve.tensor_tensor(tiles[:, 0], tiles[:, 0], tiles[:, 1], ALU.add)
            dve.drain()
            dve.tensor_tensor(pre[:], pre[:], tiles[:, 2:3, :].broadcast_to([P, NT, E]), ALU.add)
            dve.drain()
            for i in range(2):
                dve.tensor_tensor(picked[:, i], pre[:], picked[:, i], ALU.mult)
            dve.drain()
            for i in range(2):
                dve.tensor_reduce(posf[:, i], picked[:, i], AX.X, ALU.add)
            for sl in range(NS):
                dve.tensor_scalar(cmp3[:, sl, :], tiles[:, 0, :], float(sl), None, ALU.is_le)
            dve.drain()
            dve.tensor_copy(pos[:], posf[:])
            dve.tensor_reduce(slotf[:], cmp3[:], AX.X, ALU.add)
            dve.drain()
            dve.tensor_scalar(slotf[:], slotf[:], float(E - 1), None, ALU.min)
            dve.drain()
            dve.tensor_copy(slot[:], slotf[:]).then_inc(routed, 1)
            with dve.Fori(B // 2, B) as b:
                shared_values(dve, b)
            dve.drain()
            dve.wait_ge(s_y_added, B + 1)
            dve.wait_ge(shared_in, 16 * 5)
            dve.tensor_tensor(g.x[:], g.x[:], bs2[:].rearrange("p (a n) -> p a n", a=1).broadcast_to([P, NT, D]), ALU.add)
            dve.wait_ge(experts_in, 16 * 4)
            dve.drain()
            with dve.Fori(0, NS // U) as i:
                e = [dve.value_load(slot[0:1, bass.ds(i * U + j, 1)], min_val=0, max_val=E - 1) for j in range(U)]
                of = lambda table_, j: table_[:, bass.ds(e[j], 1), :].rearrange("p a n -> p (a n)")
                for what, q in SLOT_STEPS:
                    pair = slice(2 * q, 2 * q + 2)
                    if what == "hidden":
                        dve.wait_ge(h_full[q], i + 1)
                        for j in range(2):
                            op = dve.tensor_tensor(hb[:, 2 * q + j], HB[q % 2][:, j], of(b13, 2 * q + j), ALU.add)
                        op.then_inc(h_biased[q], 1)
                        dve.drain()
                    elif what == "gate":
                        dve.wait_ge(h_act[q], i + 1)
                        dve.tensor_tensor(hm[:, pair], hm[:, pair], hb[:, pair, P:2 * P], ALU.mult)\
                           .then_inc(h_ready[q], 1)
                    elif what == "out":
                        dve.wait_ge(y_full[q], i + 1)
                        dve.wait_ge(y_stored[q], i * 16 + 1)
                        for j in range(2):
                            op = dve.tensor_tensor(ys[:, 2 * q + j], YB[q % 2][:, j], of(b2, 2 * q + j), ALU.add)
                        op.then_inc(y_ready[q], 1)
                dve.drain()
            for h in range(2):
                dve.wait_ge(gathered[h], 16 * NT)
                own = range(h * NT // 2, (h + 1) * NT // 2)
                for i in range(2):
                    for t in own:
                        dve.scalar_tensor_tensor(out=g.x[:, t, :], in0=rows[i][:, t, :], scalar=weight[:, i, t:t + 1],
                                                 in1=g.x[:, t, :], op0=ALU.mult, op1=ALU.add)
                    dve.drain()
                for t in own:
                    dve.bn_stats(g.stats[:, t, :], g.x[:, t, :])
            dve.drain()


def sorted_experts(nc, g, name, w):
    io = g.io
    E, F = 8, 1024
    FC = F // P
    NS = 24
    U = 4
    WROW = KD * F + FC * D + FC
    with ExitStack() as ctx:
        sb = lambda n, s, t=F32: ctx.enter_context(nc.sbuf_tensor(f"{name}_sb_{n}", s, t))
        sems, from_one = [], []

        def sem(n, one=False):
            s = ctx.enter_context(nc.semaphore(f"{name}_{n}"))
            (from_one if one else sems).append(s)
            return s
        x_slots = nc.dram_tensor(f"{name}_x_slots", (NS * P, D), F32).ap()
        y_slots = nc.dram_tensor(f"{name}_y_slots", (NS * P, D), F32).ap()
        wr = sb("wr", [P, KD, E])
        br = sb("br", [P, E])
        before_p = sb("before_p", [P, P])
        ones = sb("ones", [P, P])
        earlier = sb("earlier", [P, H, H])
        steps = sb("steps", [P, NS])
        descending, ascending = sb("descending", [P, E]), sb("ascending", [P, E])
        xnT = sb("xnT", [P, KD, B * S])
        lg = sb("lg", [P, NT, E])
        sc = sb("sc", [P, NT, E])
        red = sb("red", [P, 2, NT])
        work, tmp = sb("work", [P, NT, E]), sb("tmp", [P, NT, E])
        picked = sb("picked", [P, 2, NT, E])
        win = sb("win", [P, NT, E])
        pre = sb("pre", [P, NT, E])
        tot = sb("tot", [P, NT, E])
        run = sb("run", [P, 2, NT, E])
        tiles = sb("tiles", [P, 3, E])
        cmp2 = sb("cmp2", [P, E, NT])
        cmp3 = sb("cmp3", [P, NS, E])
        cmp4 = sb("cmp4", [P, E, E])
        posf = sb("posf", [P, NT])
        pos = sb("pos", [P, NT], mybir.dt.int32)
        slotf = sb("slotf", [P, NS])
        slot = sb("slot", [P, NS], mybir.dt.int32)
        rw = sb("rw", [P, NT])
        rows = sb("rows", [P, NT, D])
        zero = sb("zero", [P, D])
        wb = sb("wb", [P, U, WROW])
        b2 = sb("b2", [P, U, D])
        xs = sb("xs", [P, U, D])
        xsT = sb("xsT", [P, U, KD, P])
        hT = sb("hT", [P, U, FC, P])
        ys = sb("ys", [P, U, D])
        GP = [ctx.enter_context(nc.psum_tensor(f"{name}_gp{i}", [P, 2, S], F32)) for i in range(2)]
        HB = [[ctx.enter_context(nc.psum_tensor(f"{name}_hb{j}{i}", [P, FC // 2, P], F32)) for i in range(2)]
              for j in range(2)]
        YB = [ctx.enter_context(nc.psum_tensor(f"{name}_yb{j}", [P, 2, S], F32)) for j in range(2)]

        weights_in, sqrt_in, sqrt_out = sem("weights_in"), sem("sqrt_in"), sem("sqrt_out")
        fixed, cleared = sem("fixed"), sem("cleared")
        xn_ready, xn_turned, xnT_ready = sem("xn_ready"), sem("xn_turned"), sem("xnT_ready")
        logits_full = sem("logits_full")
        shifted, exp_ready = sem("shifted"), sem("exp_ready")
        win_ready, counted = sem("win_ready"), sem("counted")
        slots_known, rows_ready = sem("slots_known"), sem("rows_ready")
        scattered, gathered = g.moved[1][0], g.moved[1][1:]
        each = lambda n, one=False: [sem(f"{n}{j}", one) for j in range(U)]
        w_in, x_in, xT_ready, h_full, h_act, h_dve, y_full = (
            each(n) for n in ("w_in", "x_in", "xT_ready", "h_full", "h_act", "h_dve", "y_full"))
        turned, y_ready, y_stored = (each(n, one=True) for n in ("turned", "y_ready", "y_stored"))
        start_semaphores(nc, sems, from_one)
        block = ctx.enter_context(nc.Block())
        w1 = lambda j, k, c: wb[:, j, k * F + c * P:k * F + (c + 1) * P]
        w2 = lambda j, c: wb[:, j, KD * F + c * D:KD * F + (c + 1) * D]
        b1 = lambda j, c: wb[:, j, KD * F + FC * D + c:KD * F + FC * D + c + 1]

        @block.sync
        def _(sp):
            for dst, src in ((wr, w["wr"].rearrange("(k p) n -> p k n", p=P)),
                             (br, w["br"].rearrange("(a n) -> a n", a=1).broadcast_to([P, E])),
                             (descending, io["c_descending"][:, H - E:H]), (ascending, io["c_ascending"][:, 0:E]),
                             (before_p, io["c_before"]), (earlier, io["c_earlier"]), (steps, io["c_steps"])):
                sp.dma_start(dst[:], src).then_inc(weights_in, 16)
            sp.wait_ge(fixed, 2)
            for i in range(NS):
                sp.dma_start(x_slots[i * P:(i + 1) * P, :], zero[:]).then_inc(cleared, 16)
            sp.wait_ge(slots_known, 1)
            with sp.Fori(0, NS // U) as i:
                for j in range(U):
                    e = sp.value_load(slot[0:1, bass.ds(U * i + j, 1)], min_val=0, max_val=E - 1)
                    sp.wait_ge(y_ready[j], i + 1)
                    sp.dma_start(wb[:, j, :], w["w"][bass.ds(e, 1), :, :].rearrange("a p n -> p (a n)"))\
                      .then_inc(w_in[j], 16)
                    sp.dma_start(b2[:, j, :], w["b2"][bass.ds(e, 1), :].broadcast_to([P, D])).then_inc(w_in[j], 16)
                    sp.wait_ge(scattered, 16 * NT)
                    sp.wait_ge(turned[j], i + 1)
                    sp.dma_start(xs[:, j, :], x_slots[bass.ds((U * i + j) * P, P), :]).then_inc(x_in[j], 16)

        @block.gpsimd
        def _(pool):
            pool.memset(ones[:], 1.0).then_inc(fixed, 1)
            pool.memset(zero[:], 0.0).then_inc(fixed, 1)
            pool.wait_ge(cleared, 16 * NS)
            for t in range(NT):
                pool.wait_ge(rows_ready, t + 1)
                pool.indirect_dma_start(x_slots, bass.IndirectOffsetOnAxis(pos[:, t:t + 1], 0), rows[:, t, :], None)\
                    .then_inc(scattered, 16)
            for j in range(U):
                pool.wait_ge(y_stored[j], 16 * (NS // U) + 1)
            pool.wait_ge(scattered, 16 * NT)
            for t in range(NT):
                pool.indirect_dma_start(rows[:, t, :], None, y_slots, bass.IndirectOffsetOnAxis(pos[:, t:t + 1], 0))\
                    .then_inc(gathered[2 * t // NT], 16)

        @block.scalar
        def _(act):
            norm_sqrt(act, g, sqrt_in, sqrt_out)
            for b in range(B):
                act.wait_ge(xn_turned, b + 1)
                act.activation(xnT[:, :, b * S:(b + 1) * S], GP[b % 2][:], ACT.Copy).then_inc(xnT_ready, 1)
            act.wait_ge(shifted, 1)
            act.activation(sc[:], lg[:], ACT.Exp).then_inc(exp_ready, 1)
            with act.Fori(0, NS // U) as i:
                for pair in ((0, 1), (2, 3)):
                    for j in pair:
                        act.wait_ge(turned[j], i + 2)
                        act.activation(xsT[:, j], GP[j % 2][:, :, 0:P], ACT.Copy).then_inc(xT_ready[j], 1)
                    for j in pair:
                        act.wait_ge(h_full[j], i + 1)
                        for c in range(FC // 2):
                            op = act.activation(hT[:, j, c, :], HB[j % 2][0][:, c, :], ACT.Relu, bias=b1(j, c))
                        op.then_inc(h_act[j], 1)
                    for j in pair:
                        act.wait_ge(y_ready[j], i + 2)
                        act.dma_start(y_slots[bass.ds((U * i + j) * P, P), :], ys[:, j, :]).then_inc(y_stored[j], 16)

        @block.tensor
        def _(pe):
            pe.wait_ge(weights_in, 16 * 7)
            logits = YB[0][:].rearrange("p a n -> p (a n)")
            for b in range(B + 1):
                if b < B:
                    pe.wait_ge(xn_ready, b + 1)
                    if b >= 2:
                        pe.wait_ge(xnT_ready, b - 1)
                    transpose_xn(pe, g, rows[:, b * TT:(b + 1) * TT, :], GP[b % 2]).then_inc(xn_turned, 1)
                if b:
                    pe.wait_ge(xnT_ready, b)
                    for t in range((b - 1) * TT, b * TT):
                        for k in range(KD):
                            op = pe.matmul(logits[:, t * E:(t + 1) * E], xnT[:, k, t * P:(t + 1) * P], wr[:, k, :],
                                           start=(k == 0), stop=(k == KD - 1))
            op.then_inc(logits_full, 1)
            pe.wait_ge(win_ready, 1)
            pe.wait_ge(fixed, 2)
            flat = win[:].rearrange("p t e -> p (t e)")
            pe.matmul(HB[0][0][:, 0, :], before_p[:], flat, start=True, stop=True)
            pe.matmul(HB[0][1][:, 0, :], ones[:], flat, start=True, stop=True).then_inc(counted, 1)
            with pe.Fori(0, NS // U) as i:
                for pair in ((0, 1), (2, 3)):
                    for j in pair:
                        pe.wait_ge(x_in[j], 16 * i + 16)
                        for k in range(KD):
                            op = pe.transpose(GP[j % 2][:, k, 0:P], xs[:, j, k * P:(k + 1) * P], g.ident[:])
                        op.then_inc(turned[j], 1)
                    for j in pair:
                        pe.wait_ge(xT_ready[j], i + 1)
                        pe.wait_ge(w_in[j], 32 * i + 32)
                        for c in range(FC):
                            for k in range(KD):
                                op = pe.matmul(HB[j % 2][c // (FC // 2)][:, c % (FC // 2), :], w1(j, k, c), xsT[:, j, k, :],
                                               start=(k == 0), stop=(k == KD - 1))
                        op.then_inc(h_full[j], 1)
                    for j in pair:
                        pe.wait_ge(h_act[j], i + 1)
                        pe.wait_ge(h_dve[j], i + 1)
                        pe.wait_ge(y_ready[(j + 2) % U], i + 1 + j // 2)
                        for c in range(FC):
                            op = pe.matmul(YB[j % 2][:, 0], hT[:, j, c, :], w2(j, c), start=(c == 0), stop=(c == FC - 1))
                        op.then_inc(y_full[j], 1)

        @block.vector
        def _(dve):
            wide = lambda a: a.rearrange("p (t a) -> p t a", a=1).broadcast_to([P, NT, E])
            row = lambda a: a[:].rearrange("p (a n) -> p a n", a=1).broadcast_to([P, NT, E])
            norm_factors(dve, g, sqrt_in, sqrt_out)
            for t in range(NT):
                op = dve.tensor_scalar(rows[:, t, :], g.x[:, t, :], g.mean[:, t:t + 1], g.rstd[:, t:t + 1],
                                       ALU.subtract, ALU.mult)
                if t % TT == TT - 1:
                    op.then_inc(xn_ready, 1)
            dve.wait_ge(weights_in, 16 * 7)
            dve.wait_ge(logits_full, 1)
            src = YB[0][:].rearrange("p a n -> p (a n)")[:, 0:NT * E].rearrange("p (t e) -> p t e", e=E)
            dve.tensor_tensor(lg[:], src, row(br), ALU.add)
            dve.drain()
            dve.tensor_reduce(red[:, 0], lg[:], AX.X, ALU.max)
            dve.drain()
            dve.tensor_tensor(lg[:], lg[:], wide(red[:, 0]), ALU.subtract).then_inc(shifted, 1)
            dve.wait_ge(exp_ready, 1)
            dve.tensor_reduce(red[:, 0], sc[:], AX.X, ALU.add)
            dve.drain()
            dve.reciprocal(red[:, 1], red[:, 0])
            dve.drain()
            dve.tensor_tensor(sc[:], sc[:], wide(red[:, 1]), ALU.mult)
            dve.drain()
            dve.tensor_copy(work[:], sc[:])
            dve.drain()
            pick_two(dve, work[:], descending[:], tmp[:], red, [picked[:, 0], picked[:, 1]])
            dve.tensor_tensor(picked[:, 0], picked[:, 0], picked[:, 1], ALU.add)
            dve.tensor_scalar(work[:], sc[:], 0.0, None, ALU.is_gt)
            dve.drain()
            dve.tensor_tensor(picked[:, 0], picked[:, 0], work[:], ALU.mult)
            dve.drain()
            dve.tensor_tensor(tmp[:], picked[:, 0], row(ascending), ALU.mult)
            dve.drain()
            dve.tensor_reduce(red[:, 0], tmp[:], AX.X, ALU.max)
            dve.drain()
            dve.tensor_tensor(win[:], tmp[:], wide(red[:, 0]), ALU.is_equal)
            dve.drain()
            dve.tensor_tensor(win[:], win[:], picked[:, 0], ALU.mult).then_inc(win_ready, 1)
            dve.drain()
            dve.tensor_tensor(sc[:], sc[:], win[:], ALU.mult)
            dve.drain()
            dve.tensor_reduce(rw[:], sc[:], AX.X, ALU.add)
            dve.drain()
            dve.tensor_tensor(rw[:], rw[:], g.rstd[:], ALU.mult)
            dve.wait_ge(counted, 1)
            dve.tensor_copy(pre[:], HB[0][0][:, 0, :].rearrange("p (t e) -> p t e", e=E))
            dve.tensor_copy(tot[:], HB[0][1][:, 0, :].rearrange("p (t e) -> p t e", e=E))
            dve.tensor_copy(run[:, 0], HB[0][1][:, 0, :].rearrange("p (t e) -> p t e", e=E))
            dve.drain()
            a, d = 0, 1
            while d < NT:
                dve.tensor_copy(run[:, 1 - a, 0:d], run[:, a, 0:d])
                dve.tensor_tensor(run[:, 1 - a, d:NT], run[:, a, d:NT], run[:, a, 0:NT - d], ALU.add)
                dve.drain()
                a, d = 1 - a, 2 * d
            dve.tensor_tensor(pre[:], pre[:], tot[:], ALU.subtract)
            dve.tensor_tensor(cmp2[:], steps[:, 0:NT].rearrange("p (a n) -> p a n", a=1).broadcast_to([P, E, NT]),
                              run[:, a, NT - 1, :].rearrange("p (e a) -> p e a", a=1).broadcast_to([P, E, NT]), ALU.is_lt)
            dve.drain()
            dve.tensor_tensor(pre[:], pre[:], run[:, a], ALU.add)
            dve.tensor_reduce(tiles[:, 0], cmp2[:], AX.X, ALU.add)
            dve.drain()
            dve.tensor_tensor(cmp4[:], tiles[:, 0:1, :].broadcast_to([P, E, E]), earlier[:, 0:E, 0:E], ALU.mult)
            dve.drain()
            dve.tensor_reduce(tiles[:, 1], cmp4[:], AX.X, ALU.add)
            dve.drain()
            dve.tensor_tensor(tiles[:, 0], tiles[:, 0], tiles[:, 1], ALU.add)
            dve.tensor_scalar(tiles[:, 2], tiles[:, 1], float(P), None, ALU.mult)
            dve.drain()
            dve.tensor_tensor(pre[:], pre[:], tiles[:, 2:3, :].broadcast_to([P, NT, E]), ALU.add)
            for sl in range(NS):
                dve.tensor_scalar(cmp3[:, sl, :], tiles[:, 0, :], float(sl), None, ALU.is_le)
            dve.drain()
            dve.tensor_tensor(pre[:], pre[:], win[:], ALU.mult)
            dve.tensor_reduce(slotf[:], cmp3[:], AX.X, ALU.add)
            dve.drain()
            dve.tensor_reduce(posf[:], pre[:], AX.X, ALU.add)
            dve.tensor_scalar(slotf[:], slotf[:], float(E - 1), None, ALU.min)
            dve.drain()
            dve.tensor_copy(pos[:], posf[:])
            dve.tensor_copy(slot[:], slotf[:]).then_inc(slots_known, 1)
            dve.drain()
            for t in range(NT):
                dve.tensor_scalar(rows[:, t, :], g.x[:, t, :], g.mean[:, t:t + 1], rw[:, t:t + 1],
                                  ALU.subtract, ALU.mult).then_inc(rows_ready, 1)
            with dve.Fori(0, NS // U) as i:
                for pair in ((0, 1), (2, 3)):
                    for j in pair:
                        dve.wait_ge(h_full[j], i + 1)
                        for c in range(FC // 2):
                            op = dve.tensor_scalar(hT[:, j, FC // 2 + c, :], HB[j % 2][1][:, c, :], b1(j, FC // 2 + c), 0.0,
                                                   ALU.add, ALU.max)
                        op.then_inc(h_dve[j], 1)
                    for j in pair:
                        dve.wait_ge(y_full[j], i + 1)
                        dve.wait_ge(y_stored[j], 16 * i + 1)
                        dve.tensor_tensor(ys[:, j, :], YB[j % 2][:, 0], b2[:, j, :], ALU.add).then_inc(y_ready[j], 1)
            for h in range(2):
                dve.wait_ge(gathered[h], 16 * NT // 2)
                own = slice(h * NT // 2, (h + 1) * NT // 2)
                dve.tensor_tensor(g.x[:, own, :], g.x[:, own, :], rows[:, own, :], ALU.add)
                dve.drain()
                for t in range(own.start, own.stop):
                    dve.bn_stats(g.stats[:, t, :], g.x[:, t, :])
            dve.drain()


def store_x(nc, g):
    with ExitStack() as ctx:
        stored = ctx.enter_context(nc.semaphore("x_stored"))
        start_semaphores(nc, [stored], [])
        block = ctx.enter_context(nc.Block())

        @block.sync
        def _(sp):
            sp.dma_start(g.io["out"].rearrange("b (t p) d -> p (b t) d", p=P), g.x[:]).then_inc(stored, 16)
            sp.wait_ge(stored, 16)


def constants():
    bf = lambda a: (np.ascontiguousarray(a, np.float32).view(np.uint32) >> 16).astype(np.uint16)
    c = {"c_ident": np.eye(P, dtype=np.float32), "c_eye": bf(np.eye(P))}
    for hd in (16, 64):
        m = np.zeros((P, P // hd), np.float32)
        for h in range(P // hd):
            m[h * hd:(h + 1) * hd, h] = 1
        c[f"c_mask{hd}"] = m
    sel = np.zeros((P, H, P), np.float32)
    for part in range(3):
        for h in range(H):
            sel[32 * part + h, h, :] = 1
    c["c_sel"] = bf(sel)
    c["c_earlier"] = np.broadcast_to(np.tril(np.ones((H, H), np.float32), -1), (P, H, H)).copy()
    c["c_descending"] = np.broadcast_to(np.arange(H, 0, -1, dtype=np.float32), (P, H)).copy()
    c["c_ascending"] = np.broadcast_to(np.arange(1, H + 1, dtype=np.float32), (P, H)).copy()
    c["c_before"] = np.triu(np.ones((P, P), np.float32), 1)
    c["c_steps"] = np.broadcast_to(np.arange(24, dtype=np.float32) * P, (P, 24)).copy()
    turn = np.zeros((P, P), np.float32)
    for i in range(0, P, 2):
        turn[i + 1, i], turn[i, i + 1] = -1, 1
    c["c_turn"] = turn
    c["c_tri"] = np.triu(np.ones((P, P), np.float32))
    hd = 16
    half = hd // 2
    base = (np.arange(0, hd, 2) + 0.4 * hd) / (1.4 * hd)
    power = (np.arange(-(S // 2), -(S // 2) + S) / 512.0)[:, None]
    length = base[None, :] ** power
    angle = np.arange(S)[:, None] / 10000.0 ** (np.arange(half) / half)[None, :]
    gammas = 1.0 - np.exp(np.linspace(np.log(1 / 32), np.log(1 / 512), H))
    tables = np.zeros((4, H, hd, S))
    for i, (f, sign) in enumerate(((np.cos, 1), (np.sin, 1), (np.cos, -1), (np.sin, -1))):
        t = np.repeat(f(angle) * length ** sign, 2, axis=-1).T
        tables[i] = t[None] * gammas[:, None, None] ** (sign * np.arange(S))[None, None, :]
    c["c_tables"] = tables.reshape(4, 2, P, S).transpose(2, 0, 1, 3).astype(np.float32)
    q, k = np.arange(P)[:, None], np.arange(P)[None, :]
    c["c_neg_qk"] = bf(np.where(k > q, -8e9, 0.0))
    return c


def pad_heads(w, hp):
    out = np.zeros((H, hp) + w.shape[1:], w.dtype)
    out[:, :w.shape[0] // H] = w.reshape((H, w.shape[0] // H) + w.shape[1:])
    return out.reshape((H * hp,) + w.shape[1:])


def layouts(i):
    T = lambda a: np.ascontiguousarray(np.asarray(a).T)
    a = {"x": i["x"], "ctxT": np.ascontiguousarray(np.asarray(i["ctx_1024"]).transpose(0, 2, 1))}
    wkv = np.asarray(i["L0_xattn_w_kv"])
    a["a0_wq"] = i["L0_xattn_w_q"]
    a["a0_wk"] = np.tile(wkv[:, :16], (1, 8))
    a["a0_wv"] = wkv[:, 16:]
    a["a0_wo"] = pad_heads(np.asarray(i["L0_xattn_w_concat"]), 32)
    E, I = 16, 128
    rows_of = lambda n: np.asarray(i[f"L0_ffn_We{n}"]).reshape(E, KD, P, I).transpose(2, 0, 1, 3)
    a["f0_w13"] = np.concatenate([rows_of(1), rows_of(3)], 3)
    a["f0_w2"] = np.asarray(i["L0_ffn_We2"]).transpose(1, 0, 2)
    a["f0_b13"], a["f0_b2"] = np.concatenate([i["L0_ffn_be1"], i["L0_ffn_be3"]], 1), i["L0_ffn_be2"]
    a["f0_ws13"] = np.stack([np.asarray(i[f"L0_ffn_ws{n}"]).reshape(KD, P, -1, P).transpose(1, 2, 0, 3) for n in (1, 3)], 2)
    a["f0_ws2"] = np.asarray(i["L0_ffn_ws2"]).reshape(-1, P, D).transpose(1, 0, 2)
    for n in "13":
        a[f"f0_bs{n}"] = T(np.asarray(i[f"L0_ffn_bs{n}"]).reshape(-1, P))
    a["f0_bs2"] = i["L0_ffn_bs2"]
    a["f0_wr"], a["f0_br"] = T(i["L0_ffn_gate_w"]), i["L0_ffn_gate_b"]
    per_partition = lambda n: np.asarray(i[f"L1_ffn_{n}"]).reshape(8, -1, P, i[f"L1_ffn_{n}"].shape[-1])\
        .transpose(0, 2, 1, 3).reshape(8, P, -1)
    a["f1_w"] = np.concatenate([per_partition("w1"), per_partition("w2"),
                                np.asarray(i["L1_ffn_b1"]).reshape(8, -1, P).transpose(0, 2, 1)], 2)
    a["f1_b2"], a["f1_wr"], a["f1_br"] = i["L1_ffn_b2"], i["L1_ffn_gate_w"], i["L1_ffn_gate_b"]
    a["f3_ws1"] = np.asarray(i["L3_ffn_Ws1"]).reshape(KD, P, P).transpose(1, 0, 2)
    a["f3_ws2"] = i["L3_ffn_Ws2"]
    a["f3_w1"] = np.asarray(i["L3_ffn_W1"]).reshape(-1, KD, P, P).transpose(2, 0, 1, 3)
    a["f3_w2"] = np.asarray(i["L3_ffn_W2"]).transpose(1, 0, 2)
    a["f3_wr"] = i["L3_ffn_Wr"]
    for n in "QKV":
        a[f"a1_w{n.lower()}"] = np.asarray(i[f"L1_xattn_W_{n}"]).transpose(1, 0, 2).reshape(D, D)
    a["a1_wg"], a["a1_wo"] = T(i["L1_xattn_g_w"]), T(i["L1_xattn_out_w"])
    a["a1_gb"], a["a1_bo"] = i["L1_xattn_g_b"], i["L1_xattn_out_b"]
    a["a2_wq"], a["a2_wk"], a["a2_wv"] = (T(i[f"L2_xattn_w{n}"]) for n in "qkv")
    a["a2_wo"] = pad_heads(T(i["L2_xattn_wo"]), 32)
    for n in ("bq", "bk"):
        a[f"a2_{n}"] = T(np.asarray(i[f"L2_xattn_{n}"]).reshape(-1, P))
    for n in ("bv", "bo"):
        a[f"a2_{n}"] = i[f"L2_xattn_{n}"]
    for n in "qkv":
        a[f"f2_w{n}"] = T(i[f"L2_ffn_W{n}"])
    a["f2_wo"] = pad_heads(T(i["L2_ffn_Wp"]), 32)
    a["f2_bq"], a["f2_bv"], a["f2_bo"] = (i[f"L2_ffn_b{n}"] for n in "qvp")
    a["f2_bk"] = T(np.asarray(i["L2_ffn_bk"]).reshape(-1, P))
    a["f2_wr"] = pad_heads(np.concatenate([T(i["L2_ffn_Wr"]), T(i["L2_ffn_Ws"])], 1), 32)
    a["f2_br"] = np.concatenate([np.asarray(i["L2_ffn_br"]), np.asarray(i["L2_ffn_bs"])])
    a["f2_qe"] = np.asarray(i["L2_ffn_query_embedding"]).reshape(-1)
    a["f2_temp"] = np.asarray(i["L2_ffn_temperature"]).reshape(-1)
    for n in "qkv":
        w = np.asarray(i[f"L3_xattn_W{n}"])
        a[f"a3_w{n}"] = w.transpose(1, 0, 2).reshape(D, -1)
    a["a3_wo"] = i["L3_xattn_Wo"]
    a.update(constants())
    return {k: np.ascontiguousarray(v) for k, v in a.items()}


def sub(a, pre):
    return {n[len(pre):]: v for n, v in a.items() if n.startswith(pre)}


STAGES = ["a0", "f0", "a1", "f1", "a2", "f2", "a3", "f3"]


def program(nc, io, stages):
    for n in ("c_eye", "c_sel", "c_neg_qk"):
        io[n] = io[n].bitcast(BF16)
    with ExitStack() as ctx:
        g = Common(nc, ctx, io)
        load_x(nc, g)
        for s in stages:
            w = sub(io, s + "_")
            if s == "a0":
                attention(nc, g, s, 16, w, shared_kv=True)
            elif s == "f0":
                sorted_gated_experts(nc, g, s, w)
            elif s == "f3":
                truncated_experts(nc, g, s, w)
            elif s == "f1":
                sorted_experts(nc, g, s, w)
            elif s == "a1":
                retention(nc, g, s, w)
            elif s == "a2":
                attention(nc, g, s, 16, w, bias=True)
            elif s == "a3":
                attention(nc, g, s, 64, w, causal=True, interleave=True)
            elif s == "f2":
                attention(nc, g, s, 16, w, bias=True, kv_from_x=True, router=True)
        store_x(nc, g)


def kernel(**inputs):
    import concourse.bacc as bacc
    from concourse.bass_utils import run_bass_kernel_spmd

    nc = bacc.Bacc("TRN2", target_bir_lowering=False, num_devices=1)
    arrays = layouts(inputs)
    io = {n: nc.dram_tensor(n, a.shape, mybir.dt.from_np(a.dtype), kind="ExternalInput").ap()
          for n, a in arrays.items()}
    io["out"] = nc.dram_tensor("out", (B, S, D), F32, kind="ExternalOutput").ap()
    program(nc, io, STAGES)
    result = run_bass_kernel_spmd(nc, [arrays], core_ids=[0])
    return result.results[0]["out"]
```
